# Optimizing a Trainium2 kernel written in Bass

```python
import numpy as np
import jax
import jax.numpy as jnp

def _softmax(x, axis=-1):
    return jax.nn.softmax(x, axis=axis)

def _gelu(x):
    return jax.nn.gelu(x, approximate=True)

def _silu(x):
    return jax.nn.silu(x)

def _sigmoid(x):
    return jax.nn.sigmoid(x)

def _layernorm(x, axis=-1, eps=1e-05):
    m = jnp.mean(x, axis=axis, keepdims=True)
    v = jnp.var(x, axis=axis, keepdims=True)
    return (x - m) / jnp.sqrt(v + eps)

def _scatter_add(tgt, idx, src, axis=0):
    return tgt.at[idx].add(src)

def _segment_sum(src, seg, n):
    return jax.ops.segment_sum(src, seg, n)
kernel_name = 'mk_vit_tower_d2_tok_img256_r4_867d82'

def setup_inputs(seed: int=0):
    np.random.seed(seed)
    _w = jnp.asarray

    def _rec_inputs():
        import jax
        import jax.numpy as jnp
        _rk = jax.random.key(seed)
        x = 7.57192e-06 + 1.00007 * jax.random.normal(jax.random.fold_in(_rk, 1), (32, 3, 224, 224), jnp.float32)
        return x
    x = _rec_inputs()

    def _L0_tok_setup():
        import jax, jax.numpy as jnp
        import numpy as np
        import math
        GRID = 28
        NUM_PATCHES = GRID * GRID
        PATCH = 8
        IN_CH = 3
        HIDDEN = 64
        BATCH = 64

        def build_grid_edges():
            edges = []
            for i in range(GRID):
                for j in range(GRID):
                    cur = i * GRID + j
                    if j < GRID - 1:
                        edges.append([cur, cur + 1])
                    if i < GRID - 1:
                        edges.append([cur, cur + GRID])
            e = np.asarray(edges, dtype=np.int32).T
            e = np.concatenate([e, e[::-1]], axis=1)
            return jnp.asarray(e)

        def sin_positional_encoding(n, d):
            pos = jnp.arange(n, dtype=jnp.float32)[:, None]
            div = jnp.exp(jnp.arange(0, d, 2, dtype=jnp.float32) * (-math.log(10000.0) / d))
            pe = jnp.zeros((n, d), dtype=jnp.float32)
            pe = pe.at[:, 0::2].set(jnp.sin(pos * div))
            pe = pe.at[:, 1::2].set(jnp.cos(pos * div))
            return pe
        key = jax.random.key(seed)
        ks = jax.random.split(key, 8)
        s = 0.02
        return {'x': jax.random.normal(ks[0], (BATCH, IN_CH, 224, 224), dtype=jnp.float32), 'W_embed': jax.random.normal(ks[1], (IN_CH * PATCH * PATCH, HIDDEN), dtype=jnp.float32) * s, 'b_embed': jax.random.normal(ks[2], (HIDDEN,), dtype=jnp.float32) * s, 'W_gcn': jax.random.normal(ks[3], (3, HIDDEN, HIDDEN), dtype=jnp.float32) * s, 'b_gcn': jax.random.normal(ks[4], (3, HIDDEN), dtype=jnp.float32) * s, 'W_out': jax.random.normal(ks[5], (HIDDEN, 64), dtype=jnp.float32) * s, 'b_out': jax.random.normal(ks[6], (64,), dtype=jnp.float32) * s, 'edge_index': build_grid_edges()}
    _L0_tok_all = _L0_tok_setup()
    _L0_tok_in = {k: v for k, v in _L0_tok_all.items() if k in ('W_embed', 'b_embed', 'W_gcn', 'b_gcn', 'W_out', 'b_out', 'edge_index')}
    del _L0_tok_all

    def _L0_attn_setup():
        import jax, jax.numpy as jnp
        import numpy as np
        H, D = (8, 32)
        EPS = 1e-05
        key = jax.random.key(seed)
        ks = jax.random.split(key, 4)
        B, N, C = (2, 512, 64)
        inner = H * D
        return {'node_features': jax.random.normal(ks[0], (B, N, C), jnp.float32), 'ln_gamma': jnp.ones((C,), jnp.float32), 'ln_beta': jnp.zeros((C,), jnp.float32), 'W_qkv': jax.random.normal(ks[1], (3 * inner, C), jnp.float32) * 0.02, 'W_gate': jax.random.normal(ks[2], (inner, C), jnp.float32) * 0.02, 'b_gate': jnp.ones((inner,), jnp.float32), 'W_final': jax.random.normal(ks[3], (C, inner), jnp.float32) * 0.02, 'b_final': jnp.zeros((C,), jnp.float32)}
    _L0_attn_all = _L0_attn_setup()
    _L0_attn_in = {k: v for k, v in _L0_attn_all.items() if k in ('ln_gamma', 'ln_beta', 'W_qkv', 'W_gate', 'b_gate', 'W_final', 'b_final')}
    del _L0_attn_all

    def _L0_ffn_setup():
        import jax, jax.numpy as jnp
        import numpy as np
        B, T, IN_DIM = (64, 64, 64)
        HID, OUT_DIM = (128, 64)
        N_LAYERS, N_EXPERTS, N_SHARED = (2, 16, 1)
        key = jax.random.key(seed)
        ks = jax.random.split(key, 10)
        s = 0.02
        x = jax.random.normal(ks[0], (B, T, IN_DIM), dtype=jnp.float32)
        route_id = jax.random.randint(ks[1], (B,), 0, N_EXPERTS)
        Wi = jax.random.normal(ks[2], (HID, IN_DIM), dtype=jnp.float32) * s
        bi = jnp.zeros((HID,), dtype=jnp.float32)
        Wr = jax.random.normal(ks[3], (N_LAYERS, N_EXPERTS, HID, HID), dtype=jnp.float32) * s
        br = jax.random.normal(ks[4], (N_LAYERS, N_EXPERTS, HID), dtype=jnp.float32) * s
        Ws = jax.random.normal(ks[5], (N_LAYERS, N_SHARED, HID, HID), dtype=jnp.float32) * s
        bs = jax.random.normal(ks[6], (N_LAYERS, N_SHARED, HID), dtype=jnp.float32) * s
        Wo = jax.random.normal(ks[7], (OUT_DIM, HID), dtype=jnp.float32) * s
        bo = jnp.zeros((OUT_DIM,), dtype=jnp.float32)
        return {'x': x, 'route_id': route_id, 'Wi': Wi, 'bi': bi, 'Wr': Wr, 'br': br, 'Ws': Ws, 'bs': bs, 'Wo': Wo, 'bo': bo}
    _L0_ffn_all = _L0_ffn_setup()
    _L0_ffn_in = {k: v for k, v in _L0_ffn_all.items() if k in ('route_id', 'Wi', 'bi', 'Wr', 'br', 'Ws', 'bs', 'Wo', 'bo')}
    del _L0_ffn_all

    def _L1_attn_setup():
        import jax, jax.numpy as jnp
        import numpy as np
        B, L, D = (4, 1024, 64)
        key = jax.random.key(seed)
        kx, kq, kk, kv, ko = jax.random.split(key, 5)
        std = 0.02
        return {'x': jax.random.normal(kx, (B, L, D), dtype=jnp.float32), 'Wq': std * jax.random.normal(kq, (D, D), dtype=jnp.float32), 'Wk': std * jax.random.normal(kk, (D, D), dtype=jnp.float32), 'Wv': std * jax.random.normal(kv, (D, D), dtype=jnp.float32), 'Wo': std * jax.random.normal(ko, (D, D), dtype=jnp.float32)}
    _L1_attn_all = _L1_attn_setup()
    _L1_attn_in = {k: v for k, v in _L1_attn_all.items() if k in ('Wq', 'Wk', 'Wv', 'Wo')}
    del _L1_attn_all

    def _L1_ffn_setup():
        import math
        import jax, jax.numpy as jnp
        import numpy as np
        CAPACITY_FACTOR = 1.25
        TOP_K = 2
        LN_EPS = 1e-05

        def _layer_norm(x, gamma, beta):
            mu = jnp.mean(x, axis=-1, keepdims=True)
            var = jnp.var(x, axis=-1, keepdims=True)
            return (x - mu) * jax.lax.rsqrt(var + LN_EPS) * gamma + beta
        key = jax.random.key(seed)
        ks = jax.random.split(key, 4)
        B, S, D, F, E = (8, 1024, 64, 128, 8)
        x = jax.random.normal(ks[0], (B, S, D), dtype=jnp.float32)
        Wr = jax.random.normal(ks[1], (D, E), dtype=jnp.float32) / np.sqrt(D)
        br = jnp.zeros((E,), jnp.float32)
        W1 = jax.random.normal(ks[2], (E, D, F), dtype=jnp.float32) / np.sqrt(D)
        b1 = jnp.zeros((E, F), jnp.float32)
        W2 = jax.random.normal(ks[3], (E, F, D), dtype=jnp.float32) / np.sqrt(F)
        b2 = jnp.zeros((E, D), jnp.float32)
        gamma = jnp.ones((D,), jnp.float32)
        beta = jnp.zeros((D,), jnp.float32)
        return {'x': x, 'Wr': Wr, 'br': br, 'W1': W1, 'b1': b1, 'W2': W2, 'b2': b2, 'gamma': gamma, 'beta': beta}
    _L1_ffn_all = _L1_ffn_setup()
    _L1_ffn_in = {k: v for k, v in _L1_ffn_all.items() if k in ('Wr', 'br', 'W1', 'b1', 'W2', 'b2', 'gamma', 'beta')}
    del _L1_ffn_all
    return {'x': x, 'L0_tok_W_embed': _L0_tok_in['W_embed'], 'L0_tok_b_embed': _L0_tok_in['b_embed'], 'L0_tok_W_gcn': _L0_tok_in['W_gcn'], 'L0_tok_b_gcn': _L0_tok_in['b_gcn'], 'L0_tok_W_out': _L0_tok_in['W_out'], 'L0_tok_b_out': _L0_tok_in['b_out'], 'L0_tok_edge_index': _L0_tok_in['edge_index'], 'L0_attn_ln_gamma': _L0_attn_in['ln_gamma'], 'L0_attn_ln_beta': _L0_attn_in['ln_beta'], 'L0_attn_W_qkv': _L0_attn_in['W_qkv'], 'L0_attn_W_gate': _L0_attn_in['W_gate'], 'L0_attn_b_gate': _L0_attn_in['b_gate'], 'L0_attn_W_final': _L0_attn_in['W_final'], 'L0_attn_b_final': _L0_attn_in['b_final'], 'L0_ffn_route_id': _L0_ffn_in['route_id'], 'L0_ffn_Wi': _L0_ffn_in['Wi'], 'L0_ffn_bi': _L0_ffn_in['bi'], 'L0_ffn_Wr': _L0_ffn_in['Wr'], 'L0_ffn_br': _L0_ffn_in['br'], 'L0_ffn_Ws': _L0_ffn_in['Ws'], 'L0_ffn_bs': _L0_ffn_in['bs'], 'L0_ffn_Wo': _L0_ffn_in['Wo'], 'L0_ffn_bo': _L0_ffn_in['bo'], 'L1_attn_Wq': _L1_attn_in['Wq'], 'L1_attn_Wk': _L1_attn_in['Wk'], 'L1_attn_Wv': _L1_attn_in['Wv'], 'L1_attn_Wo': _L1_attn_in['Wo'], 'L1_ffn_Wr': _L1_ffn_in['Wr'], 'L1_ffn_br': _L1_ffn_in['br'], 'L1_ffn_W1': _L1_ffn_in['W1'], 'L1_ffn_b1': _L1_ffn_in['b1'], 'L1_ffn_W2': _L1_ffn_in['W2'], 'L1_ffn_b2': _L1_ffn_in['b2'], 'L1_ffn_gamma': _L1_ffn_in['gamma'], 'L1_ffn_beta': _L1_ffn_in['beta']}

def reference(x, L0_tok_W_embed, L0_tok_b_embed, L0_tok_W_gcn, L0_tok_b_gcn, L0_tok_W_out, L0_tok_b_out, L0_tok_edge_index, L0_attn_ln_gamma, L0_attn_ln_beta, L0_attn_W_qkv, L0_attn_W_gate, L0_attn_b_gate, L0_attn_W_final, L0_attn_b_final, L0_ffn_route_id, L0_ffn_Wi, L0_ffn_bi, L0_ffn_Wr, L0_ffn_br, L0_ffn_Ws, L0_ffn_bs, L0_ffn_Wo, L0_ffn_bo, L1_attn_Wq, L1_attn_Wk, L1_attn_Wv, L1_attn_Wo, L1_ffn_Wr, L1_ffn_br, L1_ffn_W1, L1_ffn_b1, L1_ffn_W2, L1_ffn_b2, L1_ffn_gamma, L1_ffn_beta):
    import jax
    import jax.numpy as jnp

    def _L0_tok_ref(x, W_embed, b_embed, W_gcn, b_gcn, W_out, b_out, edge_index):
        import jax, jax.numpy as jnp
        import numpy as np
        import math
        GRID = 28
        NUM_PATCHES = GRID * GRID
        PATCH = 8
        IN_CH = 3
        HIDDEN = 64
        BATCH = 64

        def build_grid_edges():
            edges = []
            for i in range(GRID):
                for j in range(GRID):
                    cur = i * GRID + j
                    if j < GRID - 1:
                        edges.append([cur, cur + 1])
                    if i < GRID - 1:
                        edges.append([cur, cur + GRID])
            e = np.asarray(edges, dtype=np.int32).T
            e = np.concatenate([e, e[::-1]], axis=1)
            return jnp.asarray(e)

        def sin_positional_encoding(n, d):
            pos = jnp.arange(n, dtype=jnp.float32)[:, None]
            div = jnp.exp(jnp.arange(0, d, 2, dtype=jnp.float32) * (-math.log(10000.0) / d))
            pe = jnp.zeros((n, d), dtype=jnp.float32)
            pe = pe.at[:, 0::2].set(jnp.sin(pos * div))
            pe = pe.at[:, 1::2].set(jnp.cos(pos * div))
            return pe
        B = x.shape[0]
        N = NUM_PATCHES
        p = x.reshape(B, IN_CH, GRID, PATCH, GRID, PATCH)
        p = p.transpose(0, 2, 4, 1, 3, 5).reshape(B, N, IN_CH * PATCH * PATCH)
        h = p @ W_embed + b_embed + sin_positional_encoding(N, HIDDEN)[None]
        src, dst = (edge_index[0], edge_index[1])
        deg = jnp.zeros((N,), dtype=h.dtype).at[dst].add(1.0) + 1.0
        dinv = deg ** (-0.5)
        enorm = (dinv[src] * dinv[dst])[None, :, None]
        snorm = (1.0 / deg)[None, :, None]
        for i in range(3):
            hw = h @ W_gcn[i]
            agg = hw * snorm
            agg = agg.at[:, dst].add(hw[:, src] * enorm)
            h = jax.nn.relu(agg + b_gcn[i])
        return h @ W_out + b_out

    def _L0_attn_ref(node_features, ln_gamma, ln_beta, W_qkv, W_gate, b_gate, W_final, b_final):
        import jax, jax.numpy as jnp
        import numpy as np
        H, D = (8, 32)
        EPS = 1e-05
        x = node_features
        B, N, _ = x.shape
        mu = jnp.mean(x, axis=-1, keepdims=True)
        var = jnp.mean(jnp.square(x - mu), axis=-1, keepdims=True)
        normed = (x - mu) / jnp.sqrt(var + EPS) * ln_gamma + ln_beta
        qkv = normed @ W_qkv.T
        q, k, v = jnp.split(qkv, 3, axis=-1)

        def to_heads(t):
            return t.reshape(B, N, H, D).transpose(0, 2, 1, 3)
        q, k, v = (to_heads(q), to_heads(k), to_heads(v))
        gate = jax.nn.sigmoid(to_heads(x @ W_gate.T + b_gate))
        scores = jnp.einsum('bhid,bhjd->bhij', q, k) * D ** (-0.5)
        attn = jax.nn.softmax(scores, axis=-1)
        out = jnp.einsum('bhij,bhid->bhjd', attn, v) * gate
        out = out.transpose(0, 2, 1, 3).reshape(B, N, H * D)
        return x + out @ W_final.T + b_final

    def _L0_ffn_ref(x, route_id, Wi, bi, Wr, br, Ws, bs, Wo, bo):
        import jax, jax.numpy as jnp
        import numpy as np
        B, T, IN_DIM = (64, 64, 64)
        HID, OUT_DIM = (128, 64)
        N_LAYERS, N_EXPERTS, N_SHARED = (2, 16, 1)
        flat = x.reshape(-1, x.shape[-1])
        n_tok = flat.shape[0]
        route = jnp.repeat(route_id, n_tok // route_id.shape[0])
        h = jax.nn.relu(flat @ Wi.T + bi)
        n_layers, n_experts = (Wr.shape[0], Wr.shape[1])
        for l in range(n_layers):
            shared = (jnp.einsum('nd,shd->snh', h, Ws[l]) + bs[l][:, None, :]).mean(axis=0)
            routed = jnp.zeros_like(h)
            for e in range(n_experts):
                ye = h @ Wr[l, e].T + br[l, e]
                routed = routed + jnp.where((route == e)[:, None], ye, 0.0)
            h = jax.nn.relu(shared + routed + h)
        out = h @ Wo.T + bo
        return out.reshape(*x.shape[:-1], out.shape[-1])

    def _L1_attn_ref(x, Wq, Wk, Wv, Wo):
        import jax, jax.numpy as jnp
        import numpy as np
        B, L, D = (4, 1024, 64)
        q = x @ Wq.T
        k = x @ Wk.T
        v = x @ Wv.T
        logits = jnp.einsum('bld,bmd->blm', q, k)
        Lq = x.shape[1]
        causal_mask = jnp.triu(jnp.ones((Lq, Lq), dtype=bool), k=1)
        logits = jnp.where(causal_mask[None], jnp.asarray(0.0, logits.dtype), logits)
        attn = jax.nn.relu(logits)
        row_counts = jnp.maximum(jnp.arange(Lq, dtype=attn.dtype), 1.0)
        attn = attn / row_counts[None, :, None]
        ctx = jnp.einsum('blm,bmd->bld', attn, v)
        return ctx @ Wo.T

    def _L1_ffn_ref(x, Wr, br, W1, b1, W2, b2, gamma, beta):
        import math
        import jax, jax.numpy as jnp
        import numpy as np
        CAPACITY_FACTOR = 1.25
        TOP_K = 2
        LN_EPS = 1e-05

        def _layer_norm(x, gamma, beta):
            mu = jnp.mean(x, axis=-1, keepdims=True)
            var = jnp.var(x, axis=-1, keepdims=True)
            return (x - mu) * jax.lax.rsqrt(var + LN_EPS) * gamma + beta
        B, S, D = x.shape
        E = Wr.shape[1]
        N = B * S
        K = TOP_K
        logits = jnp.mean(x, axis=1) @ Wr + br
        routing_weights = jax.nn.softmax(logits, axis=-1)
        capacity = float(math.ceil(N * CAPACITY_FACTOR / E))
        expected_loads = routing_weights.sum(axis=0) * (N / B)
        scale = jnp.where(expected_loads > capacity, capacity / expected_loads, 1.0)
        routing_weights = jax.nn.softmax(routing_weights * scale, axis=-1)
        rw_tok = jnp.broadcast_to(routing_weights[:, None, :], (B, S, E)).reshape(N, E)
        top_w, top_i = jax.lax.top_k(rw_tok, K)
        top_w = jax.nn.softmax(top_w, axis=-1)
        xf = x.reshape(N, D)
        h = jax.nn.gelu(jnp.einsum('nd,edf->enf', xf, W1) + b1[:, None, :], approximate=False)
        y = jnp.einsum('enf,efd->end', h, W2) + b2[:, None, :]
        w_dense = jnp.zeros((N, E), x.dtype).at[jnp.arange(N)[:, None], top_i].add(top_w)
        out = jnp.einsum('ne,end->nd', w_dense, y).reshape(B, S, D)
        out = _layer_norm(out + x, gamma, beta)
        return out
    h = _L0_tok_ref(x, L0_tok_W_embed, L0_tok_b_embed, L0_tok_W_gcn, L0_tok_b_gcn, L0_tok_W_out, L0_tok_b_out, L0_tok_edge_index)
    h = h + _L0_attn_ref(_layernorm(h, axis=-1), L0_attn_ln_gamma, L0_attn_ln_beta, L0_attn_W_qkv, L0_attn_W_gate, L0_attn_b_gate, L0_attn_W_final, L0_attn_b_final)
    h = h + _L0_ffn_ref(_layernorm(h, axis=-1), L0_ffn_route_id, L0_ffn_Wi, L0_ffn_bi, L0_ffn_Wr, L0_ffn_br, L0_ffn_Ws, L0_ffn_bs, L0_ffn_Wo, L0_ffn_bo)
    h = h + _L1_attn_ref(_layernorm(h, axis=-1), L1_attn_Wq, L1_attn_Wk, L1_attn_Wv, L1_attn_Wo)
    h = h + _L1_ffn_ref(_layernorm(h, axis=-1), L1_ffn_Wr, L1_ffn_br, L1_ffn_W1, L1_ffn_b1, L1_ffn_W2, L1_ffn_b2, L1_ffn_gamma, L1_ffn_beta)
    return h

_drawn_inputs = setup_inputs


def setup_inputs(seed=0):
    import zlib

    import numpy as np

    out = dict(_drawn_inputs(seed))
    spreads = {'L0_attn_ln_gamma': (1.0, 0.6),
     'L0_attn_ln_beta': (0.0, 0.8),
     'L0_attn_b_gate': (1.0, 0.6),
     'L0_attn_b_final': (0.0, 0.1),
     'L0_ffn_bi': (0.0, 0.583),
     'L0_ffn_bo': (0.0, 0.1),
     'L1_ffn_br': (0.0, 0.8),
     'L1_ffn_b1': (0.0, 1.778),
     'L1_ffn_b2': (0.0, 1.181),
     'L1_ffn_gamma': (1.0, 0.6),
     'L1_ffn_beta': (0.0, 0.718)}
    factors = {'x': 8.0,
     'L0_tok_W_embed': 8.0,
     'L0_tok_b_embed': 21.389,
     'L0_tok_W_gcn': 4.001,
     'L0_attn_W_gate': 8.0,
     'L0_ffn_Wi': 3.221,
     'L0_ffn_Wr': 7.512,
     'L0_ffn_br': 8.0,
     'L0_ffn_Ws': 7.789,
     'L0_ffn_bs': 8.0,
     'L1_attn_Wq': 8.0,
     'L1_attn_Wk': 8.0,
     'L1_attn_Wv': 8.0,
     'L1_attn_Wo': 8.0}
    for name, (base, spread) in spreads.items():
        noise = np.random.default_rng([zlib.crc32(name.encode()), seed]).standard_normal(out[name].shape)
        drawn = base * np.exp(spread * noise) if base else spread * noise
        out[name] = jnp.asarray(drawn.astype(out[name].dtype))
    for name, factor in factors.items():
        out[name] = (out[name] * factor).astype(out[name].dtype)
    return out
```

```python
from contextlib import ExitStack

import numpy as np

import concourse.bass as bass
from concourse import mybir

ALU = mybir.AluOpType
ACT = mybir.ActivationFunctionType
AX = mybir.AxisListType
F32 = mybir.dt.float32
F16 = mybir.dt.float16
BF16 = mybir.dt.bfloat16
I32 = mybir.dt.int32
U32 = mybir.dt.uint32

P = 128
GRID, PATCH, CH, IMG = 28, 8, 3, 224
N = GRID * GRID
HALF = N // 2
TP = 112
NT = N // TP
F = 64
EPS = 1e-5
LEAD = 2


def at(n, step=1):
    return (n + 1 + LEAD) * step


class Core:

    def __init__(self, nc, stack):
        self.nc, self.stack, self.sems = nc, stack, []
        stack.callback(self.free_semaphores)

    def free_semaphores(self):
        if self.sems:
            self.nc.clear_and_free_semaphores(self.sems)
            self.nc.all_engine_barrier()

    def sb(self, name, shape, dt=F32):
        return self.stack.enter_context(self.nc.sbuf_tensor(name, shape, dt))

    def ps(self, name, shape):
        return self.stack.enter_context(self.nc.psum_tensor(name, shape, F32))

    def sem(self, name):
        self.sems.append(self.nc.alloc_semaphore(name))
        return self.sems[-1]


def wide(slot):
    return slot[:, :, 0:HALF]


def halves(tile):
    return tile.rearrange("p (h n) -> p h n", h=2)


def flat(slot):
    return slot.rearrange("p h n -> p (h n)")


def lead(eng, sems, step=1):
    for s in sems:
        eng.sem_inc(s, LEAD * step)


def build_graph(core, slots, d, A):
    nc = core.nc
    KE = d["edges"].shape[2]
    with ExitStack() as st:
        c = Core(nc, st)
        ei = c.sb("ge_idx", [TP, 2, KE], I32)
        ef = c.sb("ge_idx_f", [TP, 2, KE])
        iota = c.sb("ge_iota", [TP, N])
        onesrc = c.sb("ge_onehot_src", [TP, KE, N], BF16)
        onedst = c.sb("ge_onehot_dst", [TP, KE, N], BF16)
        ones = c.sb("ge_ones", [TP, TP])
        rd = c.sb("ge_rdeg", [TP, N])
        rs = c.sb("ge_rdeg_src", [TP, 8])
        sd = c.sb("ge_sqrt", [TP, N])
        ss = c.sb("ge_sqrt_src", [TP, 8])
        loaded, ready, hot = c.sem("ge_loaded"), c.sem("ge_ready"), c.sem("ge_hot")
        counted, kept, degs = c.sem("ge_counted"), c.sem("ge_kept"), c.sem("ge_degs")
        rooted, inverted, scaled = c.sem("ge_rooted"), c.sem("ge_inverted"), c.sem("ge_scaled")
        with nc.Block() as block:

            @block.sync
            def _(sp):
                sp.dma_start(ei[:], d["edges"]).then_inc(loaded, 16)
                sp.dma_start(iota[:], d["iota"]).then_inc(loaded, 16)

            @block.vector
            def _(v):
                v.memset(ones[:], 1.0).then_inc(ready, 1)
                v.wait_ge(loaded, 32)
                v.tensor_copy(ef[:], ei[:]).then_inc(ready, 1)
                v.wait_ge(ready, 2)
                for k in range(KE):
                    v.tensor_scalar(onesrc[:, k, :], iota[:], ef[:, 0, k:k + 1], None, ALU.is_equal)
                    v.tensor_scalar(onedst[:, k, :], iota[:], ef[:, 1, k:k + 1], None,
                                    ALU.is_equal).then_inc(hot, 1)
                for t in range(NT):
                    v.wait_ge(counted, t + 1)
                    v.tensor_copy(halves(A[:, t, :]), wide(slots[t % 2])[0:TP]).then_inc(kept, 1)
                v.wait_ge(rooted, 2)
                v.reciprocal(rd[:], sd[:]).then_inc(inverted, 1)
                v.reciprocal(rs[:, 0:NT], ss[:, 0:NT]).then_inc(inverted, 1)
                v.wait_ge(inverted, 2)
                for t in range(NT):
                    v.scalar_tensor_tensor(A[:, t, :], A[:, t, :], rs[:, t:t + 1], rd[:],
                                           ALU.mult, ALU.mult).then_inc(scaled, 1)

            @block.tensor
            def _(pe):
                for t in range(NT):
                    if t >= 2:
                        pe.wait_ge(kept, t - 1)
                    for k in range(KE):
                        if t == 0:
                            pe.wait_ge(hot, k + 1)
                        for h in range(2):
                            mm = pe.matmul(slots[t % 2][0:TP, h, 0:HALF], onesrc[:, k, t * TP:(t + 1) * TP],
                                           onedst[:, k, h * HALF:(h + 1) * HALF],
                                           start=(k == 0), stop=(k == KE - 1))
                    mm.then_inc(counted, 1)
                pe.wait_ge(kept, NT)
                for h in range(2):
                    for t in range(NT):
                        pe.matmul(slots[2][0:TP, h, 0:HALF], ones[:], A[:, t, h * HALF:(h + 1) * HALF],
                                  start=(t == 0), stop=(t == NT - 1))
                for t in range(NT):
                    for k in range(NT):
                        mm = pe.matmul(slots[3][0:TP, 0, t:t + 1], A[:, k, t * TP:(t + 1) * TP], ones[:, 0:1],
                                       start=(k == 0), stop=(k == NT - 1))
                mm.then_inc(degs, 1)

            @block.scalar
            def _(act):
                act.wait_ge(degs, 1)
                act.activation(halves(sd[:]), wide(slots[2])[0:TP], ACT.Sqrt).then_inc(rooted, 1)
                act.activation(ss[:, 0:NT], slots[3][0:TP, 0, 0:NT], ACT.Sqrt).then_inc(rooted, 1)
                act.wait_ge(scaled, NT)


def tokens(core, slots, d, H, NP):
    nc = core.nc
    KR = 2 * CH * PATCH
    with ExitStack() as st:
        c = Core(nc, st)
        A = c.sb("tk_graph", [TP, NT, N])
        build_graph(core, slots, d, A)
        X = [c.sb(f"tk_x{i}", [TP, GRID, IMG]) for i in range(2)]
        We = c.sb("tk_we", [TP, PATCH // 2, P])
        Wg = c.sb("tk_wg", [P, 3, P])
        Wo = c.sb("tk_wo", [P, P])
        be, bg, bo = c.sb("tk_be", [P, 1]), c.sb("tk_bg", [P, 3]), c.sb("tk_bo", [P, 1])
        pos = c.sb("tk_pos", [P, N])
        h = [c.sb(f"tk_h{i}", [P, N]) for i in range(2)]
        hw = [c.sb(f"tk_hw{i}", [TP, NT, P]) for i in range(2)]
        cleared, weights = c.sem("tk_cleared"), c.sem("tk_weights")
        x_in = [c.sem(f"tk_x_in{i}") for i in range(2)]
        embedded = [c.sem(f"tk_embedded{i}") for i in range(2)]
        h_ready = [[c.sem(f"tk_h_ready{i}_{l}") for l in range(4)] for i in range(2)]
        projected = [[c.sem(f"tk_projected{i}_{l}") for l in range(3)] for i in range(2)]
        hw_ready = [[c.sem(f"tk_hw_ready{i}_{l}") for l in range(3)] for i in range(2)]
        spread = [[c.sem(f"tk_spread{i}_{l}") for l in range(3)] for i in range(2)]
        out_ready = [c.sem(f"tk_out_ready{i}") for i in range(2)]
        kept = [c.sem(f"tk_kept{i}") for i in range(2)]
        loops = NP // 2
        with nc.Block() as block:

            @block.gpsimd
            def _(pool):
                for w in (We, Wg, Wo, X[0], X[1]):
                    pool.memset(w[:], 0.0).then_inc(cleared, 1)

            @block.sync
            def _(sp):
                lead(sp, x_in, 32)
                sp.wait_ge(cleared, 5)
                wv = d["W_embed"].rearrange("(r s x) f -> r s x f", s=2, x=PATCH // 2)
                n = 0
                for q in range(2):
                    for s in range(2):
                        sp.dma_start(We[64 * s + 24 * q:64 * s + 24 * q + 24, :, F * q:F * q + F],
                                     wv[:, s]).then_inc(weights, 16)
                    o = F * q
                    sp.dma_start(Wg[o:o + F, :, o:o + F], d["W_gcn"].rearrange("l i o -> i l o")).then_inc(weights, 16)
                    sp.dma_start(Wo[o:o + F, o:o + F], d["W_out"]).then_inc(weights, 16)
                    sp.dma_start(be[o:o + F, :], d["b_embed"].unsqueeze(1)).then_inc(weights, 16)
                    sp.dma_start(bg[o:o + F, :], d["b_gcn"]).then_inc(weights, 16)
                    sp.dma_start(bo[o:o + F, :], d["b_out"].unsqueeze(1)).then_inc(weights, 16)
                    n += 7
                sp.dma_start(pos[:], d["pos"]).then_inc(weights, 16)
                xv = d["x"].rearrange("b c (i y) w -> (b c) y i w", y=PATCH)
                with sp.Fori(0, loops) as i:
                    for q in range(2):
                        sp.wait_ge(embedded[q], at(i - 1))
                        src = xv[bass.ds((2 * i + q) * 2 * CH, 2 * CH)]
                        for s in range(2):
                            w = IMG - 4 * s
                            for r in range(2 * CH):
                                p0 = 64 * s + PATCH * r
                                ins = sp.dma_start(X[q][p0:p0 + PATCH, :, 0:w],
                                                   xv[bass.ds((2 * i + q) * 2 * CH + r, 1), :, :, 4 * s:IMG]
                                                   .rearrange("a y i w -> (a y) i w"))
                                ins.then_inc(x_in[q], 16)

            XIN = 4 * CH * 16

            @block.tensor
            def _(pe):
                for q in range(2):
                    lead(pe, [embedded[q], out_ready[q]] + projected[q] + spread[q])
                pe.wait_ge(weights, 16 * 15)
                with pe.Fori(0, loops) as i:
                    for q in range(2):
                        pe.wait_ge(x_in[q], i * XIN + (XIN + 32 * LEAD))
                        for hf in range(2):
                            for x in range(PATCH // 2):
                                px = X[q][:, 14 * hf:14 * hf + 14, x:x + 8 * (GRID - 1) + 1:8]
                                mm = pe.matmul(slots[2 * q][:, hf, 0:HALF], We[:, x, :], px,
                                               start=(x == 0), stop=(x == 3))
                        mm.then_inc(embedded[q], 1)
                    for l in range(3):
                        for q in range(2):
                            pe.wait_ge(h_ready[q][l], at(i))
                            if l == 0:
                                pe.wait_ge(kept[q], at(i - 1))
                            for t in range(NT):
                                mm = pe.matmul(flat(slots[2 * q + 1])[0:TP, t * P:(t + 1) * P],
                                               h[q][:, t * TP:(t + 1) * TP], Wg[:, l, :], start=True, stop=True)
                            mm.then_inc(projected[q][l], 1)
                        for q in range(2):
                            pe.wait_ge(hw_ready[q][l], at(i))
                            for hf in range(2):
                                for t in range(NT):
                                    mm = pe.matmul(slots[2 * q][:, hf, 0:HALF], hw[q][:, t, :],
                                                   A[:, t, hf * HALF:(hf + 1) * HALF],
                                                   start=(t == 0), stop=(t == NT - 1))
                            mm.then_inc(spread[q][l], 1)
                    for q in range(2):
                        pe.wait_ge(h_ready[q][3], at(i))
                        for hf in range(2):
                            mm = pe.matmul(slots[2 * q + 1][:, hf, 0:HALF], Wo[:], h[q][:, hf * HALF:(hf + 1) * HALF],
                                           start=True, stop=True)
                        mm.then_inc(out_ready[q], 1)

            @block.scalar
            def _(act):
                for q in range(2):
                    lead(act, hw_ready[q])
                with act.Fori(0, loops) as i:
                    for l in range(3):
                        for q in range(2):
                            act.wait_ge(projected[q][l], at(i))
                            act.activation(hw[q][:].rearrange("p t f -> p (t f)"),
                                           flat(slots[2 * q + 1])[0:TP, 0:NT * P], ACT.Copy)\
                               .then_inc(hw_ready[q][l], 1)

            @block.vector
            def _(v):
                for q in range(2):
                    lead(v, h_ready[q] + [kept[q]])
                v.wait_ge(weights, 16 * 15)
                with v.Fori(0, loops) as i:
                    for q in range(2):
                        v.wait_ge(embedded[q], at(i))
                        v.wait_ge(out_ready[q], at(i - 1))
                        v.scalar_tensor_tensor(halves(h[q][:]), wide(slots[2 * q]), be[:, 0:1], halves(pos[:]),
                                               ALU.add, ALU.add).then_inc(h_ready[q][0], 1)
                    for l in range(3):
                        for q in range(2):
                            v.wait_ge(spread[q][l], at(i))
                            v.tensor_scalar(halves(h[q][:]), wide(slots[2 * q]), bg[:, l:l + 1], 0.0,
                                            ALU.add, ALU.max).then_inc(h_ready[q][l + 1], 1)
                    for q in range(2):
                        v.wait_ge(out_ready[q], at(i))
                        v.tensor_scalar(H[:, bass.ds(2 * i + q, 1), :].rearrange("p a (h n) -> p (a h) n", h=2),
                                        wide(slots[2 * q + 1]), bo[:, 0:1], None, ALU.add).then_inc(kept[q], 1)
                for q in range(2):
                    v.wait_ge(kept[q], at(loops - 1))


HEADS, HD = 8, 32
GROUPS, HG = 2, 4
RING = 3
ERING, VRING = 4, 2


class Steps:

    def __init__(self, order):
        self.order = order
        self.jobs = [s for s in order if s[0] in JOB_ENGINE]
        self.by = {e: [s for s in self.jobs if JOB_ENGINE[s[0]] == e] for e in ("act", "dve")}
        assert len(self.jobs) % RING == 0

    def filled(self, job):
        return self.jobs.index(job) + 1

    def emptied(self, job):
        return self.by[JOB_ENGINE[job[0]]].index(job) + 1


JOB_ENGINE = {"center": "dve", "var": "dve", "q": "dve", "k": "dve", "g": "act", "v0": "act", "v1": "act",
              "S": "act", "final": "dve"}


def attention_order():
    order = [("center",), ("var",)]
    units = [(q, g) for q in range(2) for g in range(GROUPS)]

    def prep(q, g):
        vs = [("v0", q), ("v1", q)] if g == 0 else []
        return [("q", q, g), ("k", q, g), ("g", q, g)] + vs

    order += prep(0, 0)
    for u, (q, g) in enumerate(units):
        for t in range(NT):
            order += [("S", q, g, t, h) for h in range(HG)]
            if t > 0:
                order.append(("pv", q, g, t - 1))
            if t == 2 and u + 1 < len(units):
                order += prep(*units[u + 1])
        order += [("pv", q, g, NT - 1), ("gated", q, g)]
        if g == GROUPS - 1:
            order.append(("final", q))
    return order


def attention(core, slots, d, H, NP):
    nc = core.nc
    O = Steps(attention_order())
    J, JA, JD = len(O.jobs), len(O.by["act"]), len(O.by["dve"])
    NS = 2 * GROUPS * NT * HG
    NM = 2 * GROUPS * NT
    S_INDEX = {s: n for n, s in enumerate([s for s in O.order if s[0] == "S"])}
    M_INDEX = {s[1:]: n for n, s in enumerate([s for s in O.order if s[0] == "pv"])}
    C = float(HD) ** -0.5
    ACC = slots[3]
    with ExitStack() as st:
        c = Core(nc, st)
        center, mean = c.sb("at_center", [P, P]), c.sb("at_mean", [P, P])
        W = c.sb("at_w", [P, 4 * HEADS * HD])
        Wf = c.sb("at_wf", [P, GROUPS, F])
        gamma, beta = c.sb("at_gamma", [P, 1]), c.sb("at_beta", [P, 1])
        bg, bf, eps = c.sb("at_bg", [P, GROUPS]), c.sb("at_bf", [P, 1]), c.sb("at_eps", [P, 1])
        t0, t1, t2 = (c.sb(f"at_t{i}", [P, N]) for i in range(3))
        r1, x1, xn, hx = c.sb("at_r1", [P, N]), c.sb("at_x1", [P, N]), c.sb("at_xn", [P, N]), c.sb("at_hx", [P, N])
        split = [[c.sb(f"at_split{w}{g}", [P, 2, N], F16) for g in range(GROUPS)] for w in range(2)]
        stack = [[c.sb(f"at_stack{w}{g}", [P, HG, N], F16) for g in range(GROUPS)] for w in range(2)]
        V = [c.sb(f"at_v{q}", [TP, NT, HEADS * HD]) for q in range(2)]
        gate = [c.sb(f"at_gate{g}", [P, N]) for g in range(GROUPS)]
        og = [c.sb(f"at_og{g}", [P, N]) for g in range(GROUPS)]
        E = c.sb("at_e", [TP, ERING, HG, N])
        vs = c.sb("at_vs", [TP, VRING, P])
        peak = c.sb("at_peak", [TP, 2 * HG])
        bias = c.sb("at_bias", [TP, 2 * HG])
        total = c.sb("at_total", [TP, 2, HG])
        inv = c.sb("at_inv", [TP, 2, HG])

        weights = c.sem("at_weights")
        prepared = c.sem("at_prepared")
        filled = c.sem("at_filled")
        act_done, dve_done = c.sem("at_act_done"), c.sem("at_dve_done")
        squared, rooted1, scaled1 = c.sem("at_squared"), c.sem("at_rooted1"), c.sem("at_scaled1")
        varied, rooted2, scaled2 = c.sem("at_varied"), c.sem("at_rooted2"), c.sem("at_scaled2")
        lns, lns2, normed, summed = c.sem("at_lns"), c.sem("at_lns2"), c.sem("at_normed"), c.sem("at_summed")
        high = c.sem("at_high")
        stacked = [c.sem(f"at_stacked{g}") for g in range(GROUPS)]
        peaked, biased, exped = c.sem("at_peaked"), c.sem("at_biased"), c.sem("at_exped")
        inverted, values = c.sem("at_inverted"), c.sem("at_values")
        pv_done, gated = c.sem("at_pv_done"), c.sem("at_gated")
        STACKED = 2 * 4 * HG * 16

        def job(i, s):
            return i * J + O.filled(s)

        def emptied(i, s):
            return i * len(O.by[JOB_ENGINE[s[0]]]) + O.emptied(s) + 1

        with nc.Block() as block:

            @block.sync
            def _(sp):
                for g in range(GROUPS):
                    sp.sem_inc(stacked[g], STACKED)
                n = HEADS * HD
                for q in range(2):
                    r = slice(F * q, F * q + F)
                    sp.dma_start(W[r, 0:3 * n], d["W_qkv_t"]).then_inc(weights, 16)
                    sp.dma_start(W[r, 3 * n:4 * n], d["W_gate_t"]).then_inc(weights, 16)
                    for tile, src in ((gamma, "gamma0"), (beta, "beta0"), (bf, "b_final")):
                        sp.dma_start(tile[r, :], d[src].unsqueeze(1)).then_inc(weights, 16)
                for g in range(GROUPS):
                    sp.dma_start(Wf[:, g, :], d["W_final_t"][g * P:(g + 1) * P]).then_inc(weights, 16)
                    sp.dma_start(bg[:, g:g + 1], d["b_gate"][g * P:(g + 1) * P].unsqueeze(1)).then_inc(weights, 16)
                sp.dma_start(center[:], d["center"]).then_inc(weights, 16)
                sp.dma_start(mean[:], d["mean"]).then_inc(weights, 16)
                with sp.Fori(0, NP) as i:
                    for s in O.order:
                        if s[0] != "k":
                            continue
                        _, q, g = s
                        sp.wait_ge(dve_done, emptied(i, s))
                        for w, parts in enumerate(((0, 0, 1, 1), (0, 1, 0, 1))):
                            for b, part in enumerate(parts):
                                for h in range(HG):
                                    sp.dma_start(stack[w][g][HD * b:HD * b + HD, h, :],
                                                 split[w][g][HD * h:HD * h + HD, part, :])\
                                      .then_inc(stacked[g], 16)

            WEIGHTS = 16 * 16

            @block.tensor
            def _(pe):
                pe.sem_inc(pv_done, ERING)
                pe.wait_ge(weights, WEIGHTS)
                pe.wait_ge(prepared, 3)
                with pe.Fori(0, NP) as i:
                    for s in O.order:
                        kind = s[0]
                        if kind in JOB_ENGINE:
                            n = O.jobs.index(s)
                            slot = slots[n % RING]
                            if n >= RING:
                                old = O.jobs[n - RING]
                                pe.wait_ge({"act": act_done, "dve": dve_done}[JOB_ENGINE[old[0]]], emptied(i, old))
                        if kind == "center":
                            pe.wait_ge(act_done, i * JA + 1)
                            pe.wait_ge(dve_done, i * JD + 1)
                            for hf in range(2):
                                mm = pe.matmul(slot[:, hf, 0:HALF], center[:],
                                               H[:, bass.ds(i, 1), hf * HALF:(hf + 1) * HALF].rearrange("p a n -> p (a n)"),
                                               start=True, stop=True)
                        elif kind == "var":
                            pe.wait_ge(squared, i + 1)
                            for hf in range(2):
                                mm = pe.matmul(slot[:, hf, 0:HALF], mean[:], t0[:, hf * HALF:(hf + 1) * HALF],
                                               start=True, stop=True)
                        elif kind in ("q", "k", "g"):
                            _, q, g = s
                            if (kind, q, g) == ("q", 0, 0):
                                pe.wait_ge(normed, i + 1)
                            col = {"q": 0, "k": 1, "g": 3}[kind] * HEADS * HD + g * P
                            src = x1 if kind == "g" else xn
                            for hf in range(2):
                                mm = pe.matmul(slot[:, hf, 0:HALF], W[F * q:F * q + F, col:col + P],
                                               src[F * q:F * q + F, hf * HALF:(hf + 1) * HALF], start=True, stop=True)
                        elif kind in ("v0", "v1"):
                            q = s[1]
                            tiles = range(0, 4) if kind == "v0" else range(4, NT)
                            for k, t in enumerate(tiles):
                                mm = pe.matmul(flat(slot)[0:TP, k * 256:(k + 1) * 256],
                                               xn[F * q:F * q + F, t * TP:(t + 1) * TP],
                                               W[F * q:F * q + F, 512:768], start=True, stop=True)
                        elif kind == "S":
                            _, q, g, t, h = s
                            if (t, h) == (0, 0):
                                pe.wait_ge(stacked[g], i * 2 * STACKED + (q + 2) * STACKED)
                            for hf in range(2):
                                mm = pe.matmul(slot[0:TP, hf, 0:HALF], stack[0][g][:, h, t * TP:(t + 1) * TP],
                                               stack[1][g][:, h, hf * HALF:(hf + 1) * HALF], start=True, stop=True)
                        elif kind == "pv":
                            _, q, g, t = s
                            m = M_INDEX[s[1:]]
                            pe.wait_ge(values, i * NM + m + 1 + VRING)
                            if t == 0:
                                pe.wait_ge(gated, i * 4 + 2 * q + g + 2)
                            for hf in range(2):
                                for h in range(HG):
                                    mm = pe.matmul(ACC[HD * h:HD * h + HD, hf, 0:HALF],
                                                   vs[:, m % VRING, HD * h:HD * h + HD],
                                                   E[:, m % ERING, h, hf * HALF:(hf + 1) * HALF],
                                                   start=(t == 0), stop=(t == NT - 1))
                            mm.then_inc(pv_done, 1)
                        elif kind == "final":
                            q = s[1]
                            pe.wait_ge(gated, i * 4 + 2 * q + 4)
                            for hf in range(2):
                                for g in range(GROUPS):
                                    mm = pe.matmul(slot[F * q:F * q + F, hf, 0:HALF], Wf[:, g, :],
                                                   og[g][:, hf * HALF:(hf + 1) * HALF],
                                                   start=(g == 0), stop=(g == GROUPS - 1))
                        if kind in JOB_ENGINE:
                            mm.then_inc(filled, 1)

            @block.scalar
            def _(act):
                act.sem_inc(act_done, 1)
                act.wait_ge(prepared, 3)
                with act.Fori(0, NP) as i:
                    for s in O.order:
                        kind = s[0]
                        if kind in JOB_ENGINE:
                            slot = slots[O.jobs.index(s) % RING]
                        if kind == "center":
                            act.wait_ge(filled, job(i, s))
                            act.activation(halves(t0[:]), wide(slot), ACT.Square).then_inc(squared, 1)
                        elif kind == "var":
                            act.wait_ge(filled, job(i, s))
                            act.activation(halves(t0[:]), wide(slot), ACT.Ln, bias=eps[:, 0:1]).then_inc(lns, 1)
                            act.wait_ge(lns, i + 1)
                            act.activation(t1[:], t0[:], ACT.Exp, scale=-1.0).then_inc(rooted1, 1)
                            act.activation(r1[:], t0[:], ACT.Exp, scale=-0.5).then_inc(rooted1, 1)
                            act.wait_ge(varied, i + 1)
                            act.activation(t0[:], t2[:], ACT.Ln, bias=eps[:, 0:1]).then_inc(lns2, 1)
                            act.wait_ge(lns2, i + 1)
                            act.activation(t1[:], t0[:], ACT.Exp, scale=-0.5).then_inc(rooted2, 1)
                        elif kind in ("q", "k"):
                            _, q, g = s
                            w = 0 if kind == "q" else 1
                            act.wait_ge(filled, job(i, s))
                            act.wait_ge(stacked[g], i * 2 * STACKED + (q + 1) * STACKED)
                            act.activation(halves(split[w][g][:, 0, :]), wide(slot), ACT.Copy,
                                           scale=C if w == 0 else 1.0).then_inc(high, 1)
                        elif kind == "g":
                            _, q, g = s
                            act.wait_ge(filled, job(i, s))
                            act.wait_ge(gated, i * 4 + 2 * q + g + 1)
                            act.activation(halves(gate[g][:]), wide(slot), ACT.Tanh, bias=bg[:, g:g + 1],
                                           scale=0.5).then_inc(act_done, 1)
                        elif kind in ("v0", "v1"):
                            q, k, t = s[1], (4 if kind == "v0" else 3), (0 if kind == "v0" else 4)
                            act.wait_ge(filled, job(i, s))
                            act.activation(V[q][:, t:t + k, :].rearrange("p t c -> p (t c)"),
                                           flat(slot)[0:TP, 0:k * 256], ACT.Copy).then_inc(act_done, 1)
                        elif kind == "S":
                            _, q, g, t, h = s
                            n, m = S_INDEX[s], M_INDEX[(q, g, t)]
                            act.wait_ge(biased, i * NS + n + 1)
                            if h == 0:
                                act.wait_ge(pv_done, i * NM + m + 1)
                                act.wait_ge(inverted, i * NM + m + 1)
                            act.activation(halves(E[:, m % ERING, h, :]), wide(slot)[0:TP], ACT.Exp,
                                           bias=bias[:, n % 8:n % 8 + 1], scale=1.0,
                                           accum_out=total[:, m % 2, h:h + 1]).then_inc(act_done, 1)

            @block.vector
            def _(v):
                v.sem_inc(dve_done, 1)
                v.sem_inc(gated, 2)
                v.sem_inc(inverted, 2)
                v.memset(eps[:], EPS).then_inc(prepared, 1)
                v.wait_ge(weights, WEIGHTS)
                v.tensor_scalar(bg[:], bg[:], 0.5, None, ALU.mult).then_inc(prepared, 1)
                v.tensor_scalar(Wf[:], Wf[:], 0.5, None, ALU.mult).then_inc(prepared, 1)
                v.wait_ge(prepared, 3)

                def sums(i, s):
                    m = M_INDEX[s]
                    v.wait_ge(act_done, emptied(i, ("S",) + s + (HG - 1,)))
                    v.wait_ge(values, i * NM + m + 1)
                    v.reciprocal(inv[:, m % 2, :], total[:, m % 2, :]).then_inc(inverted, 1)

                with v.Fori(0, NP) as i:
                    for s in O.order:
                        kind = s[0]
                        if kind in JOB_ENGINE:
                            slot = slots[O.jobs.index(s) % RING]
                        if kind == "var":
                            before = slots[O.jobs.index(s) - 1]
                            v.wait_ge(rooted1, 2 * i + 2)
                            v.tensor_tensor(halves(x1[:]), wide(before), halves(r1[:]), ALU.mult).then_inc(dve_done, 1)
                            v.tensor_tensor(halves(t2[:]), wide(slot), halves(t1[:]), ALU.mult).then_inc(varied, 1)
                            v.wait_ge(varied, i + 1)
                            v.wait_ge(rooted2, i + 1)
                            v.wait_ge(dve_done, 1 + i * JD + 1)
                            v.tensor_tensor(t1[:], t1[:], x1[:], ALU.mult).then_inc(scaled2, 1)
                            v.wait_ge(scaled2, i + 1)
                            v.tensor_scalar(xn[:], t1[:], gamma[:, 0:1], beta[:, 0:1], ALU.mult, ALU.add)\
                             .then_inc(normed, 1)
                            v.tensor_tensor(hx[:], H[:, bass.ds(i, 1), :].rearrange("p a n -> p (a n)"), x1[:],
                                            ALU.add).then_inc(dve_done, 1)
                        elif kind in ("q", "k"):
                            _, q, g = s
                            w = 0 if kind == "q" else 1
                            nth = [x for x in O.order if x[0] in ("q", "k")].index(s)
                            v.wait_ge(high, i * 8 + nth + 1)
                            v.scalar_tensor_tensor(halves(split[w][g][:, 1, :]), wide(slot), C if w == 0 else 1.0,
                                                   halves(split[w][g][:, 0, :]), ALU.mult, ALU.subtract)\
                             .then_inc(dve_done, 1)
                        elif kind == "S":
                            n = S_INDEX[s]
                            v.wait_ge(filled, job(i, s))
                            v.tensor_reduce(bias[:, n % 8:n % 8 + 1], wide(slot)[0:TP], AX.XY, ALU.max, negate=True)\
                             .then_inc(biased, 1)
                        elif kind == "pv":
                            sums(i, s[1:])
                        elif kind == "gated":
                            _, q, g = s
                            m = M_INDEX[(q, g, NT - 1)]
                            v.wait_ge(pv_done, i * NM + m + 1 + ERING)
                            v.scalar_tensor_tensor(halves(og[g][:]), halves(gate[g][:]), 1.0, wide(ACC),
                                                   ALU.add, ALU.mult).then_inc(gated, 1)
                        elif kind == "final":
                            q = s[1]
                            r = slice(F * q, F * q + F)
                            v.wait_ge(filled, job(i, s))
                            v.scalar_tensor_tensor(
                                H[r, bass.ds(i, 1), :].rearrange("p a (h n) -> p (a h) n", h=2), wide(slot)[r],
                                bf[r, 0:1], halves(hx[r, :]), ALU.add, ALU.add).then_inc(dve_done, 1)

            @block.gpsimd
            def _(pool):
                pool.sem_inc(values, VRING)
                with pool.Fori(0, NP) as i:
                    for s in O.order:
                        if s[0] != "pv":
                            continue
                        _, q, g, t = s
                        m = M_INDEX[s[1:]]
                        pool.wait_ge(inverted, i * NM + m + 1 + 2)
                        pool.wait_ge(pv_done, i * NM + m + 1 + ERING - VRING)
                        pool.tensor_tensor(vs[:, m % VRING, :].rearrange("p (h c) -> p h c", h=HG),
                                           V[q][:, t, g * P:(g + 1) * P].rearrange("p (h c) -> p h c", h=HG),
                                           inv[:, m % 2, :].unsqueeze(2).broadcast_to([TP, HG, HD]), ALU.mult)\
                            .then_inc(values, 1)


HID, LAYERS = 128, 2


def routed_ffn(core, slots, d, H, NP):
    nc = core.nc
    NE = d["Wr_t"].shape[1]
    SEG = 4
    with ExitStack() as st:
        c = Core(nc, st)
        center, mean = c.sb("rf_center", [P, P]), c.sb("rf_mean", [P, P])
        Wi = c.sb("rf_wi", [P, HID])
        bi, bo, eps = c.sb("rf_bi", [P, 1]), c.sb("rf_bo", [P, 1]), c.sb("rf_eps", [P, 1])
        Wo = c.sb("rf_wo", [P, F])
        table = c.sb("rf_table", [P, NE + 1, LAYERS, HID + 1])
        shared = c.sb("rf_shared", [P, LAYERS, HID + 1])
        eye = c.sb("rf_eye", [P, P])
        ids = c.sb("rf_ids", [1, 2 * 2 * NP], I32)
        idf = c.sb("rf_idf", [1, 3, 2 * 2 * NP])
        chosen = [c.sb(f"rf_chosen{k}", [P, SEG, LAYERS, HID + 1]) for k in range(2)]
        t0 = [c.sb(f"rf_t{k}", [P, N]) for k in range(2)]
        r1 = [c.sb(f"rf_r{k}", [P, N]) for k in range(2)]
        xn = [c.sb(f"rf_xn{k}", [P, N]) for k in range(2)]
        a = [[c.sb(f"rf_a{k}{q}", [P, N]) for q in range(2)] for k in range(2)]
        weights, tables, routed = c.sem("rf_weights"), c.sem("rf_tables"), c.sem("rf_routed")
        sems = lambda name: [c.sem(f"rf_{name}{k}") for k in range(2)]
        centered, squared, varied, logged, rooted, normed = map(
            sems, ("centered", "squared", "varied", "logged", "rooted", "normed"))
        widened, hidden = sems("widened"), sems("hidden")
        mixed = [[c.sem(f"rf_mixed{k}_{l}") for l in range(LAYERS)] for k in range(2)]
        left = [[c.sem(f"rf_left{k}_{l}") for l in range(LAYERS)] for k in range(2)]
        right = [[c.sem(f"rf_right{k}_{l}") for l in range(LAYERS)] for k in range(2)]
        projected, kept, gathered = sems("projected"), sems("kept"), sems("gathered")
        loops = NP // 2
        WEIGHTS = 16 * (2 * 2 + 5 + 5)

        with nc.Block() as block:

            @block.sync
            def _(sp):
                for q in range(2):
                    sp.dma_start(Wi[F * q:F * q + F, :], d["Wi_t"]).then_inc(weights, 16)
                    sp.dma_start(bo[F * q:F * q + F, :], d["bo"].unsqueeze(1)).then_inc(weights, 16)
                for tile, src in ((bi, d["bi"].unsqueeze(1)), (Wo, d["Wo_t"]), (center, d["center"]),
                                  (mean, d["mean"]), (eye, d["eye"])):
                    sp.dma_start(tile[:], src).then_inc(weights, 16)
                for l in range(LAYERS):
                    sp.dma_start(table[:, 0:NE, l, 0:HID], d["Wr_t"][:, :, l]).then_inc(weights, 16)
                sp.dma_start(shared[:, :, 0:HID], d["Ws"]).then_inc(weights, 16)
                with nc.allow_non_contiguous_dma(reason="a bias column per expert"):
                    sp.dma_start(table[:, 0:NE, :, HID:HID + 1], d["br_t"].unsqueeze(3)).then_inc(weights, 16)
                    sp.dma_start(shared[:, :, HID:HID + 1], d["bs"].unsqueeze(2)).then_inc(weights, 16)
                sp.dma_start(ids[:], d["route"]).then_inc(routed, 16)

            @block.gpsimd
            def _(pool):
                for k in range(2):
                    pool.sem_inc(gathered[k], LEAD)
                pool.wait_ge(tables, 4)
                with pool.Fori(0, loops) as i:
                    for k in range(2):
                        pool.wait_ge(projected[k], at(i - 1))
                        for s in range(SEG):
                            e = pool.value_load(ids[0:1, bass.ds(i * 8 + (SEG * k + s), 1)], min_val=0, max_val=NE)
                            copy = pool.tensor_copy(chosen[k][:, s, :, :].rearrange("p l f -> p (l f)"),
                                                    table[:, bass.ds(e, 1), :, :].rearrange("p a l f -> p (a l f)"))
                        copy.then_inc(gathered[k], 1)

            @block.tensor
            def _(pe):
                for k in range(2):
                    lead(pe, [centered[k], varied[k], projected[k]])
                    lead(pe, [widened[k]] + mixed[k], 2)
                pe.wait_ge(weights, WEIGHTS)
                with pe.Fori(0, loops) as i:
                    for k in range(2):
                        pe.wait_ge(kept[k], at(i - 1))
                        for hf in range(2):
                            mm = pe.matmul(slots[2 * k][:, hf, 0:HALF], center[:],
                                           H[:, bass.ds(2 * i + k, 1), hf * HALF:(hf + 1) * HALF]
                                           .rearrange("p a n -> p (a n)"), start=True, stop=True)
                        mm.then_inc(centered[k], 1)
                    for k in range(2):
                        pe.wait_ge(squared[k], at(i))
                        for hf in range(2):
                            mm = pe.matmul(slots[2 * k + 1][:, hf, 0:HALF], mean[:], t0[k][:, hf * HALF:(hf + 1) * HALF],
                                           start=True, stop=True)
                        mm.then_inc(varied[k], 1)
                    for k in range(2):
                        pe.wait_ge(normed[k], at(i))
                        for q in range(2):
                            for hf in range(2):
                                mm = pe.matmul(slots[2 * k + q][:, hf, 0:HALF], Wi[F * q:F * q + F, :],
                                               xn[k][F * q:F * q + F, hf * HALF:(hf + 1) * HALF], start=True, stop=True)
                            mm.then_inc(widened[k], 1)
                    for l in range(LAYERS):
                        for k in range(2):
                            if l == 0:
                                pe.wait_ge(gathered[k], at(i))
                            for q in range(2):
                                if l == 0:
                                    pe.wait_ge(hidden[k], 2 * i + q + 1 + 2 * LEAD)
                                else:
                                    pe.wait_ge(left[k][0], 2 * i + q + 1 + 2 * LEAD)
                                    pe.wait_ge(right[k][0], 2 * i + q + 1 + 2 * LEAD)
                                for hf in range(2):
                                    mm = pe.matmul(slots[2 * k + q][:, hf, 0:HALF], chosen[k][:, 2 * q + hf, l, 0:HID],
                                                   a[k][q][:, hf * HALF:(hf + 1) * HALF], start=True, stop=True)
                                mm.then_inc(mixed[k][l], 1)
                    for k in range(2):
                        pe.wait_ge(left[k][1], 2 * i + 2 + 2 * LEAD)
                        pe.wait_ge(right[k][1], 2 * i + 2 + 2 * LEAD)
                        for hf in range(2):
                            for q in range(2):
                                mm = pe.matmul(slots[2 * k][F * q:F * q + F, hf, 0:HALF], Wo[:],
                                               a[k][q][:, hf * HALF:(hf + 1) * HALF], start=True, stop=True)
                        mm.then_inc(projected[k], 1)

            @block.scalar
            def _(act):
                for k in range(2):
                    lead(act, [squared[k], logged[k], rooted[k]])
                    lead(act, [hidden[k]] + left[k], 2)
                act.wait_ge(tables, 4)
                with act.Fori(0, loops) as i:
                    for k in range(2):
                        act.wait_ge(centered[k], at(i))
                        act.activation(halves(t0[k][:]), wide(slots[2 * k]), ACT.Square).then_inc(squared[k], 1)
                    for k in range(2):
                        act.wait_ge(varied[k], at(i))
                        act.activation(halves(r1[k][:]), wide(slots[2 * k + 1]), ACT.Ln, bias=eps[:, 0:1])\
                           .then_inc(logged[k], 1)
                    for k in range(2):
                        act.wait_ge(logged[k], at(i))
                        act.activation(t0[k][:], r1[k][:], ACT.Exp, scale=-0.5).then_inc(rooted[k], 1)
                    for k in range(2):
                        for q in range(2):
                            act.wait_ge(widened[k], 2 * i + q + 1 + 2 * LEAD)
                            act.activation(halves(a[k][q][:]), wide(slots[2 * k + q]), ACT.Relu, bias=bi[:, 0:1])\
                               .then_inc(hidden[k], 1)
                    for l in range(LAYERS):
                        for k in range(2):
                            for q in range(2):
                                act.wait_ge(mixed[k][l], 2 * i + q + 1 + 2 * LEAD)
                                act.activation(a[k][q][:, 0:HALF], slots[2 * k + q][:, 0, 0:HALF], ACT.Relu,
                                               bias=chosen[k][:, 2 * q, l, HID:HID + 1]).then_inc(left[k][l], 1)

            @block.vector
            def _(v):
                for k in range(2):
                    lead(v, [normed[k], kept[k]])
                    lead(v, right[k], 2)
                v.memset(eps[:], EPS).then_inc(tables, 1)
                v.memset(table[:, NE, :, :], 0.0).then_inc(tables, 1)
                v.wait_ge(weights, WEIGHTS)
                v.tensor_tensor(shared[:, :, 0:HID], shared[:, :, 0:HID],
                                eye[:].unsqueeze(1).broadcast_to([P, LAYERS, HID]), ALU.add).then_inc(tables, 1)
                v.wait_ge(tables, 3)
                for l in range(LAYERS):
                    ins = v.tensor_tensor(table[:, :, l, :], table[:, :, l, :],
                                          shared[:, l, :].unsqueeze(1).broadcast_to([P, NE + 1, HID + 1]), ALU.add)
                v.wait_ge(routed, 16)
                v.tensor_copy(idf[:, 0, :], ids[:]).then_inc(routed, 1)
                v.wait_ge(routed, 17)
                v.tensor_scalar(idf[:, 1, :], idf[:, 0, :], 0.0, None, ALU.is_ge).then_inc(routed, 1)
                v.tensor_scalar(idf[:, 2, :], idf[:, 0, :], float(NE), None, ALU.is_lt).then_inc(routed, 1)
                v.wait_ge(routed, 19)
                v.tensor_tensor(idf[:, 1, :], idf[:, 1, :], idf[:, 2, :], ALU.mult).then_inc(routed, 1)
                v.tensor_scalar(idf[:, 0, :], idf[:, 0, :], float(NE), None, ALU.subtract).then_inc(routed, 1)
                v.wait_ge(routed, 21)
                v.tensor_tensor(idf[:, 0, :], idf[:, 0, :], idf[:, 1, :], ALU.mult).then_inc(routed, 1)
                v.wait_ge(routed, 22)
                v.tensor_scalar(ids[:], idf[:, 0, :], float(NE), None, ALU.add).then_inc(tables, 1)
                with v.Fori(0, loops) as i:
                    for k in range(2):
                        v.wait_ge(rooted[k], at(i))
                        v.tensor_tensor(halves(xn[k][:]), wide(slots[2 * k]), halves(t0[k][:]), ALU.mult)\
                         .then_inc(normed[k], 1)
                    for l in range(LAYERS):
                        for k in range(2):
                            for q in range(2):
                                v.wait_ge(mixed[k][l], 2 * i + q + 1 + 2 * LEAD)
                                v.tensor_scalar(a[k][q][:, HALF:N], slots[2 * k + q][:, 1, 0:HALF],
                                                chosen[k][:, 2 * q + 1, l, HID:HID + 1], 0.0, ALU.add, ALU.max)\
                                 .then_inc(right[k][l], 1)
                    for k in range(2):
                        v.wait_ge(projected[k], at(i))
                        h = H[:, bass.ds(2 * i + k, 1), :].rearrange("p a (h n) -> p (a h) n", h=2)
                        v.scalar_tensor_tensor(h, wide(slots[2 * k]), bo[:, 0:1], h, ALU.add, ALU.add)\
                         .then_inc(kept[k], 1)


CUT = 448


def causal_attention(core, slots, d, H, X, sums, NP):
    nc = core.nc
    with ExitStack() as st:
        c = Core(nc, st)
        center, mean, eps = c.sb("ca_center", [P, P]), c.sb("ca_mean", [P, P]), c.sb("ca_eps", [P, 1])
        W = c.sb("ca_w", [F, 4, F])
        A, Bv = c.sb("ca_a", [P, P]), c.sb("ca_b", [P, P])
        ab = c.sb("ca_ab", [F, 2, F])
        causal = c.sb("ca_causal", [TP, TP])
        per_row = c.sb("ca_per_row", [P, N])
        t0, r1 = [c.sb(f"ca_t{k}", [P, N]) for k in range(2)], [c.sb(f"ca_r{k}", [P, N]) for k in range(2)]
        xn = [c.sb(f"ca_xn{k}", [P, N]) for k in range(2)]
        U = [c.sb(f"ca_u{k}", [P, N]) for k in range(2)]
        V = [c.sb(f"ca_v{k}", [TP, NT, P]) for k in range(2)]
        PB = 4
        prob = c.sb("ca_prob", [TP, PB, N])
        weights, ready = c.sem("ca_weights"), c.sem("ca_ready")
        sems = lambda name: [c.sem(f"ca_{name}{k}") for k in range(2)]
        centered, squared, varied, logged, rooted, normed = map(
            sems, ("centered", "squared", "varied", "logged", "rooted", "normed"))
        turned, scaled, valued, v_ready = map(sems, ("turned", "scaled", "valued", "v_ready"))
        scored, diag, rest = c.sem("ca_scored"), c.sem("ca_diag"), c.sem("ca_rest")
        used = c.sem("ca_used")
        kept, last = sems("kept"), sems("last")
        centered2, squared2, varied2, logged2, rooted2 = map(
            sems, ("centered2_", "squared2_", "varied2_", "logged2_", "rooted2_"))
        loops = NP // 2
        NS = 2 * 2 * NT
        tiles = [(k, m, q) for k in range(2) for m in range(NT) for q in range(2)]

        NR = sum(m * TP < CUT for _, m, _ in tiles)

        def rests(n):
            return sum(m * TP < CUT for _, m, _ in tiles[:n + 1])

        def parts(lo):
            return [(b, max(lo, CUT * b) - CUT * b, (CUT, N - CUT)[b], CUT * b) for b in range(2)
                    if lo < (CUT, N)[b]]

        with nc.Block() as block:

            @block.sync
            def _(sp):
                for j, name in enumerate(("Wq", "Wk", "Wv", "Wo1_t")):
                    sp.dma_start(W[:, j, :], d[name]).then_inc(weights, 16)
                for tile, name in ((center, "center"), (mean, "mean"), (causal, "causal"), (per_row, "per_row")):
                    sp.dma_start(tile[:], d[name]).then_inc(weights, 16)
                sp.wait_ge(ready, 5)
                for j, tile in enumerate((A, Bv)):
                    for q in range(2):
                        r = slice(F * q, F * q + F)
                        sp.dma_start(tile[r, r], ab[:, j, :]).then_inc(weights, 16)

            @block.gpsimd
            def _(pool):
                pool.memset(A[:], 0.0).then_inc(ready, 1)
                pool.memset(Bv[:], 0.0).then_inc(ready, 1)

            def norm_mm(pe, i, k, lhs, src, slot, wait, value, done):
                pe.wait_ge(wait, value)
                for hf in range(2):
                    mm = pe.matmul(slot[:, hf, 0:HALF], lhs[:], src[:, hf * HALF:(hf + 1) * HALF], start=True, stop=True)
                mm.then_inc(done, 1)

            @block.tensor
            def _(pe):
                for k in range(2):
                    lead(pe, [centered[k], varied[k], turned[k], valued[k], centered2[k], varied2[k]])
                pe.sem_inc(used, PB)
                pe.wait_ge(weights, 16 * 8)
                pe.matmul(slots[0][0:F, 0, 0:F], W[:, 0, :], W[:, 1, :], start=True, stop=True)
                pe.matmul(slots[0][0:F, 0, F:2 * F], W[:, 2, :], W[:, 3, :], start=True, stop=True).then_inc(ready, 1)
                pe.wait_ge(weights, 16 * 12)
                with pe.Fori(0, loops) as i:
                    for k in range(2):
                        norm_mm(pe, i, k, center, H[:, bass.ds(2 * i + k, 1), :].rearrange("p a n -> p (a n)"),
                                slots[k], last[k], at(i - 1), centered[k])
                    for k in range(2):
                        norm_mm(pe, i, k, mean, t0[k], slots[2 + k], squared[k], at(i), varied[k])
                    for k in range(2):
                        norm_mm(pe, i, k, A, xn[k], slots[k], normed[k], at(i), turned[k])
                        for t in range(NT):
                            mm = pe.matmul(flat(slots[2 + k])[0:TP, t * P:(t + 1) * P], xn[k][:, t * TP:(t + 1) * TP],
                                           Bv[:], start=True, stop=True)
                        mm.then_inc(valued[k], 1)

                    def scores(n):
                        k, m, q = tiles[n]
                        slot = slots[n % 3]
                        if n < 3:
                            pe.wait_ge(scaled[1], at(i))
                            pe.wait_ge(v_ready[0], at(i))
                        else:
                            pe.wait_ge(diag, i * NS + n - 2)
                            pe.wait_ge(rest, i * NR + rests(n - 3))
                        for b, lo, hi, c0 in parts(m * TP):
                            mm = pe.matmul(slot[0:TP, b, lo:hi], xn[k][F * q:F * q + F, m * TP:(m + 1) * TP],
                                           U[k][F * q:F * q + F, c0 + lo:c0 + hi], start=True, stop=True)
                        mm.then_inc(scored, 1)

                    def values(n):
                        k, m, _ = tiles[n]
                        if m == 0:
                            pe.wait_ge(v_ready[1], at(i))
                            if k == 1:
                                pe.wait_ge(kept[0], at(i))
                        pe.wait_ge(diag, i * NS + n + 2)
                        pe.wait_ge(rest, i * NR + rests(n + 1))
                        for b, lo, hi, c0 in parts(m * TP):
                            for q in range(2):
                                mm = pe.matmul(slots[3][F * q:F * q + F, b, lo:hi], V[k][:, m, F * q:F * q + F],
                                               prob[:, (n + q) % PB, c0 + lo:c0 + hi],
                                               start=(m == 0), stop=(m == (3 if b == 0 else NT - 1)))
                        mm.then_inc(used, 2)

                    for n in range(0, NS, 2):
                        scores(n)
                        scores(n + 1)
                        if n >= 2:
                            values(n - 2)
                    values(NS - 2)
                    for k in range(2):
                        norm_mm(pe, i, k, center, H[:, bass.ds(2 * i + k, 1), :].rearrange("p a n -> p (a n)"),
                                slots[k], kept[k], at(i), centered2[k])
                    for k in range(2):
                        norm_mm(pe, i, k, mean, t0[k], slots[2 + k], squared2[k], at(i), varied2[k])

            @block.scalar
            def _(act):
                for k in range(2):
                    lead(act, [squared[k], logged[k], rooted[k], v_ready[k], squared2[k], logged2[k], rooted2[k]])
                act.wait_ge(ready, 4)
                with act.Fori(0, loops) as i:

                    def inverse_root(centered, squared, varied, logged, rooted):
                        for k in range(2):
                            act.wait_ge(centered[k], at(i))
                            act.activation(halves(t0[k][:]), wide(slots[k]), ACT.Square).then_inc(squared[k], 1)
                        for k in range(2):
                            act.wait_ge(varied[k], at(i))
                            act.activation(halves(r1[k][:]), wide(slots[2 + k]), ACT.Ln, bias=eps[:, 0:1])\
                               .then_inc(logged[k], 1)
                        for k in range(2):
                            act.wait_ge(logged[k], at(i))
                            act.activation(t0[k][:], r1[k][:], ACT.Exp, scale=-0.5).then_inc(rooted[k], 1)

                    inverse_root(centered, squared, varied, logged, rooted)
                    for k in range(2):
                        act.wait_ge(valued[k], at(i))
                        act.activation(V[k][:].rearrange("p t f -> p (t f)"), flat(slots[2 + k])[0:TP, 0:NT * P],
                                       ACT.Copy).then_inc(v_ready[k], 1)
                    for n, (k, m, q) in enumerate(tiles):
                        if m * TP >= CUT:
                            continue
                        act.wait_ge(scored, i * NS + n + 1)
                        act.wait_ge(used, i * NS + n // 2 * 2 + 2)
                        act.activation(prob[:, n % PB, CUT:N], slots[n % 3][0:TP, 1, 0:N - CUT], ACT.Relu)\
                           .then_inc(rest, 1)
                    inverse_root(centered2, squared2, varied2, logged2, rooted2)

            @block.vector
            def _(v):
                for k in range(2):
                    lead(v, [normed[k], scaled[k], kept[k], last[k]])
                v.memset(eps[:], EPS).then_inc(ready, 1)
                v.wait_ge(ready, 4)
                v.tensor_copy(ab[:].rearrange("p a f -> p (a f)"), slots[0][0:F, 0, 0:2 * F]).then_inc(ready, 1)
                with v.Fori(0, loops) as i:
                    for k in range(2):
                        v.wait_ge(rooted[k], at(i))
                        v.tensor_tensor(halves(xn[k][:]), wide(slots[k]), halves(t0[k][:]), ALU.mult)\
                         .then_inc(normed[k], 1)
                    for k in range(2):
                        v.wait_ge(turned[k], at(i))
                        v.tensor_tensor(halves(U[k][:]), wide(slots[k]), halves(per_row[:]), ALU.mult)\
                         .then_inc(scaled[k], 1)

                    def keep(k):
                        v.wait_ge(used, i * NS + (k + 1) * 2 * NT + PB)
                        h = H[:, bass.ds(2 * i + k, 1), :].rearrange("p a n -> p (a n)")
                        v.tensor_tensor(h[:, 0:CUT], h[:, 0:CUT], slots[3][:, 0, 0:CUT], ALU.add)
                        v.tensor_tensor(h[:, CUT:N], h[:, CUT:N], slots[3][:, 1, 0:N - CUT], ALU.add)\
                         .then_inc(kept[k], 1)

                    for n, (k, m, q) in enumerate(tiles):
                        v.wait_ge(scored, i * NS + n + 1)
                        v.wait_ge(used, i * NS + n // 2 * 2 + 2)
                        slot, b, c0 = slots[n % 3], m * TP // CUT, m * TP // CUT * CUT
                        d0 = m * TP - c0
                        ins = v.scalar_tensor_tensor(prob[:, n % PB, m * TP:(m + 1) * TP], slot[0:TP, b, d0:d0 + TP],
                                                     0.0, causal[:], ALU.max, ALU.mult)
                        end = (CUT, N)[b]
                        if (m + 1) * TP < end:
                            ins = v.tensor_scalar(prob[:, n % PB, (m + 1) * TP:end],
                                                  slot[0:TP, b, d0 + TP:end - c0], 0.0, None, ALU.max)
                        ins.then_inc(diag, 1)
                        if n == 2 * NT + 3:
                            keep(0)
                    keep(1)
                    for k in range(2):
                        v.wait_ge(rooted2[k], at(i))
                        x = X[:, bass.ds(2 * i + k, 1), :].rearrange("p a (h n) -> p (a h) n", h=2)
                        v.scalar_tensor_tensor(x, wide(slots[k]), 1.0, halves(t0[k][:]), ALU.mult, ALU.mult,
                                               accum_out=sums[:, bass.ds(2 * i + k, 1)]).then_inc(last[k], 1)


TOP = 2
FF = 128


class Routes:

    def __init__(self, core, NP):
        self.expert = core.sb("rt_expert", [1, 2 * TOP, NP], I32)
        self.weight = core.sb("rt_weight", [P, 2 * TOP, NP])
        self.b2 = core.sb("rt_b2", [P, NP])


def routing(core, slots, d, sums, R, NP):
    nc = core.nc
    E = d["Wr1"].shape[1]
    B = 2 * NP
    capacity = float(-(-B * N * 5 // (4 * E)))
    with ExitStack() as st:
        c = Core(nc, st)
        Wr = c.sb("rt_wr", [P, E])
        br, ids = c.sb("rt_br", [NP, E]), c.sb("rt_ids", [NP, E])
        b2 = c.sb("rt_b2w", [E, F])
        eye, ones = c.sb("rt_eye", [P, P]), c.sb("rt_ones", [NP, NP])
        z, w = c.sb("rt_z", [NP, 2, E]), c.sb("rt_w", [NP, 2, E])
        m = c.sb("rt_m", [NP, 2])
        load = c.sb("rt_load", [NP, E])
        top, topi, topf = c.sb("rt_top", [NP, 2, 8]), c.sb("rt_topi", [NP, 2, 8], U32), c.sb("rt_topf", [NP, 2, 8])
        e2, tw = c.sb("rt_e2", [NP, 2]), c.sb("rt_tw", [NP, 2, TOP])
        wide_w = c.sb("rt_wide", [NP, 2 * TOP, P])
        dense = c.sb("rt_dense", [NP, 2, TOP, E])
        denseT = c.sb("rt_denseT", [E, 2, NP])
        loaded, step, mm_done, act_done = c.sem("rt_loaded"), c.sem("rt_step"), c.sem("rt_mm"), c.sem("rt_act")
        both = lambda t: t.unsqueeze(1).broadcast_to([NP, 2, E])
        each = lambda t: t.unsqueeze(2).broadcast_to([NP, 2, E])
        LOADED = 16 * 6
        with nc.Block() as block:

            @block.sync
            def _(sp):
                for q in range(2):
                    sp.dma_start(Wr[F * q:F * q + F, :], d["Wr1"]).then_inc(loaded, 16)
                for tile, name in ((br, "br1"), (ids, "experts"), (b2, "b2"), (eye, "eye")):
                    sp.dma_start(tile[:], d[name]).then_inc(loaded, 16)

            @block.vector
            def _(v):
                n = [0]

                def done(ins):
                    n[0] += 1
                    ins.then_inc(step, 1)
                    v.wait_ge(step, n[0])

                def softmax(turn):
                    done(v.tensor_reduce(m[:], z[:], AX.X, ALU.max))
                    done(v.tensor_tensor(z[:], z[:], each(m[:]), ALU.subtract))
                    v.wait_ge(act_done, turn)
                    done(v.tensor_reduce(m[:], w[:], AX.X, ALU.add))
                    done(v.reciprocal(m[:], m[:]))
                    done(v.tensor_tensor(w[:], w[:], each(m[:]), ALU.mult))

                v.memset(ones[:], 1.0)
                v.wait_ge(loaded, LOADED)
                v.wait_ge(mm_done, 1)
                for q in range(2):
                    v.scalar_tensor_tensor(z[:, q, :], slots[q][0:NP, 0, 0:E], 1.0 / N, br[:], ALU.mult, ALU.add)
                done(v.tensor_copy(topf[:].rearrange("p q e -> p (q e)")[:, 0:E], br[:]))
                softmax(1)
                v.wait_ge(mm_done, 2)
                done(v.tensor_copy(load[:], slots[2][0:NP, 0, 0:E]))
                done(v.tensor_tensor(load[:], load[:], slots[2][0:NP, 0, E:2 * E], ALU.add))
                done(v.tensor_scalar(load[:], load[:], float(N), 1e-30, ALU.mult, ALU.max))
                done(v.reciprocal(load[:], load[:]))
                done(v.tensor_scalar(load[:], load[:], capacity, 1.0, ALU.mult, ALU.min))
                done(v.tensor_tensor(z[:], w[:], both(load[:]), ALU.mult))
                softmax(2)
                for q in range(2):
                    done(v.max(top[:, q, :], w[:, q, :]))
                    done(v.max_index(topi[:, q, :], top[:, q, :], w[:, q, :]))
                done(v.tensor_copy(topf[:], topi[:]))
                done(v.tensor_tensor(m[:], top[:, :, 1], top[:, :, 0], ALU.subtract))
                v.wait_ge(act_done, 3)
                done(v.tensor_scalar(m[:], e2[:], 1.0, None, ALU.add))
                done(v.reciprocal(tw[:, :, 0], m[:]))
                done(v.tensor_tensor(tw[:, :, 1], tw[:, :, 0], e2[:], ALU.mult))
                done(v.tensor_copy(wide_w[:], tw[:].rearrange("p q r -> p (q r)").unsqueeze(2)
                                   .broadcast_to([NP, 2 * TOP, P])))
                for q in range(2):
                    for r in range(TOP):
                        done(v.tensor_scalar(dense[:, q, r, :], ids[:], topf[:, q, r:r + 1], tw[:, q, r:r + 1],
                                             ALU.is_equal, ALU.mult))
                done(v.tensor_tensor(dense[:, :, 0, :], dense[:, :, 0, :], dense[:, :, 1, :], ALU.add))
                v.wait_ge(mm_done, 3)
                for q in range(2):
                    v.tensor_copy(denseT[:, q, :], slots[0][0:E, 0, q * NP:(q + 1) * NP])
                v.tensor_copy(R.expert[:].rearrange("a j p -> a (j p)"), slots[1][0:1, 0, 0:2 * TOP * NP])
                done(v.tensor_copy(R.weight[:].rearrange("a j p -> a (j p)"), slots[2][:, 0, 0:2 * TOP * NP]))
                v.wait_ge(mm_done, 4)
                done(v.tensor_copy(R.b2[:], slots[3][:, 0, 0:NP]))

            @block.scalar
            def _(act):
                for turn, after in ((1, 3), (2, 14)):
                    act.wait_ge(step, after)
                    act.activation(w[:], z[:], ACT.Exp).then_inc(act_done, 1)
                act.wait_ge(step, 23)
                act.activation(e2[:], m[:], ACT.Exp).then_inc(act_done, 1)

            @block.tensor
            def _(pe):
                pe.wait_ge(loaded, LOADED)
                for q in range(2):
                    mm = pe.matmul(slots[q][0:NP, 0, 0:E], sums[F * q:F * q + F, :], Wr[F * q:F * q + F, :],
                                   start=True, stop=True)
                mm.then_inc(mm_done, 1)
                pe.wait_ge(step, 6)
                pe.matmul(slots[2][0:NP, 0, 0:2 * E], ones[:], w[:].rearrange("p q e -> p (q e)"),
                          start=True, stop=True).then_inc(mm_done, 1)
                pe.wait_ge(step, 32)
                for q in range(2):
                    pe.matmul(slots[0][0:E, 0, q * NP:(q + 1) * NP], dense[:, q, 0, :], eye[0:NP, 0:NP],
                              start=True, stop=True)
                for q in range(2):
                    for r in range(TOP):
                        j = 2 * q + r
                        pe.matmul(slots[1][0:1, 0, j * NP:(j + 1) * NP], topf[:, q, r:r + 1], eye[0:NP, 0:NP],
                                  start=True, stop=True)
                for j in range(2 * TOP):
                    mm = pe.matmul(slots[2][:, 0, j * NP:(j + 1) * NP], wide_w[:, j, :], eye[0:NP, 0:NP],
                                   start=True, stop=True)
                mm.then_inc(mm_done, 1)
                pe.wait_ge(step, 33)
                for q in range(2):
                    mm = pe.matmul(slots[3][F * q:F * q + F, 0, 0:NP], b2[:], denseT[:, q, :], start=True, stop=True)
                mm.then_inc(mm_done, 1)


def mixture(core, slots, d, H, X, R, out, NP):
    nc = core.nc
    E = d["W1"].shape[1]
    with ExitStack() as st:
        c = Core(nc, st)
        center, mean, eye = c.sb("mx_center", [P, P]), c.sb("mx_mean", [P, P]), c.sb("mx_eye", [P, P])
        eps, gamma, beta = c.sb("mx_eps", [P, 1]), c.sb("mx_gamma", [P, 1]), c.sb("mx_beta", [P, 1])
        T1, b1, T2 = c.sb("mx_w1", [P, E, FF]), c.sb("mx_b1", [FF, E]), c.sb("mx_w2", [FF, E, F])
        pair = lambda name, shape: [c.sb(f"mx_{name}{k}", shape) for k in range(2)]
        C1, cb1, C2 = pair("c1_", [P, 2 * TOP, FF]), pair("cb1_", [FF, 2, TOP]), pair("c2_", [FF, 2, TOP, F])
        xs, t0, r1, z = pair("xs", [P, N]), pair("t", [P, N]), pair("r", [P, N]), pair("z", [P, N])
        G = [[[c.sb(f"mx_g{k}{q}{r}", [FF, N]) for r in range(TOP)] for q in range(2)] for k in range(2)]
        OT = pair("out", [TP, 2, NT, F])
        weights, ready = c.sem("mx_weights"), c.sem("mx_ready")
        sems = lambda name: [c.sem(f"mx_{name}{k}") for k in range(2)]
        x_in, gathered, lifted, gelued, lowered, summed = map(
            sems, ("x_in", "gathered", "lifted", "gelued", "lowered", "summed"))
        centered, squared, varied, logged, rooted = map(
            sems, ("centered", "squared", "varied", "logged", "rooted"))
        normed, scaled, shifted, turned, copied, stored = map(
            sems, ("normed", "scaled", "shifted", "turned", "copied", "stored"))
        loops = NP // 2
        WEIGHTS = 16 * (3 * 2 + 5)
        out_v = out.rearrange("b (p t) f -> p b (t f)", t=NT)

        with nc.Block() as block:

            @block.sync
            def _(sp):
                for k in range(2):
                    lead(sp, [x_in[k], stored[k]], 16)
                for q in range(2):
                    r = slice(F * q, F * q + F)
                    sp.dma_start(T1[r], d["W1"]).then_inc(weights, 16)
                    sp.dma_start(gamma[r, :], d["gamma1"].unsqueeze(1)).then_inc(weights, 16)
                    sp.dma_start(beta[r, :], d["beta1"].unsqueeze(1)).then_inc(weights, 16)
                for tile, name in ((center, "center"), (mean, "mean"), (eye, "eye"), (b1, "b1"), (T2, "W2")):
                    sp.dma_start(tile[:], d[name]).then_inc(weights, 16)
                with sp.Fori(0, loops) as i:
                    for k in range(2):
                        sp.wait_ge(summed[k], at(i - 1))
                        sp.dma_start(xs[k][:], X[:, bass.ds(2 * i + k, 1), :].rearrange("p a n -> p (a n)"))\
                          .then_inc(x_in[k], 16)
                    for k in range(2):
                        sp.wait_ge(copied[k], at(i))
                        sp.dma_start(out_v[:, bass.ds(4 * i + 2 * k, 2), :],
                                     OT[k][:].rearrange("p q t f -> p q (t f)")).then_inc(stored[k], 16)
                for k in range(2):
                    sp.wait_ge(stored[k], at(loops - 1, 16))

            @block.gpsimd
            def _(pool):
                for k in range(2):
                    lead(pool, [gathered[k]])
                pool.wait_ge(weights, WEIGHTS)
                with pool.Fori(0, loops) as i:
                    for k in range(2):
                        pool.wait_ge(lowered[k], at(i - 1))
                        for q in range(2):
                            for r in range(TOP):
                                j = 2 * q + r
                                e = pool.value_load(R.expert[0:1, j, bass.ds(2 * i + k, 1)], min_val=0, max_val=E - 1)
                                pool.tensor_copy(C1[k][:, j, :], T1[:, bass.ds(e, 1), :].rearrange("p a f -> p (a f)"))
                                pool.tensor_copy(cb1[k][:, q, r:r + 1], b1[:, bass.ds(e, 1)])
                                ins = pool.tensor_tensor(C2[k][:, q, r, :],
                                                         T2[:, bass.ds(e, 1), :].rearrange("p a f -> p (a f)"),
                                                         R.weight[:, j, bass.ds(2 * i + k, 1)].broadcast_to([FF, F]),
                                                         ALU.mult)
                        ins.then_inc(gathered[k], 1)

            @block.tensor
            def _(pe):
                for k in range(2):
                    lead(pe, [lifted[k]], 4)
                    lead(pe, [lowered[k], centered[k], varied[k], turned[k]])
                pe.wait_ge(weights, WEIGHTS)
                with pe.Fori(0, loops) as i:
                    for k in range(2):
                        pe.wait_ge(gathered[k], at(i))
                        pe.wait_ge(x_in[k], i * 16 + (16 + 16 * LEAD))
                        pe.wait_ge(copied[k], at(i - 1))
                    for q in range(2):
                        for k in range(2):
                            for r in range(TOP):
                                j = 2 * q + r
                                if q == 1:
                                    pe.wait_ge(gelued[k], 4 * i + (j - 1) + 4 * LEAD)
                                for hf in range(2):
                                    mm = pe.matmul(slots[2 * k + r][:, hf, 0:HALF], C1[k][F * q:F * q + F, j, :],
                                                   xs[k][F * q:F * q + F, hf * HALF:(hf + 1) * HALF],
                                                   start=True, stop=True)
                                mm.then_inc(lifted[k], 1)
                    for k in range(2):
                        pe.wait_ge(gelued[k], 4 * i + 4 + 4 * LEAD)
                        for hf in range(2):
                            for r in range(TOP):
                                for q in range(2):
                                    mm = pe.matmul(slots[2 * k][F * q:F * q + F, hf, 0:HALF], C2[k][:, q, r, :],
                                                   G[k][q][r][:, hf * HALF:(hf + 1) * HALF],
                                                   start=(r == 0), stop=(r == TOP - 1))
                        mm.then_inc(lowered[k], 1)
                    for k in range(2):
                        pe.wait_ge(summed[k], at(i))
                        for hf in range(2):
                            mm = pe.matmul(slots[2 * k + 1][:, hf, 0:HALF], center[:], z[k][:, hf * HALF:(hf + 1) * HALF],
                                           start=True, stop=True)
                        mm.then_inc(centered[k], 1)
                    for k in range(2):
                        pe.wait_ge(squared[k], at(i))
                        for hf in range(2):
                            mm = pe.matmul(slots[2 * k][:, hf, 0:HALF], mean[:], t0[k][:, hf * HALF:(hf + 1) * HALF],
                                           start=True, stop=True)
                        mm.then_inc(varied[k], 1)
                    for k in range(2):
                        pe.wait_ge(shifted[k], at(i))
                        for t in range(NT):
                            mm = pe.transpose(flat(slots[2 * k])[0:TP, t * P:(t + 1) * P],
                                              z[k][:, t:t + NT * (TP - 1) + 1:NT], eye[:])
                        mm.then_inc(turned[k], 1)

            @block.scalar
            def _(act):
                for k in range(2):
                    lead(act, [gelued[k]], 4)
                    lead(act, [squared[k], logged[k], rooted[k], copied[k]])
                act.wait_ge(ready, 1)
                with act.Fori(0, loops) as i:
                    for q in range(2):
                        for k in range(2):
                            for r in range(TOP):
                                j = 2 * q + r
                                act.wait_ge(lifted[k], 4 * i + (j + 1) + 4 * LEAD)
                                act.activation(halves(G[k][q][r][:]), wide(slots[2 * k + r]), ACT.Gelu,
                                               bias=cb1[k][:, q, r:r + 1]).then_inc(gelued[k], 1)
                    for k in range(2):
                        act.wait_ge(centered[k], at(i))
                        act.activation(halves(t0[k][:]), wide(slots[2 * k + 1]), ACT.Square).then_inc(squared[k], 1)
                    for k in range(2):
                        act.wait_ge(varied[k], at(i))
                        act.activation(halves(r1[k][:]), wide(slots[2 * k]), ACT.Ln, bias=eps[:, 0:1])\
                           .then_inc(logged[k], 1)
                    for k in range(2):
                        act.wait_ge(logged[k], at(i))
                        act.activation(t0[k][:], r1[k][:], ACT.Exp, scale=-0.5).then_inc(rooted[k], 1)
                    for k in range(2):
                        act.wait_ge(turned[k], at(i))
                        act.wait_ge(stored[k], i * 16 + 16 * LEAD)
                        act.activation(OT[k][:].rearrange("p q t f -> p t q f"),
                                       flat(slots[2 * k])[0:TP, 0:NT * P].rearrange("p (t q f) -> p t q f", t=NT, q=2),
                                       ACT.Copy).then_inc(copied[k], 1)

            @block.vector
            def _(v):
                for k in range(2):
                    lead(v, [summed[k], normed[k], scaled[k], shifted[k]])
                v.memset(eps[:], EPS).then_inc(ready, 1)
                v.wait_ge(weights, WEIGHTS)
                with v.Fori(0, loops) as i:
                    for k in range(2):
                        v.wait_ge(lowered[k], at(i))
                        v.scalar_tensor_tensor(halves(z[k][:]), wide(slots[2 * k]), R.b2[:, bass.ds(2 * i + k, 1)],
                                               halves(xs[k][:]), ALU.add, ALU.add).then_inc(summed[k], 1)
                    for k in range(2):
                        v.wait_ge(rooted[k], at(i))
                        v.tensor_tensor(halves(r1[k][:]), wide(slots[2 * k + 1]), halves(t0[k][:]), ALU.mult)\
                         .then_inc(normed[k], 1)
                    for k in range(2):
                        v.wait_ge(normed[k], at(i))
                        v.scalar_tensor_tensor(r1[k][:], r1[k][:], gamma[:, 0:1],
                                               H[:, bass.ds(2 * i + k, 1), :].rearrange("p a n -> p (a n)"),
                                               ALU.mult, ALU.add).then_inc(scaled[k], 1)
                    for k in range(2):
                        v.wait_ge(scaled[k], at(i))
                        v.tensor_scalar(z[k][:], r1[k][:], beta[:, 0:1], None, ALU.add).then_inc(shifted[k], 1)


def tower(nc, d, out):
    B = d["x"].shape[0]
    NP = B // 2
    with ExitStack() as st:
        core = Core(nc, st)
        slots = [core.ps(f"slot{i}", [P, 2, 512]) for i in range(4)]
        H = core.sb("H", [P, NP, N])
        tokens(core, slots, d, H, NP)
        attention(core, slots, d, H, NP)
        routed_ffn(core, slots, d, H, NP)
        X = core.sb("X", [P, NP, N])
        sums = core.sb("X_sums", [P, NP])
        causal_attention(core, slots, d, H, X, sums, NP)
        R = Routes(core, NP)
        routing(core, slots, d, sums, R, NP)
        mixture(core, slots, d, H, X, R, out, NP)


def shape_constants(pairs, experts):
    pos = np.arange(N, dtype=np.float32)[:, None]
    step = np.arange(0, F, 2, dtype=np.float32) * np.float32(-np.log(10000.0) / F)
    angle = (pos * np.exp(step.astype(np.float64)).astype(np.float32)).astype(np.float64)
    pe = np.zeros((N, F), np.float32)
    pe[:, 0::2] = np.sin(angle)
    pe[:, 1::2] = np.cos(angle)
    img = np.arange(P) // F
    same = (img[:, None] == img[None, :]).astype(np.float32)
    eye = np.eye(P, dtype=np.float32)
    patch = np.arange(N, dtype=np.float32)
    return {
        "pos": np.concatenate([pe.T, pe.T]).copy(),
        "iota": np.tile(patch, (TP, 1)),
        "center": eye - same / F,
        "mean": same / F,
        "eye": eye,
        "causal": np.triu(np.ones((TP, TP), np.float32)),
        "experts": np.tile(np.arange(experts, dtype=np.float32), (pairs, 1)),
        "per_row": np.tile(1.0 / np.maximum(patch, 1.0), (P, 1)).astype(np.float32),
    }


def laid_out(inputs):
    a = {k: np.asarray(v) for k, v in inputs.items()}
    B = a["x"].shape[0]
    edges = a["L0_tok_edge_index"].astype(np.int32)
    E = edges.shape[1]
    KE = -(-E // TP)
    rows = np.full((2, KE * TP), -1, np.int32)
    rows[:, :E] = edges
    own = np.tile(np.arange(N, dtype=np.int32), (2, 1))
    t = lambda x, *axes: np.ascontiguousarray(np.transpose(x, axes or None))
    d = {
        "x": a["x"],
        "edges": t(np.concatenate([rows, own], 1).reshape(2, KE + NT, TP), 2, 0, 1),
        "W_embed": a["L0_tok_W_embed"], "b_embed": a["L0_tok_b_embed"],
        "W_gcn": a["L0_tok_W_gcn"], "b_gcn": t(a["L0_tok_b_gcn"]),
        "W_out": a["L0_tok_W_out"], "b_out": a["L0_tok_b_out"],
        "gamma0": a["L0_attn_ln_gamma"], "beta0": a["L0_attn_ln_beta"],
        "W_qkv_t": t(a["L0_attn_W_qkv"]), "W_gate_t": t(a["L0_attn_W_gate"]),
        "b_gate": a["L0_attn_b_gate"], "W_final_t": t(a["L0_attn_W_final"]), "b_final": a["L0_attn_b_final"],
        "route": a["L0_ffn_route_id"].astype(np.int32).reshape(1, -1),
        "Wi_t": t(a["L0_ffn_Wi"]), "bi": a["L0_ffn_bi"],
        "Wr_t": t(a["L0_ffn_Wr"], 3, 1, 0, 2), "br_t": t(a["L0_ffn_br"], 2, 1, 0),
        "Ws": t(a["L0_ffn_Ws"][:, 0], 2, 0, 1), "bs": t(a["L0_ffn_bs"][:, 0]),
        "Wo_t": t(a["L0_ffn_Wo"]), "bo": a["L0_ffn_bo"],
        "Wq": a["L1_attn_Wq"], "Wk": a["L1_attn_Wk"], "Wv": a["L1_attn_Wv"], "Wo1_t": t(a["L1_attn_Wo"]),
        "Wr1": a["L1_ffn_Wr"], "br1": np.tile(a["L1_ffn_br"], (B // 2, 1)),
        "W1": t(a["L1_ffn_W1"], 1, 0, 2), "b1": t(a["L1_ffn_b1"]),
        "W2": t(a["L1_ffn_W2"], 1, 0, 2), "b2": a["L1_ffn_b2"],
        "gamma1": a["L1_ffn_gamma"], "beta1": a["L1_ffn_beta"],
    }
    return {**d, **shape_constants(B // 2, a["L1_ffn_br"].size)}


def kernel(**inputs):
    import concourse.bacc as _bacc
    from concourse import mybir as _mybir
    from concourse.bass_utils import run_bass_kernel_spmd as _run

    nc = _bacc.Bacc("TRN2", target_bir_lowering=False, num_devices=1)
    data = laid_out(inputs)
    B = data["x"].shape[0]
    d = {n: nc.dram_tensor(f"in_{n}", a.shape, _mybir.dt.from_np(a.dtype), kind="ExternalInput").ap()
         for n, a in data.items()}
    out = nc.dram_tensor("tokens_out", (B, N, F), F32, kind="ExternalOutput").ap()
    tower(nc, d, out)
    r = _run(nc, [{f"in_{n}": a for n, a in data.items()}], core_ids=[0])
    return r.results[0]["tokens_out"]
```

```python
from contextlib import ExitStack

import numpy as np

import concourse.bass as bass
from concourse import mybir

ALU = mybir.AluOpType
ACT = mybir.ActivationFunctionType
AX = mybir.AxisListType
F32 = mybir.dt.float32
F16 = mybir.dt.float16
BF16 = mybir.dt.bfloat16
I32 = mybir.dt.int32
U32 = mybir.dt.uint32

P = 128
GRID, PATCH, CH, IMG = 28, 8, 3, 224
N = GRID * GRID
HALF = N // 2
TP = 112
NT = N // TP
F = 64
EPS = 1e-5
LEAD = 2


def at(n, step=1):
    return (n + 1 + LEAD) * step


class Core:

    def __init__(self, nc, stack):
        self.nc, self.stack, self.sems = nc, stack, []
        stack.callback(self.free_semaphores)

    def free_semaphores(self):
        if self.sems:
            self.nc.clear_and_free_semaphores(self.sems)
            self.nc.all_engine_barrier()

    def sb(self, name, shape, dt=F32):
        return self.stack.enter_context(self.nc.sbuf_tensor(name, shape, dt))

    def ps(self, name, shape):
        return self.stack.enter_context(self.nc.psum_tensor(name, shape, F32))

    def sem(self, name):
        self.sems.append(self.nc.alloc_semaphore(name))
        return self.sems[-1]


def wide(slot):
    return slot[:, :, 0:HALF]


def halves(tile):
    return tile.rearrange("p (h n) -> p h n", h=2)


def flat(slot):
    return slot.rearrange("p h n -> p (h n)")


def lead(eng, sems, step=1):
    for s in sems:
        eng.sem_inc(s, LEAD * step)


def build_graph(core, slots, d, A):
    nc = core.nc
    KE = d["edges"].shape[2]
    with ExitStack() as st:
        c = Core(nc, st)
        ei = c.sb("ge_idx", [TP, 2, KE], I32)
        ef = c.sb("ge_idx_f", [TP, 2, KE])
        iota = c.sb("ge_iota", [TP, N])
        onesrc = c.sb("ge_onehot_src", [TP, KE, N], BF16)
        onedst = c.sb("ge_onehot_dst", [TP, KE, N], BF16)
        ones = c.sb("ge_ones", [TP, TP])
        rd = c.sb("ge_rdeg", [TP, N])
        rs = c.sb("ge_rdeg_src", [TP, 8])
        sd = c.sb("ge_sqrt", [TP, N])
        ss = c.sb("ge_sqrt_src", [TP, 8])
        loaded, ready, hot = c.sem("ge_loaded"), c.sem("ge_ready"), c.sem("ge_hot")
        counted, kept, degs = c.sem("ge_counted"), c.sem("ge_kept"), c.sem("ge_degs")
        rooted, inverted, scaled = c.sem("ge_rooted"), c.sem("ge_inverted"), c.sem("ge_scaled")
        with nc.Block() as block:

            @block.sync
            def _(sp):
                sp.dma_start(ei[:], d["edges"]).then_inc(loaded, 16)
                sp.dma_start(iota[:], d["iota"]).then_inc(loaded, 16)

            @block.vector
            def _(v):
                v.memset(ones[:], 1.0).then_inc(ready, 1)
                v.wait_ge(loaded, 32)
                v.tensor_copy(ef[:], ei[:]).then_inc(ready, 1)
                v.wait_ge(ready, 2)
                for k in range(KE):
                    v.tensor_scalar(onesrc[:, k, :], iota[:], ef[:, 0, k:k + 1], None, ALU.is_equal)
                    v.tensor_scalar(onedst[:, k, :], iota[:], ef[:, 1, k:k + 1], None,
                                    ALU.is_equal).then_inc(hot, 1)
                for t in range(NT):
                    v.wait_ge(counted, t + 1)
                    v.tensor_copy(halves(A[:, t, :]), wide(slots[t % 2])[0:TP]).then_inc(kept, 1)
                v.wait_ge(rooted, 2)
                v.reciprocal(rd[:], sd[:]).then_inc(inverted, 1)
                v.reciprocal(rs[:, 0:NT], ss[:, 0:NT]).then_inc(inverted, 1)
                v.wait_ge(inverted, 2)
                for t in range(NT):
                    v.scalar_tensor_tensor(A[:, t, :], A[:, t, :], rs[:, t:t + 1], rd[:],
                                           ALU.mult, ALU.mult).then_inc(scaled, 1)

            @block.tensor
            def _(pe):
                for t in range(NT):
                    if t >= 2:
                        pe.wait_ge(kept, t - 1)
                    for k in range(KE):
                        if t == 0:
                            pe.wait_ge(hot, k + 1)
                        for h in range(2):
                            mm = pe.matmul(slots[t % 2][0:TP, h, 0:HALF], onesrc[:, k, t * TP:(t + 1) * TP],
                                           onedst[:, k, h * HALF:(h + 1) * HALF],
                                           start=(k == 0), stop=(k == KE - 1))
                    mm.then_inc(counted, 1)
                pe.wait_ge(kept, NT)
                for h in range(2):
                    for t in range(NT):
                        pe.matmul(slots[2][0:TP, h, 0:HALF], ones[:], A[:, t, h * HALF:(h + 1) * HALF],
                                  start=(t == 0), stop=(t == NT - 1))
                for t in range(NT):
                    for k in range(NT):
                        mm = pe.matmul(slots[3][0:TP, 0, t:t + 1], A[:, k, t * TP:(t + 1) * TP], ones[:, 0:1],
                                       start=(k == 0), stop=(k == NT - 1))
                mm.then_inc(degs, 1)

            @block.scalar
            def _(act):
                act.wait_ge(degs, 1)
                act.activation(halves(sd[:]), wide(slots[2])[0:TP], ACT.Sqrt).then_inc(rooted, 1)
                act.activation(ss[:, 0:NT], slots[3][0:TP, 0, 0:NT], ACT.Sqrt).then_inc(rooted, 1)
                act.wait_ge(scaled, NT)


def tokens(core, slots, d, H, scratch, NP):
    nc = core.nc
    KR = 2 * CH * PATCH
    with ExitStack() as st:
        c = Core(nc, st)
        A = c.sb("tk_graph", [TP, NT, N])
        build_graph(core, slots, d, A)
        X = [c.sb(f"tk_x{i}", [TP, GRID, IMG]) for i in range(2)]
        We = c.sb("tk_we", [TP, PATCH // 2, P])
        Wg = c.sb("tk_wg", [P, 3, P])
        Wo = c.sb("tk_wo", [P, P])
        be, bg, bo = c.sb("tk_be", [P, 1]), c.sb("tk_bg", [P, 3]), c.sb("tk_bo", [P, 1])
        pos = c.sb("tk_pos", [P, N])
        center, mean, eps = c.sb("tk_center", [P, P]), c.sb("tk_mean", [P, P]), c.sb("tk_eps", [P, 1])
        gamma, beta = c.sb("tk_gamma", [P, 1]), c.sb("tk_beta", [P, 1])
        t0, r1 = ([c.sb(f"tk_{name}{i}", [P, N]) for i in range(2)] for name in ("t", "r"))
        both = [c.sb(f"tk_norms{i}", [P, 2, N]) for i in range(2)]
        xn, x1 = ([both[i][:, j, :] for i in range(2)] for j in range(2))
        h = [c.sb(f"tk_h{i}", [P, N]) for i in range(2)]
        hw = [c.sb(f"tk_hw{i}", [TP, NT, P]) for i in range(2)]
        cleared, weights = c.sem("tk_cleared"), c.sem("tk_weights")
        x_in = [c.sem(f"tk_x_in{i}") for i in range(2)]
        embedded = [c.sem(f"tk_embedded{i}") for i in range(2)]
        h_ready = [[c.sem(f"tk_h_ready{i}_{l}") for l in range(5)] for i in range(2)]
        projected = [[c.sem(f"tk_projected{i}_{l}") for l in range(3)] for i in range(2)]
        hw_ready = [[c.sem(f"tk_hw_ready{i}_{l}") for l in range(3)] for i in range(2)]
        spread = [[c.sem(f"tk_spread{i}_{l}") for l in range(3)] for i in range(2)]
        out_ready = [c.sem(f"tk_out_ready{i}") for i in range(2)]
        sems = lambda name: [c.sem(f"tk_{name}{i}") for i in range(2)]
        centered, squared, varied, logged, inverse, rooted = map(
            sems, ("centered", "squared", "varied", "logged", "inverse", "rooted"))
        normed, unit_var, logged2, rooted2, normed2, scaled = map(
            sems, ("normed", "unit_var", "logged2_", "rooted2_", "normed2_", "scaled"))
        kept, stored = sems("kept"), sems("stored")
        loops = NP // 2
        with nc.Block() as block:

            @block.gpsimd
            def _(pool):
                for w in (We, Wg, Wo, X[0], X[1]):
                    pool.memset(w[:], 0.0).then_inc(cleared, 1)

            @block.sync
            def _(sp):
                lead(sp, x_in, 32)
                sp.wait_ge(cleared, 5)
                wv = d["W_embed"].rearrange("(r s x) f -> r s x f", s=2, x=PATCH // 2)
                for q in range(2):
                    for s in range(2):
                        sp.dma_start(We[64 * s + 24 * q:64 * s + 24 * q + 24, :, F * q:F * q + F],
                                     wv[:, s]).then_inc(weights, 16)
                    o = F * q
                    sp.dma_start(Wg[o:o + F, :, o:o + F], d["W_gcn"].rearrange("l i o -> i l o")).then_inc(weights, 16)
                    sp.dma_start(Wo[o:o + F, o:o + F], d["W_out"]).then_inc(weights, 16)
                    sp.dma_start(be[o:o + F, :], d["b_embed"].unsqueeze(1)).then_inc(weights, 16)
                    sp.dma_start(bg[o:o + F, :], d["b_gcn"]).then_inc(weights, 16)
                    for tile, name in ((bo, "b_out"), (gamma, "gamma0"), (beta, "beta0")):
                        sp.dma_start(tile[o:o + F, :], d[name].unsqueeze(1)).then_inc(weights, 16)
                for tile, name in ((pos, "pos"), (center, "center"), (mean, "mean")):
                    sp.dma_start(tile[:], d[name]).then_inc(weights, 16)
                xv = d["x"].rearrange("b c (i y) w -> (b c) y i w", y=PATCH)

                def load(q, pair):
                    for s in range(2):
                        w = IMG - 4 * s
                        for r in range(2 * CH):
                            p0 = 64 * s + PATCH * r
                            sp.dma_start(X[q][p0:p0 + PATCH, :, 0:w],
                                         xv[bass.ds(pair * 2 * CH + r, 1), :, :, 4 * s:IMG]
                                         .rearrange("a y i w -> (a y) i w")).then_inc(x_in[q], 16)

                def store(q, pair):
                    sp.dma_start(scratch[:, pair].rearrange("p a j n -> p (a j) n"), both[q][:]).then_inc(stored[q], 16)

                for q in range(2):
                    lead(sp, [stored[q]], 16)
                    load(q, q)
                with sp.Fori(0, loops - 1) as i:
                    for q in range(2):
                        sp.wait_ge(embedded[q], at(i))
                        load(q, 2 * i + (q + 2))
                    for q in range(2):
                        sp.wait_ge(scaled[q], at(i))
                        store(q, bass.ds(2 * i + q, 1))
                for q in range(2):
                    sp.wait_ge(scaled[q], at(loops - 1))
                    store(q, slice(NP - 2 + q, NP - 1 + q))
                store(1, slice(NP, NP + 1))
                sp.wait_ge(stored[0], at(loops - 1, 16))
                sp.wait_ge(stored[1], at(loops, 16))

            XIN = 4 * CH * 16
            WEIGHTS = 16 * (2 * 9 + 3 + 1)

            @block.tensor
            def _(pe):
                for q in range(2):
                    lead(pe, [embedded[q], out_ready[q], centered[q], varied[q]] + projected[q] + spread[q])
                pe.wait_ge(weights, WEIGHTS)
                with pe.Fori(0, loops) as i:
                    for q in range(2):
                        pe.wait_ge(x_in[q], i * XIN + (XIN + 32 * LEAD))
                        pe.wait_ge(normed[q], at(i - 1))
                        for hf in range(2):
                            for x in range(PATCH // 2):
                                px = X[q][:, 14 * hf:14 * hf + 14, x:x + 8 * (GRID - 1) + 1:8]
                                mm = pe.matmul(slots[2 * q][:, hf, 0:HALF], We[:, x, :], px,
                                               start=(x == 0), stop=(x == 3))
                        mm.then_inc(embedded[q], 1)
                    for l in range(3):
                        for q in range(2):
                            pe.wait_ge(h_ready[q][l], at(i))
                            if l == 0:
                                pe.wait_ge(unit_var[q], at(i - 1))
                            for t in range(NT):
                                mm = pe.matmul(flat(slots[2 * q + 1])[0:TP, t * P:(t + 1) * P],
                                               h[q][:, t * TP:(t + 1) * TP], Wg[:, l, :], start=True, stop=True)
                            mm.then_inc(projected[q][l], 1)
                        for q in range(2):
                            pe.wait_ge(hw_ready[q][l], at(i))
                            for hf in range(2):
                                for t in range(NT):
                                    mm = pe.matmul(slots[2 * q][:, hf, 0:HALF], hw[q][:, t, :],
                                                   A[:, t, hf * HALF:(hf + 1) * HALF],
                                                   start=(t == 0), stop=(t == NT - 1))
                            mm.then_inc(spread[q][l], 1)
                    for q in range(2):
                        pe.wait_ge(h_ready[q][3], at(i))
                        for hf in range(2):
                            mm = pe.matmul(slots[2 * q + 1][:, hf, 0:HALF], Wo[:], h[q][:, hf * HALF:(hf + 1) * HALF],
                                           start=True, stop=True)
                        mm.then_inc(out_ready[q], 1)
                    for q in range(2):
                        pe.wait_ge(h_ready[q][4], at(i))
                        for hf in range(2):
                            mm = pe.matmul(slots[2 * q][:, hf, 0:HALF], center[:], h[q][:, hf * HALF:(hf + 1) * HALF],
                                           start=True, stop=True)
                        mm.then_inc(centered[q], 1)
                    for q in range(2):
                        pe.wait_ge(squared[q], at(i))
                        for hf in range(2):
                            mm = pe.matmul(slots[2 * q + 1][:, hf, 0:HALF], mean[:], t0[q][:, hf * HALF:(hf + 1) * HALF],
                                           start=True, stop=True)
                        mm.then_inc(varied[q], 1)

            @block.scalar
            def _(act):
                for q in range(2):
                    lead(act, hw_ready[q] + [squared[q], logged[q], inverse[q], rooted[q], logged2[q], rooted2[q]])
                with act.Fori(0, loops) as i:
                    for l in range(3):
                        for q in range(2):
                            act.wait_ge(projected[q][l], at(i))
                            act.activation(hw[q][:].rearrange("p t f -> p (t f)"),
                                           flat(slots[2 * q + 1])[0:TP, 0:NT * P], ACT.Copy)\
                               .then_inc(hw_ready[q][l], 1)
                    for q in range(2):
                        act.wait_ge(centered[q], at(i))
                        act.activation(halves(t0[q][:]), wide(slots[2 * q]), ACT.Square).then_inc(squared[q], 1)
                    for q in range(2):
                        act.wait_ge(varied[q], at(i))
                        act.wait_ge(stored[q], at(i - 1, 16))
                        act.activation(halves(xn[q]), wide(slots[2 * q + 1]), ACT.Ln, bias=eps[:, 0:1])\
                           .then_inc(logged[q], 1)
                    for q in range(2):
                        act.wait_ge(logged[q], at(i))
                        act.activation(r1[q][:], xn[q], ACT.Exp, scale=-0.5).then_inc(rooted[q], 1)
                        act.activation(t0[q][:], xn[q], ACT.Exp, scale=-1.0).then_inc(inverse[q], 1)
                    for q in range(2):
                        act.wait_ge(unit_var[q], at(i))
                        act.activation(r1[q][:], t0[q][:], ACT.Ln, bias=eps[:, 0:1]).then_inc(logged2[q], 1)
                    for q in range(2):
                        act.wait_ge(logged2[q], at(i))
                        act.activation(t0[q][:], r1[q][:], ACT.Exp, scale=-0.5).then_inc(rooted2[q], 1)

            @block.vector
            def _(v):
                for q in range(2):
                    lead(v, h_ready[q] + [normed[q], unit_var[q], normed2[q], scaled[q], kept[q]])
                v.memset(eps[:], EPS).then_inc(weights, 16)
                v.wait_ge(weights, WEIGHTS)
                with v.Fori(0, loops) as i:
                    for q in range(2):
                        v.wait_ge(embedded[q], at(i))
                        v.wait_ge(kept[q], at(i - 1))
                        v.scalar_tensor_tensor(halves(h[q][:]), wide(slots[2 * q]), be[:, 0:1], halves(pos[:]),
                                               ALU.add, ALU.add).then_inc(h_ready[q][0], 1)
                    for l in range(3):
                        for q in range(2):
                            v.wait_ge(spread[q][l], at(i))
                            v.tensor_scalar(halves(h[q][:]), wide(slots[2 * q]), bg[:, l:l + 1], 0.0,
                                            ALU.add, ALU.max).then_inc(h_ready[q][l + 1], 1)
                    for q in range(2):
                        v.wait_ge(out_ready[q], at(i))
                        v.tensor_scalar(halves(h[q][:]), wide(slots[2 * q + 1]), bo[:, 0:1], None, ALU.add)\
                         .then_inc(h_ready[q][4], 1)
                    for q in range(2):
                        v.wait_ge(rooted[q], at(i))
                        v.tensor_tensor(halves(x1[q]), wide(slots[2 * q]), halves(r1[q][:]), ALU.mult)\
                         .then_inc(normed[q], 1)
                        v.wait_ge(inverse[q], at(i))
                        v.tensor_tensor(halves(t0[q][:]), wide(slots[2 * q + 1]), halves(t0[q][:]), ALU.mult)\
                         .then_inc(unit_var[q], 1)
                    for q in range(2):
                        v.wait_ge(normed[q], at(i))
                        v.tensor_tensor(H[:, bass.ds(2 * i + q + 1, 1), :].rearrange("p a n -> p (a n)"),
                                        h[q][:], x1[q], ALU.add).then_inc(kept[q], 1)
                    for q in range(2):
                        v.wait_ge(rooted2[q], at(i))
                        v.tensor_tensor(xn[q], x1[q], t0[q][:], ALU.mult).then_inc(normed2[q], 1)
                    for q in range(2):
                        v.wait_ge(normed2[q], at(i))
                        v.tensor_scalar(xn[q], xn[q], gamma[:, 0:1], beta[:, 0:1], ALU.mult, ALU.add)\
                         .then_inc(scaled[q], 1)


HEADS, HD = 8, 32
GROUPS, HG = 2, 4
RING = 3
ERING, VRING = 4, 2
LAG = 2
V_TILES = (range(0, 3), range(3, 5), range(5, 7))
UNITS = [(q, g) for q in range(2) for g in range(GROUPS)]

LAST_READER = {"q": "dve", "k": "dve", "g": "act", "v": "act", "S": "act", "final": "dve"}


def prepare(q, g, pair):
    steps = [(0, ("q", q, g, pair)), (1, ("k", q, g, pair)), (3, ("g", q, g, pair))]
    if g == 0:
        steps += [(4, ("v", q, 0, pair)), (5, ("v", q, 1, pair)), (6, ("v", q, 2, pair))]
    return steps


def attention_order():
    order = []
    for u, (q, g) in enumerate(UNITS):
        nxt, npair = UNITS[(u + 1) % 4], int(u == 3)
        pq, pg, ppair = (*UNITS[u - 1], 0) if u else (*UNITS[3], -1)
        extra = prepare(*nxt, npair)
        for t in range(NT):
            late = (q, g, t - LAG, 0) if t >= LAG else (pq, pg, t - LAG + NT, ppair)
            order += [("S", q, g, t, 0), ("S", q, g, t, 1), ("pv", *late, 0)]
            if t > 0:
                order.append(("inv", q, g, t - 1))
            order += [("S", q, g, t, 2)]
            order += [s for when, s in extra if when == t]
            order += [("S", q, g, t, 3), ("pv", *late, 1)]
            if t == LAG - 1:
                order.append(("gated", pq, pg, ppair))
            if t == LAG and pg == GROUPS - 1:
                order.append(("final", pq, ppair))
        order.append(("inv", q, g, NT - 1))
        if u == 2:
            order.insert(len(order) - 10, ("load",))
    return order


class Counts:

    def __init__(self, first, body, start=0, unit=1):
        self.first, self.body, self.start, self.unit = first, body, start, unit

    def ahead(self, step):
        return self.start + (self.first.index(step) + 1) * self.unit

    def turn(self, i, step):
        n = self.start + (len(self.first) + self.body.index(step) + 1) * self.unit
        return i * (len(self.body) * self.unit) + n

    def turn_before(self, i, step):
        n = self.start + (len(self.first) + self.body.index(step) + 1 - len(self.body)) * self.unit
        return i * (len(self.body) * self.unit) + n


def attention(core, slots, d, H, scratch, NP):
    nc = core.nc
    order = attention_order()
    first = [s for _, s in prepare(0, 0, 1)]
    final = [("final", 1, -1)]
    is_job = lambda s: s[0] in LAST_READER
    jobs = [s for s in order if is_job(s)]
    by = {e: [s for s in jobs if LAST_READER[s[0]] == e] for e in ("act", "dve")}
    by_first = {e: [s for s in first if LAST_READER[s[0]] == e] for e in ("act", "dve")}
    assert len(jobs) % RING == 0
    n_filled = Counts(first, jobs)
    n_read = {e: Counts(by_first[e], by[e], start=RING) for e in by}
    qk = lambda steps: [s for s in steps if s[0] in ("q", "k")]
    n_high = Counts(qk(first), qk(order))
    gs = [s for s in order if s[0] == "gated"]
    n_gated = Counts([], gs, start=1)
    tiles = [s for s in order if s[0] == "S"]
    n_biased = Counts([], tiles)
    NM = len(tiles) // HG
    C = float(HD) ** -0.5
    ACC = slots[3]

    def slot_of(s, ahead=False):
        return slots[(first.index(s) if ahead else len(first) + jobs.index(s)) % RING]

    def group(q, g, t):
        return UNITS.index((q, g)) * NT + t

    with ExitStack() as st:
        c = Core(nc, st)
        W = c.sb("at_w", [P, 4 * HEADS * HD])
        Wf = c.sb("at_wf", [P, GROUPS, F])
        bg, bf = c.sb("at_bg", [P, GROUPS]), c.sb("at_bf", [P, 1])
        norms = c.sb("at_norms", [P, 2, N])
        xn, x1 = norms[:, 0, :], norms[:, 1, :]
        split = [[c.sb(f"at_split{w}{g}", [P, 2, N], F16) for g in range(GROUPS)] for w in range(2)]
        stack = [[c.sb(f"at_stack{w}{g}", [P, HG, N], F16) for g in range(GROUPS)] for w in range(2)]
        V = [c.sb(f"at_v{q}", [TP, NT, HEADS * HD]) for q in range(2)]
        gate = [c.sb(f"at_gate{g}", [P, N]) for g in range(GROUPS)]
        og = [c.sb(f"at_og{g}", [P, N]) for g in range(GROUPS)]
        E = c.sb("at_e", [TP, ERING, HG, N])
        vs = c.sb("at_vs", [TP, VRING, P])
        bias = c.sb("at_bias", [TP, 2 * HG])
        total = c.sb("at_total", [TP, 2, HG])
        inv = c.sb("at_inv", [TP, 2, HG])

        weights, prepared, loaded = c.sem("at_weights"), c.sem("at_prepared"), c.sem("at_loaded")
        filled = c.sem("at_filled")
        read = {"act": c.sem("at_act_read"), "dve": c.sem("at_dve_read")}
        high = c.sem("at_high")
        stacked = [c.sem(f"at_stacked{g}") for g in range(GROUPS)]
        biased, inverted, values = c.sem("at_biased"), c.sem("at_inverted"), c.sem("at_values")
        pv_done, gated = c.sem("at_pv_done"), c.sem("at_gated")
        STACKED = 2 * 4 * HG * 16

        def stacks(i, s, before=0):
            _, q, g, pair = s
            n = q + 2 * pair + 2 - before + (0 if g == 0 else 0)
            return i * (2 * STACKED) + n * STACKED

        with nc.Block() as block:

            @block.sync
            def _(sp):
                for g in range(GROUPS):
                    sp.sem_inc(stacked[g], STACKED)
                n = HEADS * HD
                for q in range(2):
                    r = slice(F * q, F * q + F)
                    sp.dma_start(W[r, 0:3 * n], d["W_qkv_t"]).then_inc(weights, 16)
                    sp.dma_start(W[r, 3 * n:4 * n], d["W_gate_t"]).then_inc(weights, 16)
                    sp.dma_start(bf[r, :], d["b_final"].unsqueeze(1)).then_inc(weights, 16)
                for g in range(GROUPS):
                    sp.dma_start(Wf[:, g, :], d["W_final_t"][g * P:(g + 1) * P]).then_inc(weights, 16)
                    sp.dma_start(bg[:, g:g + 1], d["b_gate"][g * P:(g + 1) * P].unsqueeze(1)).then_inc(weights, 16)

                def load(p):
                    sp.dma_start(norms[:], scratch[:, p].rearrange("p a j n -> p (a j) n")).then_inc(loaded, 16)

                def restack(q, g):
                    for h in range(HG):
                        for w, parts in enumerate(((0, 0, 1, 1), (0, 1, 0, 1))):
                            for b, part in enumerate(parts):
                                sp.dma_start(stack[w][g][HD * b:HD * b + HD, h, :],
                                             split[w][g][HD * h:HD * h + HD, part, :]).then_inc(stacked[g], 16)

                load(slice(0, 1))
                sp.wait_ge(read["dve"], n_read["dve"].ahead(("k", 0, 0, 1)))
                restack(0, 0)
                with sp.Fori(0, NP) as i:
                    for s in order:
                        if s[0] == "k":
                            sp.wait_ge(read["dve"], n_read["dve"].turn(i, s))
                            restack(*s[1:3])
                        elif s[0] == "load":
                            sp.wait_ge(filled, n_filled.turn(i, ("g", 1, 1, 0)))
                            load(bass.ds(i + 1, 1))
                sp.wait_ge(loaded, 16 * (NP + 1))
                for g in range(GROUPS):
                    sp.wait_ge(stacked[g], (2 * NP + 2 - g) * STACKED)

            WEIGHTS = 16 * 10

            @block.tensor
            def _(pe):
                pe.sem_inc(pv_done, 2)
                pe.wait_ge(weights, WEIGHTS)
                pe.wait_ge(prepared, 7)

                def project(s, slot):
                    kind, q, g = s[0:3]
                    if kind == "v":
                        for k, t in enumerate(V_TILES[g]):
                            mm = pe.matmul(flat(slot)[0:TP, k * 256:(k + 1) * 256],
                                           xn[F * q:F * q + F, t * TP:(t + 1) * TP],
                                           W[F * q:F * q + F, 512:768], start=True, stop=True)
                    else:
                        col = {"q": 0, "k": 1, "g": 3}[kind] * HEADS * HD + g * P
                        src = x1 if kind == "g" else xn
                        for hf in range(2):
                            mm = pe.matmul(slot[:, hf, 0:HALF], W[F * q:F * q + F, col:col + P],
                                           src[F * q:F * q + F, hf * HALF:(hf + 1) * HALF], start=True, stop=True)
                    mm.then_inc(filled, 1)

                def attend(m, hf, t):
                    for h in range(HG):
                        mm = pe.matmul(ACC[HD * h:HD * h + HD, hf, 0:HALF], vs[:, m % VRING, HD * h:HD * h + HD],
                                       E[:, m % ERING, h, hf * HALF:(hf + 1) * HALF],
                                       start=(t == 0), stop=(t == NT - 1))
                    return mm

                def finish(q, slot):
                    for hf in range(2):
                        for g in range(GROUPS):
                            mm = pe.matmul(slot[F * q:F * q + F, hf, 0:HALF], Wf[:, g, :],
                                           og[g][:, hf * HALF:(hf + 1) * HALF],
                                           start=(g == 0), stop=(g == GROUPS - 1))
                    mm.then_inc(filled, 1)

                pe.wait_ge(loaded, 16)
                for n, s in enumerate(first):
                    if n >= RING:
                        old = first[n - RING]
                        e = LAST_READER[old[0]]
                        pe.wait_ge(read[e], n_read[e].ahead(old))
                    project(s, slot_of(s, ahead=True))
                for e in by:
                    pe.wait_ge(read[e], RING + len(by_first[e]))
                for hf in range(2):
                    attend(NM - LAG, hf, 0)
                with pe.Fori(0, NP) as i:
                    for s in order:
                        kind = s[0]
                        if is_job(s):
                            n = jobs.index(s)
                            old = jobs[n - RING]
                            e = LAST_READER[old[0]]
                            pe.wait_ge(read[e], n_read[e].turn(i, old) if n >= RING else n_read[e].turn_before(i, old))
                        if kind in ("q", "k", "g", "v"):
                            if s == ("q", 0, 0, 1):
                                pe.wait_ge(loaded, i * 16 + 32)
                            project(s, slot_of(s))
                        elif kind == "S":
                            _, q, g, t, h = s
                            if (t, h) == (0, 0):
                                pe.wait_ge(stacked[g], stacks(i, (0, q, g, 0)))
                            slot = slot_of(s)
                            for hf in range(2):
                                mm = pe.matmul(slot[0:TP, hf, 0:HALF], stack[0][g][:, h, t * TP:(t + 1) * TP],
                                               stack[1][g][:, h, hf * HALF:(hf + 1) * HALF], start=True, stop=True)
                            mm.then_inc(filled, 1)
                        elif kind == "pv":
                            _, q, g, t, pair, hf = s
                            m = group(q, g, t)
                            if hf == 0:
                                pe.wait_ge(values, i * NM + m + NM * pair + 1 + VRING)
                                if t == 0:
                                    u = UNITS.index((q, g))
                                    pe.wait_ge(gated, n_gated.turn(i, gs[u]))
                                attend(m, 0, t)
                            else:
                                attend(m, 1, t).then_inc(pv_done, 1)
                        elif kind == "final":
                            _, q, pair = s
                            pe.wait_ge(gated, n_gated.turn(i, ("gated", q, 1, pair)))
                            finish(q, slot_of(s))
                for t in range(NT - LAG, NT):
                    m = group(1, 1, t)
                    pe.wait_ge(values, (NP - 1) * NM + m + 1 + VRING)
                    attend(m, 0, t)
                    attend(m, 1, t).then_inc(pv_done, 1)
                pe.wait_ge(gated, NP * 4 + 2)
                for e in by:
                    pe.wait_ge(read[e], RING + len(by_first[e]) + NP * len(by[e]))
                finish(1, slots[0])

            @block.scalar
            def _(act):
                act.sem_inc(read["act"], RING)
                act.wait_ge(prepared, 7)

                def read_out(s, slot, high_done):
                    kind, q, g = s[0:3]
                    if kind in ("q", "k"):
                        w = 0 if kind == "q" else 1
                        act.activation(halves(split[w][g][:, 0, :]), wide(slot), ACT.Copy,
                                       scale=C if w == 0 else 1.0).then_inc(high, 1)
                    elif kind == "g":
                        act.activation(halves(gate[g][:]), wide(slot), ACT.Tanh, bias=bg[:, g:g + 1],
                                       scale=0.5).then_inc(read["act"], 1)
                    else:
                        ts = V_TILES[g]
                        act.activation(V[q][:, ts[0]:ts[-1] + 1, :].rearrange("p t c -> p (t c)"),
                                       flat(slot)[0:TP, 0:len(ts) * 256], ACT.Copy).then_inc(read["act"], 1)

                for s in first:
                    act.wait_ge(filled, n_filled.ahead(s))
                    read_out(s, slot_of(s, ahead=True), None)
                with act.Fori(0, NP) as i:
                    for s in order:
                        kind = s[0]
                        if kind in ("q", "k", "g", "v"):
                            if kind in ("q", "k"):
                                act.wait_ge(stacked[s[2]], stacks(i, s, before=1))
                            if kind == "g":
                                u = UNITS.index(s[1:3]) + 4 * s[3]
                                act.wait_ge(gated, n_gated.turn(i, gs[u - 1]))
                            act.wait_ge(filled, n_filled.turn(i, s))
                            read_out(s, slot_of(s), None)
                        elif kind == "S":
                            _, q, g, t, h = s
                            n, m = tiles.index(s), group(q, g, t)
                            if h == 0:
                                act.wait_ge(pv_done, i * NM + m + 1)
                                act.wait_ge(inverted, i * NM + m + 1)
                            act.wait_ge(biased, n_biased.turn(i, s))
                            act.activation(halves(E[:, m % ERING, h, :]), wide(slot_of(s))[0:TP], ACT.Exp,
                                           bias=bias[:, n % 8:n % 8 + 1], scale=1.0,
                                           accum_out=total[:, m % 2, h:h + 1]).then_inc(read["act"], 1)

            @block.vector
            def _(v):
                v.sem_inc(read["dve"], RING)
                v.sem_inc(gated, 1)
                v.sem_inc(inverted, 2)
                for tile in (gate[1][:], og[0][:], E[:, NM % ERING - 2 + ERING:ERING], vs[:], H[:, 0, :]):
                    v.memset(tile, 0.0).then_inc(prepared, 1)
                v.wait_ge(weights, WEIGHTS)
                v.tensor_scalar(bg[:], bg[:], 0.5, None, ALU.mult).then_inc(prepared, 1)
                v.tensor_scalar(Wf[:], Wf[:], 0.5, None, ALU.mult).then_inc(prepared, 1)
                v.wait_ge(prepared, 7)

                def low(s, slot):
                    w, g = (0 if s[0] == "q" else 1), s[2]
                    v.scalar_tensor_tensor(halves(split[w][g][:, 1, :]), wide(slot), C if w == 0 else 1.0,
                                           halves(split[w][g][:, 0, :]), ALU.mult, ALU.subtract)\
                     .then_inc(read["dve"], 1)

                def apply_gate(g):
                    v.scalar_tensor_tensor(halves(og[g][:]), halves(gate[g][:]), 1.0, wide(ACC),
                                           ALU.add, ALU.mult).then_inc(gated, 1)

                def keep(q, slot, p):
                    r = slice(F * q, F * q + F)
                    h = H[r, p, :].rearrange("p a (h n) -> p (a h) n", h=2)
                    v.scalar_tensor_tensor(h, wide(slot)[r], bf[r, 0:1], h, ALU.add, ALU.add).then_inc(read["dve"], 1)

                for s in qk(first):
                    v.wait_ge(high, n_high.ahead(s))
                    low(s, slot_of(s, ahead=True))
                with v.Fori(0, NP) as i:
                    for s in order:
                        kind = s[0]
                        if kind in ("q", "k"):
                            v.wait_ge(high, n_high.turn(i, s))
                            low(s, slot_of(s))
                        elif kind == "S":
                            n = tiles.index(s)
                            v.wait_ge(filled, n_filled.turn(i, s))
                            v.tensor_reduce(bias[:, n % 8:n % 8 + 1], wide(slot_of(s))[0:TP], AX.XY, ALU.max, negate=True)\
                             .then_inc(biased, 1)
                        elif kind == "inv":
                            m = group(*s[1:])
                            v.wait_ge(read["act"], n_read["act"].turn(i, ("S",) + s[1:] + (HG - 1,)))
                            v.wait_ge(values, i * NM + m + 1)
                            v.reciprocal(inv[:, m % 2, :], total[:, m % 2, :]).then_inc(inverted, 1)
                        elif kind == "gated":
                            _, q, g, pair = s
                            v.wait_ge(pv_done, i * NM + (group(q, g, NT - 1) + NM * pair + 5))
                            apply_gate(g)
                        elif kind == "final":
                            _, q, pair = s
                            v.wait_ge(filled, n_filled.turn(i, s))
                            keep(q, slot_of(s), bass.ds(i + 1 + pair, 1))
                v.wait_ge(pv_done, NP * NM + 4)
                apply_gate(1)
                v.wait_ge(filled, len(first) + NP * len(jobs) + 1)
                keep(1, slots[0], slice(NP, NP + 1))

            @block.gpsimd
            def _(pool):
                pool.sem_inc(values, VRING)
                with pool.Fori(0, NP) as i:
                    for s in order:
                        if s[0] != "inv":
                            continue
                        _, q, g, t = s
                        m = group(q, g, t)
                        pool.wait_ge(inverted, i * NM + m + 1 + 2)
                        pool.wait_ge(pv_done, i * NM + m + 3)
                        pool.tensor_tensor(vs[:, m % VRING, :].rearrange("p (h c) -> p h c", h=HG),
                                           V[q][:, t, g * P:(g + 1) * P].rearrange("p (h c) -> p h c", h=HG),
                                           inv[:, m % 2, :].unsqueeze(2).broadcast_to([TP, HG, HD]), ALU.mult)\
                            .then_inc(values, 1)


HID, LAYERS = 128, 2


def routed_ffn(core, slots, d, H, NP):
    nc = core.nc
    NE = d["Wr_t"].shape[1]
    SEG = 4
    with ExitStack() as st:
        c = Core(nc, st)
        center, mean = c.sb("rf_center", [P, P]), c.sb("rf_mean", [P, P])
        Wi = c.sb("rf_wi", [P, HID])
        bi, bo, eps = c.sb("rf_bi", [P, 1]), c.sb("rf_bo", [P, 1]), c.sb("rf_eps", [P, 1])
        Wo = c.sb("rf_wo", [P, F])
        table = c.sb("rf_table", [P, NE + 1, LAYERS, HID + 1])
        shared = c.sb("rf_shared", [P, LAYERS, HID + 1])
        eye = c.sb("rf_eye", [P, P])
        ids = c.sb("rf_ids", [1, 2 * 2 * NP], I32)
        idf = c.sb("rf_idf", [1, 3, 2 * 2 * NP])
        chosen = [c.sb(f"rf_chosen{k}", [P, SEG, LAYERS, HID + 1]) for k in range(2)]
        t0 = [c.sb(f"rf_t{k}", [P, N]) for k in range(2)]
        r1 = [c.sb(f"rf_r{k}", [P, N]) for k in range(2)]
        xn = [c.sb(f"rf_xn{k}", [P, N]) for k in range(2)]
        a = [[c.sb(f"rf_a{k}{q}", [P, N]) for q in range(2)] for k in range(2)]
        weights, tables, routed = c.sem("rf_weights"), c.sem("rf_tables"), c.sem("rf_routed")
        sems = lambda name: [c.sem(f"rf_{name}{k}") for k in range(2)]
        centered, squared, varied, logged, rooted, normed = map(
            sems, ("centered", "squared", "varied", "logged", "rooted", "normed"))
        widened, hidden = sems("widened"), sems("hidden")
        mixed = [[c.sem(f"rf_mixed{k}_{l}") for l in range(LAYERS)] for k in range(2)]
        left = [[c.sem(f"rf_left{k}_{l}") for l in range(LAYERS)] for k in range(2)]
        right = [[c.sem(f"rf_right{k}_{l}") for l in range(LAYERS)] for k in range(2)]
        projected, kept, gathered = sems("projected"), sems("kept"), sems("gathered")
        loops = NP // 2
        WEIGHTS = 16 * (2 * 2 + 5 + 5)

        with nc.Block() as block:

            @block.sync
            def _(sp):
                for q in range(2):
                    sp.dma_start(Wi[F * q:F * q + F, :], d["Wi_t"]).then_inc(weights, 16)
                    sp.dma_start(bo[F * q:F * q + F, :], d["bo"].unsqueeze(1)).then_inc(weights, 16)
                for tile, src in ((bi, d["bi"].unsqueeze(1)), (Wo, d["Wo_t"]), (center, d["center"]),
                                  (mean, d["mean"]), (eye, d["eye"])):
                    sp.dma_start(tile[:], src).then_inc(weights, 16)
                for l in range(LAYERS):
                    sp.dma_start(table[:, 0:NE, l, 0:HID], d["Wr_t"][:, :, l]).then_inc(weights, 16)
                sp.dma_start(shared[:, :, 0:HID], d["Ws"]).then_inc(weights, 16)
                with nc.allow_non_contiguous_dma(reason="a bias column per expert"):
                    sp.dma_start(table[:, 0:NE, :, HID:HID + 1], d["br_t"].unsqueeze(3)).then_inc(weights, 16)
                    sp.dma_start(shared[:, :, HID:HID + 1], d["bs"].unsqueeze(2)).then_inc(weights, 16)
                sp.dma_start(ids[:], d["route"]).then_inc(routed, 16)

            @block.gpsimd
            def _(pool):
                for k in range(2):
                    pool.sem_inc(gathered[k], LEAD)
                pool.wait_ge(tables, 4)
                with pool.Fori(0, loops) as i:
                    for k in range(2):
                        pool.wait_ge(projected[k], at(i - 1))
                        for s in range(SEG):
                            e = pool.value_load(ids[0:1, bass.ds(i * 8 + (SEG * k + s), 1)], min_val=0, max_val=NE)
                            copy = pool.tensor_copy(chosen[k][:, s, :, :].rearrange("p l f -> p (l f)"),
                                                    table[:, bass.ds(e, 1), :, :].rearrange("p a l f -> p (a l f)"))
                        copy.then_inc(gathered[k], 1)

            @block.tensor
            def _(pe):
                for k in range(2):
                    lead(pe, [centered[k], varied[k], projected[k]])
                    lead(pe, [widened[k]] + mixed[k], 2)
                pe.wait_ge(weights, WEIGHTS)
                with pe.Fori(0, loops) as i:
                    for k in range(2):
                        pe.wait_ge(kept[k], at(i - 1))
                        for hf in range(2):
                            mm = pe.matmul(slots[2 * k][:, hf, 0:HALF], center[:],
                                           H[:, bass.ds(2 * i + k + 1, 1), hf * HALF:(hf + 1) * HALF]
                                           .rearrange("p a n -> p (a n)"), start=True, stop=True)
                        mm.then_inc(centered[k], 1)
                    for k in range(2):
                        pe.wait_ge(squared[k], at(i))
                        for hf in range(2):
                            mm = pe.matmul(slots[2 * k + 1][:, hf, 0:HALF], mean[:], t0[k][:, hf * HALF:(hf + 1) * HALF],
                                           start=True, stop=True)
                        mm.then_inc(varied[k], 1)
                    for k in range(2):
                        pe.wait_ge(normed[k], at(i))
                        for q in range(2):
                            for hf in range(2):
                                mm = pe.matmul(slots[2 * k + q][:, hf, 0:HALF], Wi[F * q:F * q + F, :],
                                               xn[k][F * q:F * q + F, hf * HALF:(hf + 1) * HALF], start=True, stop=True)
                            mm.then_inc(widened[k], 1)
                    for l in range(LAYERS):
                        for k in range(2):
                            if l == 0:
                                pe.wait_ge(gathered[k], at(i))
                            for q in range(2):
                                if l == 0:
                                    pe.wait_ge(hidden[k], 2 * i + q + 1 + 2 * LEAD)
                                else:
                                    pe.wait_ge(left[k][0], 2 * i + q + 1 + 2 * LEAD)
                                    pe.wait_ge(right[k][0], 2 * i + q + 1 + 2 * LEAD)
                                for hf in range(2):
                                    mm = pe.matmul(slots[2 * k + q][:, hf, 0:HALF], chosen[k][:, 2 * q + hf, l, 0:HID],
                                                   a[k][q][:, hf * HALF:(hf + 1) * HALF], start=True, stop=True)
                                mm.then_inc(mixed[k][l], 1)
                    for k in range(2):
                        pe.wait_ge(left[k][1], 2 * i + 2 + 2 * LEAD)
                        pe.wait_ge(right[k][1], 2 * i + 2 + 2 * LEAD)
                        for hf in range(2):
                            for q in range(2):
                                mm = pe.matmul(slots[2 * k][F * q:F * q + F, hf, 0:HALF], Wo[:],
                                               a[k][q][:, hf * HALF:(hf + 1) * HALF], start=True, stop=True)
                        mm.then_inc(projected[k], 1)

            @block.scalar
            def _(act):
                for k in range(2):
                    lead(act, [squared[k], logged[k], rooted[k]])
                    lead(act, [hidden[k]] + left[k], 2)
                act.wait_ge(tables, 4)
                with act.Fori(0, loops) as i:
                    for k in range(2):
                        act.wait_ge(centered[k], at(i))
                        act.activation(halves(t0[k][:]), wide(slots[2 * k]), ACT.Square).then_inc(squared[k], 1)
                    for k in range(2):
                        act.wait_ge(varied[k], at(i))
                        act.activation(halves(r1[k][:]), wide(slots[2 * k + 1]), ACT.Ln, bias=eps[:, 0:1])\
                           .then_inc(logged[k], 1)
                    for k in range(2):
                        act.wait_ge(logged[k], at(i))
                        act.activation(t0[k][:], r1[k][:], ACT.Exp, scale=-0.5).then_inc(rooted[k], 1)
                    for k in range(2):
                        for q in range(2):
                            act.wait_ge(widened[k], 2 * i + q + 1 + 2 * LEAD)
                            act.activation(halves(a[k][q][:]), wide(slots[2 * k + q]), ACT.Relu, bias=bi[:, 0:1])\
                               .then_inc(hidden[k], 1)
                    for l in range(LAYERS):
                        for k in range(2):
                            for q in range(2):
                                act.wait_ge(mixed[k][l], 2 * i + q + 1 + 2 * LEAD)
                                act.activation(a[k][q][:, 0:HALF], slots[2 * k + q][:, 0, 0:HALF], ACT.Relu,
                                               bias=chosen[k][:, 2 * q, l, HID:HID + 1]).then_inc(left[k][l], 1)

            @block.vector
            def _(v):
                for k in range(2):
                    lead(v, [normed[k], kept[k]])
                    lead(v, right[k], 2)
                v.memset(eps[:], EPS).then_inc(tables, 1)
                v.memset(table[:, NE, :, :], 0.0).then_inc(tables, 1)
                v.wait_ge(weights, WEIGHTS)
                v.tensor_tensor(shared[:, :, 0:HID], shared[:, :, 0:HID],
                                eye[:].unsqueeze(1).broadcast_to([P, LAYERS, HID]), ALU.add).then_inc(tables, 1)
                v.wait_ge(tables, 3)
                for l in range(LAYERS):
                    ins = v.tensor_tensor(table[:, :, l, :], table[:, :, l, :],
                                          shared[:, l, :].unsqueeze(1).broadcast_to([P, NE + 1, HID + 1]), ALU.add)
                v.wait_ge(routed, 16)
                v.tensor_copy(idf[:, 0, :], ids[:]).then_inc(routed, 1)
                v.wait_ge(routed, 17)
                v.tensor_scalar(idf[:, 1, :], idf[:, 0, :], 0.0, None, ALU.is_ge).then_inc(routed, 1)
                v.tensor_scalar(idf[:, 2, :], idf[:, 0, :], float(NE), None, ALU.is_lt).then_inc(routed, 1)
                v.wait_ge(routed, 19)
                v.tensor_tensor(idf[:, 1, :], idf[:, 1, :], idf[:, 2, :], ALU.mult).then_inc(routed, 1)
                v.tensor_scalar(idf[:, 0, :], idf[:, 0, :], float(NE), None, ALU.subtract).then_inc(routed, 1)
                v.wait_ge(routed, 21)
                v.tensor_tensor(idf[:, 0, :], idf[:, 0, :], idf[:, 1, :], ALU.mult).then_inc(routed, 1)
                v.wait_ge(routed, 22)
                v.tensor_scalar(ids[:], idf[:, 0, :], float(NE), None, ALU.add).then_inc(tables, 1)
                with v.Fori(0, loops) as i:
                    for k in range(2):
                        v.wait_ge(rooted[k], at(i))
                        v.tensor_tensor(halves(xn[k][:]), wide(slots[2 * k]), halves(t0[k][:]), ALU.mult)\
                         .then_inc(normed[k], 1)
                    for l in range(LAYERS):
                        for k in range(2):
                            for q in range(2):
                                v.wait_ge(mixed[k][l], 2 * i + q + 1 + 2 * LEAD)
                                v.tensor_scalar(a[k][q][:, HALF:N], slots[2 * k + q][:, 1, 0:HALF],
                                                chosen[k][:, 2 * q + 1, l, HID:HID + 1], 0.0, ALU.add, ALU.max)\
                                 .then_inc(right[k][l], 1)
                    for k in range(2):
                        v.wait_ge(projected[k], at(i))
                        h = H[:, bass.ds(2 * i + k + 1, 1), :].rearrange("p a (h n) -> p (a h) n", h=2)
                        v.scalar_tensor_tensor(h, wide(slots[2 * k]), bo[:, 0:1], h, ALU.add, ALU.add)\
                         .then_inc(kept[k], 1)


CUT = 448


def causal_attention(core, slots, d, H, X, sums, NP):
    nc = core.nc
    with ExitStack() as st:
        c = Core(nc, st)
        center, mean, eps = c.sb("ca_center", [P, P]), c.sb("ca_mean", [P, P]), c.sb("ca_eps", [P, 1])
        W = c.sb("ca_w", [F, 4, F])
        A, Bv = c.sb("ca_a", [P, P]), c.sb("ca_b", [P, P])
        ab = c.sb("ca_ab", [F, 2, F])
        causal = c.sb("ca_causal", [TP, TP])
        per_row = c.sb("ca_per_row", [P, N])
        t0, r1 = [c.sb(f"ca_t{k}", [P, N]) for k in range(2)], [c.sb(f"ca_r{k}", [P, N]) for k in range(2)]
        xn = [c.sb(f"ca_xn{k}", [P, N]) for k in range(2)]
        U = [c.sb(f"ca_u{k}", [P, N]) for k in range(2)]
        V = [c.sb(f"ca_v{k}", [TP, NT, P]) for k in range(2)]
        PB = 4
        prob = c.sb("ca_prob", [TP, PB, N])
        weights, ready = c.sem("ca_weights"), c.sem("ca_ready")
        sems = lambda name: [c.sem(f"ca_{name}{k}") for k in range(2)]
        centered, squared, varied, logged, rooted, normed = map(
            sems, ("centered", "squared", "varied", "logged", "rooted", "normed"))
        turned, scaled, valued, v_ready = map(sems, ("turned", "scaled", "valued", "v_ready"))
        scored, diag, rest = c.sem("ca_scored"), c.sem("ca_diag"), c.sem("ca_rest")
        used = c.sem("ca_used")
        kept, last = sems("kept"), sems("last")
        centered2, squared2, varied2, logged2, rooted2 = map(
            sems, ("centered2_", "squared2_", "varied2_", "logged2_", "rooted2_"))
        loops = NP // 2
        NS = 2 * 2 * NT
        tiles = [(k, m, q) for k in range(2) for m in range(NT) for q in range(2)]

        NR = sum(m * TP < CUT for _, m, _ in tiles)

        def rests(n):
            return sum(m * TP < CUT for _, m, _ in tiles[:n + 1])

        def parts(lo):
            return [(b, max(lo, CUT * b) - CUT * b, (CUT, N - CUT)[b], CUT * b) for b in range(2)
                    if lo < (CUT, N)[b]]

        with nc.Block() as block:

            @block.sync
            def _(sp):
                for j, name in enumerate(("Wq", "Wk", "Wv", "Wo1_t")):
                    sp.dma_start(W[:, j, :], d[name]).then_inc(weights, 16)
                for tile, name in ((center, "center"), (mean, "mean"), (causal, "causal"), (per_row, "per_row")):
                    sp.dma_start(tile[:], d[name]).then_inc(weights, 16)
                sp.wait_ge(ready, 5)
                for j, tile in enumerate((A, Bv)):
                    for q in range(2):
                        r = slice(F * q, F * q + F)
                        sp.dma_start(tile[r, r], ab[:, j, :]).then_inc(weights, 16)

            @block.gpsimd
            def _(pool):
                pool.memset(A[:], 0.0).then_inc(ready, 1)
                pool.memset(Bv[:], 0.0).then_inc(ready, 1)

            def norm_mm(pe, i, k, lhs, src, slot, wait, value, done):
                pe.wait_ge(wait, value)
                for hf in range(2):
                    mm = pe.matmul(slot[:, hf, 0:HALF], lhs[:], src[:, hf * HALF:(hf + 1) * HALF], start=True, stop=True)
                mm.then_inc(done, 1)

            @block.tensor
            def _(pe):
                for k in range(2):
                    lead(pe, [centered[k], varied[k], turned[k], valued[k], centered2[k], varied2[k]])
                pe.sem_inc(used, PB)
                pe.wait_ge(weights, 16 * 8)
                pe.matmul(slots[0][0:F, 0, 0:F], W[:, 0, :], W[:, 1, :], start=True, stop=True)
                pe.matmul(slots[0][0:F, 0, F:2 * F], W[:, 2, :], W[:, 3, :], start=True, stop=True).then_inc(ready, 1)
                pe.wait_ge(weights, 16 * 12)
                with pe.Fori(0, loops) as i:
                    for k in range(2):
                        norm_mm(pe, i, k, center, H[:, bass.ds(2 * i + k + 1, 1), :].rearrange("p a n -> p (a n)"),
                                slots[k], last[k], at(i - 1), centered[k])
                    for k in range(2):
                        norm_mm(pe, i, k, mean, t0[k], slots[2 + k], squared[k], at(i), varied[k])
                    for k in range(2):
                        norm_mm(pe, i, k, A, xn[k], slots[k], normed[k], at(i), turned[k])
                        for t in range(NT):
                            mm = pe.matmul(flat(slots[2 + k])[0:TP, t * P:(t + 1) * P], xn[k][:, t * TP:(t + 1) * TP],
                                           Bv[:], start=True, stop=True)
                        mm.then_inc(valued[k], 1)

                    def scores(n):
                        k, m, q = tiles[n]
                        slot = slots[n % 3]
                        if n < 3:
                            pe.wait_ge(scaled[1], at(i))
                            pe.wait_ge(v_ready[0], at(i))
                        else:
                            pe.wait_ge(diag, i * NS + n - 2)
                            pe.wait_ge(rest, i * NR + rests(n - 3))
                        for b, lo, hi, c0 in parts(m * TP):
                            mm = pe.matmul(slot[0:TP, b, lo:hi], xn[k][F * q:F * q + F, m * TP:(m + 1) * TP],
                                           U[k][F * q:F * q + F, c0 + lo:c0 + hi], start=True, stop=True)
                        mm.then_inc(scored, 1)

                    def values(n):
                        k, m, _ = tiles[n]
                        if m == 0:
                            pe.wait_ge(v_ready[1], at(i))
                            if k == 1:
                                pe.wait_ge(kept[0], at(i))
                        pe.wait_ge(diag, i * NS + n + 2)
                        pe.wait_ge(rest, i * NR + rests(n + 1))
                        for b, lo, hi, c0 in parts(m * TP):
                            for q in range(2):
                                mm = pe.matmul(slots[3][F * q:F * q + F, b, lo:hi], V[k][:, m, F * q:F * q + F],
                                               prob[:, (n + q) % PB, c0 + lo:c0 + hi],
                                               start=(m == 0), stop=(m == (3 if b == 0 else NT - 1)))
                        mm.then_inc(used, 2)

                    for n in range(0, NS, 2):
                        scores(n)
                        scores(n + 1)
                        if n >= 2:
                            values(n - 2)
                    values(NS - 2)
                    for k in range(2):
                        norm_mm(pe, i, k, center, H[:, bass.ds(2 * i + k + 1, 1), :].rearrange("p a n -> p (a n)"),
                                slots[k], kept[k], at(i), centered2[k])
                    for k in range(2):
                        norm_mm(pe, i, k, mean, t0[k], slots[2 + k], squared2[k], at(i), varied2[k])

            @block.scalar
            def _(act):
                for k in range(2):
                    lead(act, [squared[k], logged[k], rooted[k], v_ready[k], squared2[k], logged2[k], rooted2[k]])
                act.wait_ge(ready, 4)
                with act.Fori(0, loops) as i:

                    def inverse_root(centered, squared, varied, logged, rooted):
                        for k in range(2):
                            act.wait_ge(centered[k], at(i))
                            act.activation(halves(t0[k][:]), wide(slots[k]), ACT.Square).then_inc(squared[k], 1)
                        for k in range(2):
                            act.wait_ge(varied[k], at(i))
                            act.activation(halves(r1[k][:]), wide(slots[2 + k]), ACT.Ln, bias=eps[:, 0:1])\
                               .then_inc(logged[k], 1)
                        for k in range(2):
                            act.wait_ge(logged[k], at(i))
                            act.activation(t0[k][:], r1[k][:], ACT.Exp, scale=-0.5).then_inc(rooted[k], 1)

                    inverse_root(centered, squared, varied, logged, rooted)
                    for k in range(2):
                        act.wait_ge(valued[k], at(i))
                        act.activation(V[k][:].rearrange("p t f -> p (t f)"), flat(slots[2 + k])[0:TP, 0:NT * P],
                                       ACT.Copy).then_inc(v_ready[k], 1)
                    for n, (k, m, q) in enumerate(tiles):
                        if m * TP >= CUT:
                            continue
                        act.wait_ge(scored, i * NS + n + 1)
                        act.wait_ge(used, i * NS + n // 2 * 2 + 2)
                        act.activation(prob[:, n % PB, CUT:N], slots[n % 3][0:TP, 1, 0:N - CUT], ACT.Relu)\
                           .then_inc(rest, 1)
                    inverse_root(centered2, squared2, varied2, logged2, rooted2)

            @block.vector
            def _(v):
                for k in range(2):
                    lead(v, [normed[k], scaled[k], kept[k], last[k]])
                v.memset(eps[:], EPS).then_inc(ready, 1)
                v.wait_ge(ready, 4)
                v.tensor_copy(ab[:].rearrange("p a f -> p (a f)"), slots[0][0:F, 0, 0:2 * F]).then_inc(ready, 1)
                with v.Fori(0, loops) as i:
                    for k in range(2):
                        v.wait_ge(rooted[k], at(i))
                        v.tensor_tensor(halves(xn[k][:]), wide(slots[k]), halves(t0[k][:]), ALU.mult)\
                         .then_inc(normed[k], 1)
                    for k in range(2):
                        v.wait_ge(turned[k], at(i))
                        v.tensor_tensor(halves(U[k][:]), wide(slots[k]), halves(per_row[:]), ALU.mult)\
                         .then_inc(scaled[k], 1)

                    def keep(k):
                        v.wait_ge(used, i * NS + (k + 1) * 2 * NT + PB)
                        h = H[:, bass.ds(2 * i + k + 1, 1), :].rearrange("p a n -> p (a n)")
                        v.tensor_tensor(h[:, 0:CUT], h[:, 0:CUT], slots[3][:, 0, 0:CUT], ALU.add)
                        v.tensor_tensor(h[:, CUT:N], h[:, CUT:N], slots[3][:, 1, 0:N - CUT], ALU.add)\
                         .then_inc(kept[k], 1)

                    for n, (k, m, q) in enumerate(tiles):
                        v.wait_ge(scored, i * NS + n + 1)
                        v.wait_ge(used, i * NS + n // 2 * 2 + 2)
                        slot, b, c0 = slots[n % 3], m * TP // CUT, m * TP // CUT * CUT
                        d0 = m * TP - c0
                        ins = v.scalar_tensor_tensor(prob[:, n % PB, m * TP:(m + 1) * TP], slot[0:TP, b, d0:d0 + TP],
                                                     0.0, causal[:], ALU.max, ALU.mult)
                        end = (CUT, N)[b]
                        if (m + 1) * TP < end:
                            ins = v.tensor_scalar(prob[:, n % PB, (m + 1) * TP:end],
                                                  slot[0:TP, b, d0 + TP:end - c0], 0.0, None, ALU.max)
                        ins.then_inc(diag, 1)
                        if n == 2 * NT + 3:
                            keep(0)
                    keep(1)
                    for k in range(2):
                        v.wait_ge(rooted2[k], at(i))
                        x = X[:, bass.ds(2 * i + k, 1), :].rearrange("p a (h n) -> p (a h) n", h=2)
                        v.scalar_tensor_tensor(x, wide(slots[k]), 1.0, halves(t0[k][:]), ALU.mult, ALU.mult,
                                               accum_out=sums[:, bass.ds(2 * i + k, 1)]).then_inc(last[k], 1)


TOP = 2
FF = 128


class Routes:

    def __init__(self, core, NP):
        self.expert = core.sb("rt_expert", [1, 2 * TOP, NP], I32)
        self.weight = core.sb("rt_weight", [P, 2 * TOP, NP])
        self.b2 = core.sb("rt_b2", [P, NP])


def routing(core, slots, d, sums, R, NP):
    nc = core.nc
    E = d["Wr1"].shape[1]
    B = 2 * NP
    capacity = float(-(-B * N * 5 // (4 * E)))
    with ExitStack() as st:
        c = Core(nc, st)
        Wr = c.sb("rt_wr", [P, E])
        br, ids = c.sb("rt_br", [NP, E]), c.sb("rt_ids", [NP, E])
        b2 = c.sb("rt_b2w", [E, F])
        eye, ones = c.sb("rt_eye", [P, P]), c.sb("rt_ones", [NP, NP])
        z, w = c.sb("rt_z", [NP, 2, E]), c.sb("rt_w", [NP, 2, E])
        m = c.sb("rt_m", [NP, 2])
        load = c.sb("rt_load", [NP, E])
        top, topi, topf = c.sb("rt_top", [NP, 2, 8]), c.sb("rt_topi", [NP, 2, 8], U32), c.sb("rt_topf", [NP, 2, 8])
        e2, tw = c.sb("rt_e2", [NP, 2]), c.sb("rt_tw", [NP, 2, TOP])
        wide_w = c.sb("rt_wide", [NP, 2 * TOP, P])
        dense = c.sb("rt_dense", [NP, 2, TOP, E])
        denseT = c.sb("rt_denseT", [E, 2, NP])
        loaded, step, mm_done, act_done = c.sem("rt_loaded"), c.sem("rt_step"), c.sem("rt_mm"), c.sem("rt_act")
        both = lambda t: t.unsqueeze(1).broadcast_to([NP, 2, E])
        each = lambda t: t.unsqueeze(2).broadcast_to([NP, 2, E])
        LOADED = 16 * 6
        with nc.Block() as block:

            @block.sync
            def _(sp):
                for q in range(2):
                    sp.dma_start(Wr[F * q:F * q + F, :], d["Wr1"]).then_inc(loaded, 16)
                for tile, name in ((br, "br1"), (ids, "experts"), (b2, "b2"), (eye, "eye")):
                    sp.dma_start(tile[:], d[name]).then_inc(loaded, 16)

            @block.vector
            def _(v):
                n = [0]

                def done(ins):
                    n[0] += 1
                    ins.then_inc(step, 1)
                    v.wait_ge(step, n[0])

                def softmax(turn):
                    done(v.tensor_reduce(m[:], z[:], AX.X, ALU.max))
                    done(v.tensor_tensor(z[:], z[:], each(m[:]), ALU.subtract))
                    v.wait_ge(act_done, turn)
                    done(v.tensor_reduce(m[:], w[:], AX.X, ALU.add))
                    done(v.reciprocal(m[:], m[:]))
                    done(v.tensor_tensor(w[:], w[:], each(m[:]), ALU.mult))

                v.memset(ones[:], 1.0)
                v.wait_ge(loaded, LOADED)
                v.wait_ge(mm_done, 1)
                for q in range(2):
                    v.scalar_tensor_tensor(z[:, q, :], slots[q][0:NP, 0, 0:E], 1.0 / N, br[:], ALU.mult, ALU.add)
                done(v.tensor_copy(topf[:].rearrange("p q e -> p (q e)")[:, 0:E], br[:]))
                softmax(1)
                v.wait_ge(mm_done, 2)
                done(v.tensor_copy(load[:], slots[2][0:NP, 0, 0:E]))
                done(v.tensor_tensor(load[:], load[:], slots[2][0:NP, 0, E:2 * E], ALU.add))
                done(v.tensor_scalar(load[:], load[:], float(N), 1e-30, ALU.mult, ALU.max))
                done(v.reciprocal(load[:], load[:]))
                done(v.tensor_scalar(load[:], load[:], capacity, 1.0, ALU.mult, ALU.min))
                done(v.tensor_tensor(z[:], w[:], both(load[:]), ALU.mult))
                softmax(2)
                for q in range(2):
                    done(v.max(top[:, q, :], w[:, q, :]))
                    done(v.max_index(topi[:, q, :], top[:, q, :], w[:, q, :]))
                done(v.tensor_copy(topf[:], topi[:]))
                done(v.tensor_tensor(m[:], top[:, :, 1], top[:, :, 0], ALU.subtract))
                v.wait_ge(act_done, 3)
                done(v.tensor_scalar(m[:], e2[:], 1.0, None, ALU.add))
                done(v.reciprocal(tw[:, :, 0], m[:]))
                done(v.tensor_tensor(tw[:, :, 1], tw[:, :, 0], e2[:], ALU.mult))
                done(v.tensor_copy(wide_w[:], tw[:].rearrange("p q r -> p (q r)").unsqueeze(2)
                                   .broadcast_to([NP, 2 * TOP, P])))
                for q in range(2):
                    for r in range(TOP):
                        done(v.tensor_scalar(dense[:, q, r, :], ids[:], topf[:, q, r:r + 1], tw[:, q, r:r + 1],
                                             ALU.is_equal, ALU.mult))
                done(v.tensor_tensor(dense[:, :, 0, :], dense[:, :, 0, :], dense[:, :, 1, :], ALU.add))
                v.wait_ge(mm_done, 3)
                for q in range(2):
                    v.tensor_copy(denseT[:, q, :], slots[0][0:E, 0, q * NP:(q + 1) * NP])
                v.tensor_copy(R.expert[:].rearrange("a j p -> a (j p)"), slots[1][0:1, 0, 0:2 * TOP * NP])
                done(v.tensor_copy(R.weight[:].rearrange("a j p -> a (j p)"), slots[2][:, 0, 0:2 * TOP * NP]))
                v.wait_ge(mm_done, 4)
                done(v.tensor_copy(R.b2[:], slots[3][:, 0, 0:NP]))

            @block.scalar
            def _(act):
                for turn, after in ((1, 3), (2, 14)):
                    act.wait_ge(step, after)
                    act.activation(w[:], z[:], ACT.Exp).then_inc(act_done, 1)
                act.wait_ge(step, 23)
                act.activation(e2[:], m[:], ACT.Exp).then_inc(act_done, 1)

            @block.tensor
            def _(pe):
                pe.wait_ge(loaded, LOADED)
                for q in range(2):
                    mm = pe.matmul(slots[q][0:NP, 0, 0:E], sums[F * q:F * q + F, :], Wr[F * q:F * q + F, :],
                                   start=True, stop=True)
                mm.then_inc(mm_done, 1)
                pe.wait_ge(step, 6)
                pe.matmul(slots[2][0:NP, 0, 0:2 * E], ones[:], w[:].rearrange("p q e -> p (q e)"),
                          start=True, stop=True).then_inc(mm_done, 1)
                pe.wait_ge(step, 32)
                for q in range(2):
                    pe.matmul(slots[0][0:E, 0, q * NP:(q + 1) * NP], dense[:, q, 0, :], eye[0:NP, 0:NP],
                              start=True, stop=True)
                for q in range(2):
                    for r in range(TOP):
                        j = 2 * q + r
                        pe.matmul(slots[1][0:1, 0, j * NP:(j + 1) * NP], topf[:, q, r:r + 1], eye[0:NP, 0:NP],
                                  start=True, stop=True)
                for j in range(2 * TOP):
                    mm = pe.matmul(slots[2][:, 0, j * NP:(j + 1) * NP], wide_w[:, j, :], eye[0:NP, 0:NP],
                                   start=True, stop=True)
                mm.then_inc(mm_done, 1)
                pe.wait_ge(step, 33)
                for q in range(2):
                    mm = pe.matmul(slots[3][F * q:F * q + F, 0, 0:NP], b2[:], denseT[:, q, :], start=True, stop=True)
                mm.then_inc(mm_done, 1)


def mixture(core, slots, d, H, X, R, out, NP):
    nc = core.nc
    E = d["W1"].shape[1]
    with ExitStack() as st:
        c = Core(nc, st)
        center, mean, eye = c.sb("mx_center", [P, P]), c.sb("mx_mean", [P, P]), c.sb("mx_eye", [P, P])
        eps, gamma, beta = c.sb("mx_eps", [P, 1]), c.sb("mx_gamma", [P, 1]), c.sb("mx_beta", [P, 1])
        T1, b1, T2 = c.sb("mx_w1", [P, E, FF]), c.sb("mx_b1", [FF, E]), c.sb("mx_w2", [FF, E, F])
        pair = lambda name, shape: [c.sb(f"mx_{name}{k}", shape) for k in range(2)]
        C1, cb1, C2 = pair("c1_", [P, 2 * TOP, FF]), pair("cb1_", [FF, 2, TOP]), pair("c2_", [FF, 2, TOP, F])
        xs, t0, r1, z = pair("xs", [P, N]), pair("t", [P, N]), pair("r", [P, N]), pair("z", [P, N])
        G = [[[c.sb(f"mx_g{k}{q}{r}", [FF, N]) for r in range(TOP)] for q in range(2)] for k in range(2)]
        OT = pair("out", [TP, 2, NT, F])
        weights, ready = c.sem("mx_weights"), c.sem("mx_ready")
        sems = lambda name: [c.sem(f"mx_{name}{k}") for k in range(2)]
        x_in, gathered, lifted, gelued, lowered, summed = map(
            sems, ("x_in", "gathered", "lifted", "gelued", "lowered", "summed"))
        centered, squared, varied, logged, rooted = map(
            sems, ("centered", "squared", "varied", "logged", "rooted"))
        normed, scaled, shifted, turned, copied, stored = map(
            sems, ("normed", "scaled", "shifted", "turned", "copied", "stored"))
        loops = NP // 2
        WEIGHTS = 16 * (3 * 2 + 5)
        out_v = out.rearrange("b (p t) f -> p b (t f)", t=NT)

        with nc.Block() as block:

            @block.sync
            def _(sp):
                for k in range(2):
                    lead(sp, [x_in[k], stored[k]], 16)
                for q in range(2):
                    r = slice(F * q, F * q + F)
                    sp.dma_start(T1[r], d["W1"]).then_inc(weights, 16)
                    sp.dma_start(gamma[r, :], d["gamma1"].unsqueeze(1)).then_inc(weights, 16)
                    sp.dma_start(beta[r, :], d["beta1"].unsqueeze(1)).then_inc(weights, 16)
                for tile, name in ((center, "center"), (mean, "mean"), (eye, "eye"), (b1, "b1"), (T2, "W2")):
                    sp.dma_start(tile[:], d[name]).then_inc(weights, 16)
                with sp.Fori(0, loops) as i:
                    for k in range(2):
                        sp.wait_ge(summed[k], at(i - 1))
                        sp.dma_start(xs[k][:], X[:, bass.ds(2 * i + k, 1), :].rearrange("p a n -> p (a n)"))\
                          .then_inc(x_in[k], 16)
                    for k in range(2):
                        sp.wait_ge(copied[k], at(i))
                        sp.dma_start(out_v[:, bass.ds(4 * i + 2 * k, 2), :],
                                     OT[k][:].rearrange("p q t f -> p q (t f)")).then_inc(stored[k], 16)
                for k in range(2):
                    sp.wait_ge(stored[k], at(loops - 1, 16))

            @block.gpsimd
            def _(pool):
                for k in range(2):
                    lead(pool, [gathered[k]])
                pool.wait_ge(weights, WEIGHTS)
                with pool.Fori(0, loops) as i:
                    for k in range(2):
                        pool.wait_ge(lowered[k], at(i - 1))
                        for q in range(2):
                            for r in range(TOP):
                                j = 2 * q + r
                                e = pool.value_load(R.expert[0:1, j, bass.ds(2 * i + k, 1)], min_val=0, max_val=E - 1)
                                pool.tensor_copy(C1[k][:, j, :], T1[:, bass.ds(e, 1), :].rearrange("p a f -> p (a f)"))
                                pool.tensor_copy(cb1[k][:, q, r:r + 1], b1[:, bass.ds(e, 1)])
                                ins = pool.tensor_tensor(C2[k][:, q, r, :],
                                                         T2[:, bass.ds(e, 1), :].rearrange("p a f -> p (a f)"),
                                                         R.weight[:, j, bass.ds(2 * i + k, 1)].broadcast_to([FF, F]),
                                                         ALU.mult)
                        ins.then_inc(gathered[k], 1)

            @block.tensor
            def _(pe):
                for k in range(2):
                    lead(pe, [lifted[k]], 4)
                    lead(pe, [lowered[k], centered[k], varied[k], turned[k]])
                pe.wait_ge(weights, WEIGHTS)
                with pe.Fori(0, loops) as i:
                    for k in range(2):
                        pe.wait_ge(gathered[k], at(i))
                        pe.wait_ge(x_in[k], i * 16 + (16 + 16 * LEAD))
                        pe.wait_ge(copied[k], at(i - 1))
                    for q in range(2):
                        for k in range(2):
                            for r in range(TOP):
                                j = 2 * q + r
                                if q == 1:
                                    pe.wait_ge(gelued[k], 4 * i + (j - 1) + 4 * LEAD)
                                for hf in range(2):
                                    mm = pe.matmul(slots[2 * k + r][:, hf, 0:HALF], C1[k][F * q:F * q + F, j, :],
                                                   xs[k][F * q:F * q + F, hf * HALF:(hf + 1) * HALF],
                                                   start=True, stop=True)
                                mm.then_inc(lifted[k], 1)
                    for k in range(2):
                        pe.wait_ge(gelued[k], 4 * i + 4 + 4 * LEAD)
                        for hf in range(2):
                            for r in range(TOP):
                                for q in range(2):
                                    mm = pe.matmul(slots[2 * k][F * q:F * q + F, hf, 0:HALF], C2[k][:, q, r, :],
                                                   G[k][q][r][:, hf * HALF:(hf + 1) * HALF],
                                                   start=(r == 0), stop=(r == TOP - 1))
                        mm.then_inc(lowered[k], 1)
                    for k in range(2):
                        pe.wait_ge(summed[k], at(i))
                        for hf in range(2):
                            mm = pe.matmul(slots[2 * k + 1][:, hf, 0:HALF], center[:], z[k][:, hf * HALF:(hf + 1) * HALF],
                                           start=True, stop=True)
                        mm.then_inc(centered[k], 1)
                    for k in range(2):
                        pe.wait_ge(squared[k], at(i))
                        for hf in range(2):
                            mm = pe.matmul(slots[2 * k][:, hf, 0:HALF], mean[:], t0[k][:, hf * HALF:(hf + 1) * HALF],
                                           start=True, stop=True)
                        mm.then_inc(varied[k], 1)
                    for k in range(2):
                        pe.wait_ge(shifted[k], at(i))
                        for t in range(NT):
                            mm = pe.transpose(flat(slots[2 * k])[0:TP, t * P:(t + 1) * P],
                                              z[k][:, t:t + NT * (TP - 1) + 1:NT], eye[:])
                        mm.then_inc(turned[k], 1)

            @block.scalar
            def _(act):
                for k in range(2):
                    lead(act, [gelued[k]], 4)
                    lead(act, [squared[k], logged[k], rooted[k], copied[k]])
                act.wait_ge(ready, 1)
                with act.Fori(0, loops) as i:
                    for q in range(2):
                        for k in range(2):
                            for r in range(TOP):
                                j = 2 * q + r
                                act.wait_ge(lifted[k], 4 * i + (j + 1) + 4 * LEAD)
                                act.activation(halves(G[k][q][r][:]), wide(slots[2 * k + r]), ACT.Gelu,
                                               bias=cb1[k][:, q, r:r + 1]).then_inc(gelued[k], 1)
                    for k in range(2):
                        act.wait_ge(centered[k], at(i))
                        act.activation(halves(t0[k][:]), wide(slots[2 * k + 1]), ACT.Square).then_inc(squared[k], 1)
                    for k in range(2):
                        act.wait_ge(varied[k], at(i))
                        act.activation(halves(r1[k][:]), wide(slots[2 * k]), ACT.Ln, bias=eps[:, 0:1])\
                           .then_inc(logged[k], 1)
                    for k in range(2):
                        act.wait_ge(logged[k], at(i))
                        act.activation(t0[k][:], r1[k][:], ACT.Exp, scale=-0.5).then_inc(rooted[k], 1)
                    for k in range(2):
                        act.wait_ge(turned[k], at(i))
                        act.wait_ge(stored[k], i * 16 + 16 * LEAD)
                        act.activation(OT[k][:].rearrange("p q t f -> p t q f"),
                                       flat(slots[2 * k])[0:TP, 0:NT * P].rearrange("p (t q f) -> p t q f", t=NT, q=2),
                                       ACT.Copy).then_inc(copied[k], 1)

            @block.vector
            def _(v):
                for k in range(2):
                    lead(v, [summed[k], normed[k], scaled[k], shifted[k]])
                v.memset(eps[:], EPS).then_inc(ready, 1)
                v.wait_ge(weights, WEIGHTS)
                with v.Fori(0, loops) as i:
                    for k in range(2):
                        v.wait_ge(lowered[k], at(i))
                        v.scalar_tensor_tensor(halves(z[k][:]), wide(slots[2 * k]), R.b2[:, bass.ds(2 * i + k, 1)],
                                               halves(xs[k][:]), ALU.add, ALU.add).then_inc(summed[k], 1)
                    for k in range(2):
                        v.wait_ge(rooted[k], at(i))
                        v.tensor_tensor(halves(r1[k][:]), wide(slots[2 * k + 1]), halves(t0[k][:]), ALU.mult)\
                         .then_inc(normed[k], 1)
                    for k in range(2):
                        v.wait_ge(normed[k], at(i))
                        v.scalar_tensor_tensor(r1[k][:], r1[k][:], gamma[:, 0:1],
                                               H[:, bass.ds(2 * i + k + 1, 1), :].rearrange("p a n -> p (a n)"),
                                               ALU.mult, ALU.add).then_inc(scaled[k], 1)
                    for k in range(2):
                        v.wait_ge(scaled[k], at(i))
                        v.tensor_scalar(z[k][:], r1[k][:], beta[:, 0:1], None, ALU.add).then_inc(shifted[k], 1)


def tower(nc, d, out):
    B = d["x"].shape[0]
    NP = B // 2
    with ExitStack() as st:
        core = Core(nc, st)
        slots = [core.ps(f"slot{i}", [P, 2, 512]) for i in range(4)]
        H = core.sb("H", [P, NP + 1, N])
        scratch = nc.dram_tensor("norms", (P, NP + 1, 2, N), F32, kind="Internal").ap()
        tokens(core, slots, d, H, scratch, NP)
        attention(core, slots, d, H, scratch, NP)
        routed_ffn(core, slots, d, H, NP)
        X = core.sb("X", [P, NP, N])
        sums = core.sb("X_sums", [P, NP])
        causal_attention(core, slots, d, H, X, sums, NP)
        R = Routes(core, NP)
        routing(core, slots, d, sums, R, NP)
        mixture(core, slots, d, H, X, R, out, NP)


def shape_constants(pairs, experts):
    pos = np.arange(N, dtype=np.float32)[:, None]
    step = np.arange(0, F, 2, dtype=np.float32) * np.float32(-np.log(10000.0) / F)
    angle = (pos * np.exp(step.astype(np.float64)).astype(np.float32)).astype(np.float64)
    pe = np.zeros((N, F), np.float32)
    pe[:, 0::2] = np.sin(angle)
    pe[:, 1::2] = np.cos(angle)
    img = np.arange(P) // F
    same = (img[:, None] == img[None, :]).astype(np.float32)
    eye = np.eye(P, dtype=np.float32)
    patch = np.arange(N, dtype=np.float32)
    return {
        "pos": np.concatenate([pe.T, pe.T]).copy(),
        "iota": np.tile(patch, (TP, 1)),
        "center": eye - same / F,
        "mean": same / F,
        "eye": eye,
        "causal": np.triu(np.ones((TP, TP), np.float32)),
        "experts": np.tile(np.arange(experts, dtype=np.float32), (pairs, 1)),
        "per_row": np.tile(1.0 / np.maximum(patch, 1.0), (P, 1)).astype(np.float32),
    }


def laid_out(inputs):
    a = {k: np.asarray(v) for k, v in inputs.items()}
    B = a["x"].shape[0]
    edges = a["L0_tok_edge_index"].astype(np.int32)
    E = edges.shape[1]
    KE = -(-E // TP)
    rows = np.full((2, KE * TP), -1, np.int32)
    rows[:, :E] = edges
    own = np.tile(np.arange(N, dtype=np.int32), (2, 1))
    t = lambda x, *axes: np.ascontiguousarray(np.transpose(x, axes or None))
    d = {
        "x": a["x"],
        "edges": t(np.concatenate([rows, own], 1).reshape(2, KE + NT, TP), 2, 0, 1),
        "W_embed": a["L0_tok_W_embed"], "b_embed": a["L0_tok_b_embed"],
        "W_gcn": a["L0_tok_W_gcn"], "b_gcn": t(a["L0_tok_b_gcn"]),
        "W_out": a["L0_tok_W_out"], "b_out": a["L0_tok_b_out"],
        "gamma0": a["L0_attn_ln_gamma"], "beta0": a["L0_attn_ln_beta"],
        "W_qkv_t": t(a["L0_attn_W_qkv"]), "W_gate_t": t(a["L0_attn_W_gate"]),
        "b_gate": a["L0_attn_b_gate"], "W_final_t": t(a["L0_attn_W_final"]), "b_final": a["L0_attn_b_final"],
        "route": a["L0_ffn_route_id"].astype(np.int32).reshape(1, -1),
        "Wi_t": t(a["L0_ffn_Wi"]), "bi": a["L0_ffn_bi"],
        "Wr_t": t(a["L0_ffn_Wr"], 3, 1, 0, 2), "br_t": t(a["L0_ffn_br"], 2, 1, 0),
        "Ws": t(a["L0_ffn_Ws"][:, 0], 2, 0, 1), "bs": t(a["L0_ffn_bs"][:, 0]),
        "Wo_t": t(a["L0_ffn_Wo"]), "bo": a["L0_ffn_bo"],
        "Wq": a["L1_attn_Wq"], "Wk": a["L1_attn_Wk"], "Wv": a["L1_attn_Wv"], "Wo1_t": t(a["L1_attn_Wo"]),
        "Wr1": a["L1_ffn_Wr"], "br1": np.tile(a["L1_ffn_br"], (B // 2, 1)),
        "W1": t(a["L1_ffn_W1"], 1, 0, 2), "b1": t(a["L1_ffn_b1"]),
        "W2": t(a["L1_ffn_W2"], 1, 0, 2), "b2": a["L1_ffn_b2"],
        "gamma1": a["L1_ffn_gamma"], "beta1": a["L1_ffn_beta"],
    }
    return {**d, **shape_constants(B // 2, a["L1_ffn_br"].size)}


def kernel(**inputs):
    import concourse.bacc as _bacc
    from concourse import mybir as _mybir
    from concourse.bass_utils import run_bass_kernel_spmd as _run

    nc = _bacc.Bacc("TRN2", target_bir_lowering=False, num_devices=1)
    data = laid_out(inputs)
    B = data["x"].shape[0]
    d = {n: nc.dram_tensor(f"in_{n}", a.shape, _mybir.dt.from_np(a.dtype), kind="ExternalInput").ap()
         for n, a in data.items()}
    out = nc.dram_tensor("tokens_out", (B, N, F), F32, kind="ExternalOutput").ap()
    tower(nc, d, out)
    r = _run(nc, [{f"in_{n}": a for n, a in data.items()}], core_ids=[0])
    return r.results[0]["tokens_out"]
```

```python
from contextlib import ExitStack

import numpy as np

import concourse.bass as bass
from concourse import mybir

ALU = mybir.AluOpType
ACT = mybir.ActivationFunctionType
AX = mybir.AxisListType
F32 = mybir.dt.float32
F16 = mybir.dt.float16
BF16 = mybir.dt.bfloat16
I32 = mybir.dt.int32
U32 = mybir.dt.uint32

P = 128
GRID, PATCH, CH, IMG = 28, 8, 3, 224
N = GRID * GRID
HALF = N // 2
TP = 112
NT = N // TP
F = 64
EPS = 1e-5
LEAD = 2


def at(n, step=1):
    return (n + 1 + LEAD) * step


class Core:

    def __init__(self, nc, stack):
        self.nc, self.stack, self.sems = nc, stack, []
        stack.callback(self.free_semaphores)

    def free_semaphores(self):
        if self.sems:
            self.nc.clear_and_free_semaphores(self.sems)
            self.nc.all_engine_barrier()

    def sb(self, name, shape, dt=F32):
        return self.stack.enter_context(self.nc.sbuf_tensor(name, shape, dt))

    def ps(self, name, shape):
        return self.stack.enter_context(self.nc.psum_tensor(name, shape, F32))

    def sem(self, name):
        self.sems.append(self.nc.alloc_semaphore(name))
        return self.sems[-1]


def wide(slot):
    return slot[:, :, 0:HALF]


def halves(tile):
    return tile.rearrange("p (h n) -> p h n", h=2)


def flat(slot):
    return slot.rearrange("p h n -> p (h n)")


def lead(eng, sems, step=1):
    for s in sems:
        eng.sem_inc(s, LEAD * step)


def staggered(steps, first=False, last=False):
    half = len(steps) // 2
    for n, step in enumerate(steps):
        m = (n + half) % len(steps)
        if not last:
            yield step, 0, 0
        if m >= half if last else (m < half or not first):
            yield steps[m], 1, int(m >= half)


def run_staggered(eng, loops, steps, part):
    for step, k, _ in staggered(steps, first=True):
        part(step, k, 0)
    with eng.Fori(1, loops) as i:
        for step, k, back in staggered(steps):
            part(step, k, i - back if back else i)
    for step, k, _ in staggered(steps, last=True):
        part(step, k, loops - 1)


SPAN = TP + 2 * GRID
CHUNK = 8
FAR = 512 + HALF


def band(t):
    lo, hi = max(0, t * TP - GRID), min(N, (t + 1) * TP + GRID)
    cuts = [(b, max(lo, b * HALF), min(hi, (b + 1) * HALF)) for b in range(2)]
    return [(a - lo, b, a - b * HALF, e - b * HALF) for b, a, e in cuts if a < e]


def build_graph(core, slots, d, near, far, turns):
    nc = core.nc
    KE = d["edges"].shape[2]
    with ExitStack() as st:
        c = Core(nc, st)
        most, turns_f = c.sb("ge_most", [TP, 1]), c.sb("ge_turns_f", [1, 2])
        ei = c.sb("ge_idx", [TP, 2, KE], I32)
        ef = c.sb("ge_idx_f", [TP, 2, KE])
        iota = c.sb("ge_iota", [TP, N])
        onesrc = c.sb("ge_onehot_src", [TP, KE, N], BF16)
        onedst = c.sb("ge_onehot_dst", [TP, KE, N], BF16)
        ones = c.sb("ge_ones", [TP, TP])
        rd = c.sb("ge_rdeg", [TP, N])
        rs = c.sb("ge_rdeg_src", [TP, 8])
        sd = c.sb("ge_sqrt", [TP, N])
        eye, diagonal = c.sb("ge_eye", [TP, TP]), c.sb("ge_diagonal", [TP, TP])
        loaded, ready, hot = c.sem("ge_loaded"), c.sem("ge_ready"), c.sem("ge_hot")
        counted, kept, degs = c.sem("ge_counted"), c.sem("ge_kept"), c.sem("ge_degs")
        rooted, inverted, scaled = c.sem("ge_rooted"), c.sem("ge_inverted"), c.sem("ge_scaled")
        placed, checked = c.sem("ge_placed"), c.sem("ge_checked")
        with nc.Block() as block:

            @block.gpsimd
            def _(pool):
                pool.memset(far[:], 0.0).then_inc(placed, 1)

            @block.sync
            def _(sp):
                sp.dma_start(ei[:], d["edges"]).then_inc(loaded, 16)
                sp.dma_start(iota[:], d["iota"]).then_inc(loaded, 16)
                sp.dma_start(eye[:], d["eye"][0:TP, 0:TP]).then_inc(loaded, 16)

            @block.vector
            def _(v):
                v.memset(ones[:], 1.0).then_inc(ready, 1)
                v.wait_ge(loaded, 16 * 3)
                v.tensor_copy(ef[:], ei[:]).then_inc(ready, 1)
                v.wait_ge(ready, 2)
                for k in range(KE):
                    v.tensor_scalar(onesrc[:, k, :], iota[:], ef[:, 0, k:k + 1], None, ALU.is_equal)
                    v.tensor_scalar(onedst[:, k, :], iota[:], ef[:, 1, k:k + 1], None,
                                    ALU.is_equal).then_inc(hot, 1)
                v.wait_ge(placed, 1)
                for t in range(NT):
                    v.wait_ge(counted, t + 1)
                    v.tensor_copy(far[:, t, :, 0:HALF], wide(slots[t % 2])[0:TP]).then_inc(kept, 1)
                v.wait_ge(rooted, 1)
                v.reciprocal(rd[:], sd[:]).then_inc(inverted, 1)
                v.wait_ge(inverted, 1)
                for t in range(NT):
                    if t > 0:
                        v.wait_ge(inverted, t + 1)
                    v.scalar_tensor_tensor(diagonal[:], rd[:, t * TP:(t + 1) * TP], 1.0, eye[:], ALU.mult, ALU.mult,
                                           accum_out=rs[:, t:t + 1]).then_inc(inverted, 1)
                v.wait_ge(inverted, NT + 1)
                for t in range(NT):
                    v.scalar_tensor_tensor(far[:, t, :, 0:HALF], far[:, t, :, 0:HALF], rs[:, t:t + 1],
                                           halves(rd[:]), ALU.mult, ALU.mult).then_inc(scaled, 1)
                v.wait_ge(scaled, NT)
                n = 1
                for t in range(NT):
                    for first, b, lo, hi in band(t):
                        v.tensor_copy(near[:, t, first:first + hi - lo], far[:, t, b, lo:hi]).then_inc(placed, 1)
                        n += 1
                v.wait_ge(placed, n)
                for t in range(NT):
                    for first, b, lo, hi in band(t):
                        v.memset(far[:, t, b, lo:hi], 0.0).then_inc(placed, 1)
                        n += 1
                v.wait_ge(placed, n)
                v.tensor_reduce(most[:], far[:].rearrange("p t h n -> p t (h n)"), AX.XY, ALU.max).then_inc(checked, 1)
                v.wait_ge(checked, 2)
                v.tensor_scalar(turns_f[:, 0:1], slots[0][0:1, 0, 0:1], 0.0, float(FAR // CHUNK - 1),
                                ALU.is_gt, ALU.mult).then_inc(checked, 1)
                v.wait_ge(checked, 3)
                v.tensor_scalar(turns[:], turns_f[:, 0:1], 1.0, None, ALU.add).then_inc(checked, 1)
                v.wait_ge(checked, 4)

            @block.tensor
            def _(pe):
                for t in range(NT):
                    if t >= 2:
                        pe.wait_ge(kept, t - 1)
                    for k in range(KE):
                        if t == 0:
                            pe.wait_ge(hot, k + 1)
                        for h in range(2):
                            mm = pe.matmul(slots[t % 2][0:TP, h, 0:HALF], onesrc[:, k, t * TP:(t + 1) * TP],
                                           onedst[:, k, h * HALF:(h + 1) * HALF],
                                           start=(k == 0), stop=(k == KE - 1))
                    mm.then_inc(counted, 1)
                pe.wait_ge(kept, NT)
                for h in range(2):
                    for t in range(NT):
                        mm = pe.matmul(slots[2][0:TP, h, 0:HALF], ones[:], far[:, t, h, 0:HALF],
                                       start=(t == 0), stop=(t == NT - 1))
                mm.then_inc(degs, 1)
                pe.wait_ge(checked, 1)
                pe.matmul(slots[0][0:1, 0, 0:1], most[:], ones[:, 0:1], start=True, stop=True).then_inc(checked, 1)

            @block.scalar
            def _(act):
                act.wait_ge(degs, 1)
                act.activation(halves(sd[:]), wide(slots[2])[0:TP], ACT.Sqrt).then_inc(rooted, 1)
                act.wait_ge(scaled, NT)


def tokens(core, slots, d, H, scratch, NP):
    nc = core.nc
    KR = 2 * CH * PATCH
    with ExitStack() as st:
        c = Core(nc, st)
        near, far = c.sb("tk_near", [TP, NT, SPAN]), c.sb("tk_far", [TP, NT, 2, 512])
        turns = c.sb("tk_turns", [1, 1], I32)
        nothing = c.sb("tk_nothing", [1, HALF], BF16)
        build_graph(core, slots, d, near, far, turns)
        X = [c.sb(f"tk_x{i}", [TP, GRID, IMG]) for i in range(2)]
        We = c.sb("tk_we", [TP, PATCH // 2, P])
        Wg = c.sb("tk_wg", [P, 3, P])
        Wo = c.sb("tk_wo", [P, P])
        be, bg, bo = c.sb("tk_be", [P, 1]), c.sb("tk_bg", [P, 3]), c.sb("tk_bo", [P, 1])
        pos = c.sb("tk_pos", [P, N])
        center, mean, eps = c.sb("tk_center", [P, P]), c.sb("tk_mean", [P, P]), c.sb("tk_eps", [P, 1])
        gamma, beta = c.sb("tk_gamma", [P, 1]), c.sb("tk_beta", [P, 1])
        t0, r1 = ([c.sb(f"tk_{name}{i}", [P, N]) for i in range(2)] for name in ("t", "r"))
        both = [c.sb(f"tk_norms{i}", [P, 2, N]) for i in range(2)]
        xn, x1 = ([both[i][:, j, :] for i in range(2)] for j in range(2))
        h = [c.sb(f"tk_h{i}", [P, N]) for i in range(2)]
        hw = [c.sb(f"tk_hw{i}", [TP, NT, P]) for i in range(2)]
        cleared, weights = c.sem("tk_cleared"), c.sem("tk_weights")
        x_in = [c.sem(f"tk_x_in{i}") for i in range(2)]
        embedded = [c.sem(f"tk_embedded{i}") for i in range(2)]
        h_ready = [[c.sem(f"tk_h_ready{i}_{l}") for l in range(5)] for i in range(2)]
        projected = [[c.sem(f"tk_projected{i}_{l}") for l in range(3)] for i in range(2)]
        hw_ready = [[c.sem(f"tk_hw_ready{i}_{l}") for l in range(3)] for i in range(2)]
        spread = [[c.sem(f"tk_spread{i}_{l}") for l in range(3)] for i in range(2)]
        out_ready = [c.sem(f"tk_out_ready{i}") for i in range(2)]
        sems = lambda name: [c.sem(f"tk_{name}{i}") for i in range(2)]
        centered, squared, varied, logged, inverse, rooted = map(
            sems, ("centered", "squared", "varied", "logged", "inverse", "rooted"))
        normed, unit_var, logged2, rooted2, normed2, scaled = map(
            sems, ("normed", "unit_var", "logged2_", "rooted2_", "normed2_", "scaled"))
        kept, stored = sems("kept"), sems("stored")
        loops = NP // 2
        with nc.Block() as block:

            @block.gpsimd
            def _(pool):
                pool.memset(X[0][:], 0.0).then_inc(cleared, 1)

            @block.sync
            def _(sp):
                lead(sp, x_in, 32)
                for q in range(2):
                    o = F * q
                    sp.dma_start(bg[o:o + F, :], d["b_gcn"]).then_inc(weights, 16)
                    for tile, name in ((be, "b_embed"), (bo, "b_out"), (gamma, "gamma0"), (beta, "beta0")):
                        sp.dma_start(tile[o:o + F, :], d[name].unsqueeze(1)).then_inc(weights, 16)
                for tile, name in ((pos, "pos"), (center, "center"), (mean, "mean")):
                    sp.dma_start(tile[:], d[name]).then_inc(weights, 16)
                sp.wait_ge(cleared, 5)
                wv = d["W_embed"].rearrange("(r s x) f -> r s x f", s=2, x=PATCH // 2)
                for q in range(2):
                    for s in range(2):
                        sp.dma_start(We[64 * s + 24 * q:64 * s + 24 * q + 24, :, F * q:F * q + F],
                                     wv[:, s]).then_inc(weights, 16)
                    o = F * q
                    sp.dma_start(Wg[o:o + F, :, o:o + F], d["W_gcn"].rearrange("l i o -> i l o")).then_inc(weights, 16)
                    sp.dma_start(Wo[o:o + F, o:o + F], d["W_out"]).then_inc(weights, 16)
                xv = d["x"].rearrange("b c (i y) w -> (b c) y i w", y=PATCH)

                def load(q, pair):
                    for s in range(2):
                        w = IMG - 4 * s
                        for r in range(2 * CH):
                            p0 = 64 * s + PATCH * r
                            sp.dma_start(X[q][p0:p0 + PATCH, :, 0:w],
                                         xv[bass.ds(pair * 2 * CH + r, 1), :, :, 4 * s:IMG]
                                         .rearrange("a y i w -> (a y) i w")).then_inc(x_in[q], 16)

                def store(q, pair):
                    sp.dma_start(scratch[:, pair].rearrange("p a j n -> p (a j) n"), both[q][:]).then_inc(stored[q], 16)

                for q in range(2):
                    lead(sp, [stored[q]], 16)
                    load(q, q)
                with sp.Fori(0, loops - 1) as i:
                    for q in range(2):
                        sp.wait_ge(embedded[q], at(i))
                        load(q, 2 * i + (q + 2))
                    for q in range(2):
                        sp.wait_ge(scaled[q], at(i))
                        store(q, bass.ds(2 * i + q, 1))
                for q in range(2):
                    sp.wait_ge(scaled[q], at(loops - 1))
                    store(q, slice(NP - 2 + q, NP - 1 + q))
                store(1, slice(NP, NP + 1))
                sp.wait_ge(stored[0], at(loops - 1, 16))
                sp.wait_ge(stored[1], at(loops, 16))

            XIN = 4 * CH * 16
            WEIGHTS = 16 * (2 * 9 + 3 + 2)

            @block.tensor
            def _(pe):
                for q in range(2):
                    lead(pe, [embedded[q], out_ready[q], centered[q], varied[q]] + projected[q] + spread[q])
                pe.wait_ge(weights, WEIGHTS)
                n_far = pe.value_load(turns[:], min_val=1, max_val=FAR // CHUNK)
                with pe.Fori(0, loops) as i:
                    for q in range(2):
                        pe.wait_ge(x_in[q], i * XIN + (XIN + 32 * LEAD))
                        pe.wait_ge(normed[q], at(i - 1))
                        for hf in range(2):
                            for x in range(PATCH // 2):
                                px = X[q][:, 14 * hf:14 * hf + 14, x:x + 8 * (GRID - 1) + 1:8]
                                mm = pe.matmul(slots[2 * q][:, hf, 0:HALF], We[:, x, :], px,
                                               start=(x == 0), stop=(x == 3))
                        mm.then_inc(embedded[q], 1)
                    for l in range(3):
                        for q in range(2):
                            pe.wait_ge(h_ready[q][l], at(i))
                            if l == 0:
                                pe.wait_ge(unit_var[q], at(i - 1))
                            for t in range(NT):
                                mm = pe.matmul(flat(slots[2 * q + 1])[0:TP, t * P:(t + 1) * P],
                                               h[q][:, t * TP:(t + 1) * TP], Wg[:, l, :], start=True, stop=True)
                            mm.then_inc(projected[q][l], 1)
                        for q in range(2):
                            pe.wait_ge(hw_ready[q][l], at(i))
                            def add(piece, start, stop):
                                t, first, b, lo, hi = piece
                                return pe.matmul(slots[2 * q][:, b, lo:hi], hw[q][:, t, :],
                                                 near[:, t, first:first + hi - lo], start=start, stop=stop)

                            pieces = [(t, *piece) for t in range(NT) for piece in band(t)]
                            ends = [[p for p in pieces if p[2] == b][-1] for b in range(2)]
                            for b in range(2):
                                pe.matmul(slots[2 * q][:, b, 0:HALF], nothing[:, 0:P], nothing[:, 0:HALF],
                                          start=True, stop=False)
                            for p in pieces:
                                if p not in ends:
                                    add(p, False, False)
                            with pe.Fori(0, n_far) as k:
                                for t in range(NT):
                                    pe.matmul(flat(slots[2 * q])[:, bass.ds(k * CHUNK, CHUNK)], hw[q][:, t, :],
                                              far[:, t].rearrange("p h n -> p (h n)")[:, bass.ds(k * CHUNK, CHUNK)],
                                              start=False, stop=False)
                            for p in ends:
                                mm = add(p, False, True)
                            mm.then_inc(spread[q][l], 1)
                    for q in range(2):
                        pe.wait_ge(h_ready[q][3], at(i))
                        for hf in range(2):
                            mm = pe.matmul(slots[2 * q + 1][:, hf, 0:HALF], Wo[:], h[q][:, hf * HALF:(hf + 1) * HALF],
                                           start=True, stop=True)
                        mm.then_inc(out_ready[q], 1)
                    for q in range(2):
                        pe.wait_ge(h_ready[q][4], at(i))
                        for hf in range(2):
                            mm = pe.matmul(slots[2 * q][:, hf, 0:HALF], center[:], h[q][:, hf * HALF:(hf + 1) * HALF],
                                           start=True, stop=True)
                        mm.then_inc(centered[q], 1)
                    for q in range(2):
                        pe.wait_ge(squared[q], at(i))
                        for hf in range(2):
                            mm = pe.matmul(slots[2 * q + 1][:, hf, 0:HALF], mean[:], t0[q][:, hf * HALF:(hf + 1) * HALF],
                                           start=True, stop=True)
                        mm.then_inc(varied[q], 1)

            @block.scalar
            def _(act):
                for q in range(2):
                    lead(act, hw_ready[q] + [squared[q], logged[q], inverse[q], rooted[q], logged2[q], rooted2[q]])
                with act.Fori(0, loops) as i:
                    for l in range(3):
                        for q in range(2):
                            act.wait_ge(projected[q][l], at(i))
                            act.activation(hw[q][:].rearrange("p t f -> p (t f)"),
                                           flat(slots[2 * q + 1])[0:TP, 0:NT * P], ACT.Copy)\
                               .then_inc(hw_ready[q][l], 1)
                    for q in range(2):
                        act.wait_ge(centered[q], at(i))
                        act.activation(halves(t0[q][:]), wide(slots[2 * q]), ACT.Square).then_inc(squared[q], 1)
                    for q in range(2):
                        act.wait_ge(varied[q], at(i))
                        act.wait_ge(stored[q], at(i - 1, 16))
                        act.activation(halves(xn[q]), wide(slots[2 * q + 1]), ACT.Ln, bias=eps[:, 0:1])\
                           .then_inc(logged[q], 1)
                    for q in range(2):
                        act.wait_ge(logged[q], at(i))
                        act.activation(r1[q][:], xn[q], ACT.Exp, scale=-0.5).then_inc(rooted[q], 1)
                        act.activation(t0[q][:], xn[q], ACT.Exp, scale=-1.0).then_inc(inverse[q], 1)
                    for q in range(2):
                        act.wait_ge(unit_var[q], at(i))
                        act.activation(r1[q][:], t0[q][:], ACT.Ln, bias=eps[:, 0:1]).then_inc(logged2[q], 1)
                    for q in range(2):
                        act.wait_ge(logged2[q], at(i))
                        act.activation(t0[q][:], r1[q][:], ACT.Exp, scale=-0.5).then_inc(rooted2[q], 1)

            @block.vector
            def _(v):
                for q in range(2):
                    lead(v, h_ready[q] + [normed[q], unit_var[q], normed2[q], scaled[q], kept[q]])
                for w in (We, Wg, Wo, X[1]):
                    v.memset(w[:], 0.0).then_inc(cleared, 1)
                v.memset(eps[:], EPS).then_inc(weights, 16)
                v.memset(nothing[:], 0.0).then_inc(weights, 16)
                v.wait_ge(weights, WEIGHTS)
                with v.Fori(0, loops) as i:
                    for q in range(2):
                        v.wait_ge(embedded[q], at(i))
                        v.wait_ge(kept[q], at(i - 1))
                        v.scalar_tensor_tensor(halves(h[q][:]), wide(slots[2 * q]), be[:, 0:1], halves(pos[:]),
                                               ALU.add, ALU.add).then_inc(h_ready[q][0], 1)
                    for l in range(3):
                        for q in range(2):
                            v.wait_ge(spread[q][l], at(i))
                            v.tensor_scalar(halves(h[q][:]), wide(slots[2 * q]), bg[:, l:l + 1], 0.0,
                                            ALU.add, ALU.max).then_inc(h_ready[q][l + 1], 1)
                    for q in range(2):
                        v.wait_ge(out_ready[q], at(i))
                        v.tensor_scalar(halves(h[q][:]), wide(slots[2 * q + 1]), bo[:, 0:1], None, ALU.add)\
                         .then_inc(h_ready[q][4], 1)
                    for q in range(2):
                        v.wait_ge(rooted[q], at(i))
                        v.tensor_tensor(halves(x1[q]), wide(slots[2 * q]), halves(r1[q][:]), ALU.mult)\
                         .then_inc(normed[q], 1)
                        v.wait_ge(inverse[q], at(i))
                        v.tensor_tensor(halves(t0[q][:]), wide(slots[2 * q + 1]), halves(t0[q][:]), ALU.mult)\
                         .then_inc(unit_var[q], 1)
                    for q in range(2):
                        v.wait_ge(normed[q], at(i))
                        v.tensor_tensor(H[:, bass.ds(2 * i + q + 1, 1), :].rearrange("p a n -> p (a n)"),
                                        h[q][:], x1[q], ALU.add).then_inc(kept[q], 1)
                    for q in range(2):
                        v.wait_ge(rooted2[q], at(i))
                        v.tensor_tensor(xn[q], x1[q], t0[q][:], ALU.mult).then_inc(normed2[q], 1)
                    for q in range(2):
                        v.wait_ge(normed2[q], at(i))
                        v.tensor_scalar(xn[q], xn[q], gamma[:, 0:1], beta[:, 0:1], ALU.mult, ALU.add)\
                         .then_inc(scaled[q], 1)


HEADS, HD = 8, 32
GROUPS, HG = 2, 4
RING = 3
ERING, VRING = 4, 2
LAG = 2
FINAL = ((LAG + 1, 2), (LAG + 2, 2))
V_TILES = (range(0, 4), range(4, 7))
UNITS = [(q, g) for q in range(2) for g in range(GROUPS)]

LAST_READER = {"q": "act", "k": "act", "g": "act", "v": "act", "S": "act", "final": "dve"}


def prepare(q, g, pair):
    steps = [((0, 3), ("q", q, g, pair)), ((1, 3), ("k", q, g, pair)), ((3, 3), ("g", q, g, pair))]
    if g == 0:
        steps += [((4, 3), ("v", q, 0, pair)), ((5, 3), ("v", q, 1, pair))]
    return steps


def attention_order():
    order = []
    for u, (q, g) in enumerate(UNITS):
        nxt, npair = UNITS[(u + 1) % 4], int(u == 3)
        pq, pg, ppair = (*UNITS[u - 1], 0) if u else (*UNITS[3], -1)
        extra = prepare(*nxt, npair)
        for t in range(NT):
            late = (q, g, t - LAG, 0) if t >= LAG else (pq, pg, t - LAG + NT, ppair)
            for h in range(HG):
                order.append(("S", q, g, t, h))
                if h % 2:
                    order.append(("pv", *late, h // 2))
                if h == 1:
                    order.append(("inv", q, g, t - 1, 0) if t else ("inv", pq, pg, NT - 1, ppair))
                order += [s for when, s in extra if when == (t, h)]
                if pg == GROUPS - 1 and (t, h) in FINAL:
                    order.append(("final", pq, ppair, FINAL.index((t, h))))
            if t == LAG - 1:
                order.append(("gated", pq, pg, ppair))
        if u == 2:
            order.insert(order.index(("g", 1, 1, 0)) + 20, ("load",))
    return order


class Counts:

    def __init__(self, first, body, start=0, unit=1):
        self.first, self.body, self.start, self.unit = first, body, start, unit

    def ahead(self, step):
        return self.start + (self.first.index(step) + 1) * self.unit

    def turn(self, i, step):
        n = self.start + (len(self.first) + self.body.index(step) + 1) * self.unit
        return i * (len(self.body) * self.unit) + n

    def turn_before(self, i, step):
        n = self.start + (len(self.first) + self.body.index(step) + 1 - len(self.body)) * self.unit
        return i * (len(self.body) * self.unit) + n


def attention(core, slots, d, H, scratch, NP):
    nc = core.nc
    order = attention_order()
    first = [s for _, s in prepare(0, 0, 1)]
    is_job = lambda s: s[0] in LAST_READER
    jobs = [s for s in order if is_job(s)]
    by = {e: [s for s in jobs if LAST_READER[s[0]] == e] for e in ("act", "dve")}
    by_first = {e: [s for s in first if LAST_READER[s[0]] == e] for e in ("act", "dve")}
    assert len(jobs) % RING == 0
    n_filled = Counts(first, jobs)
    n_read = {e: Counts(by_first[e], by[e], start=RING) for e in by}
    qk = lambda steps: [s for s in steps if s[0] in ("q", "k")]
    n_split = Counts(qk(first), qk(order))
    gs = [s for s in order if s[0] == "gated"]
    n_gated = Counts([], gs, start=1)
    tiles = [s for s in order if s[0] == "S"]
    n_biased = Counts([], tiles)
    NM = len(tiles) // HG
    C = float(HD) ** -0.5
    ACC = slots[3]

    def slot_of(s, ahead=False):
        return slots[(first.index(s) if ahead else len(first) + jobs.index(s)) % RING]

    def group(q, g, t):
        return UNITS.index((q, g)) * NT + t

    with ExitStack() as st:
        c = Core(nc, st)
        W = c.sb("at_w", [P, 4 * HEADS * HD])
        Wf = c.sb("at_wf", [P, GROUPS, F])
        bg, bf = c.sb("at_bg", [P, GROUPS]), c.sb("at_bf", [P, 1])
        norms = c.sb("at_norms", [P, 2, N])
        xn, x1 = norms[:, 0, :], norms[:, 1, :]
        split = [[c.sb(f"at_split{w}{g}", [P, 2, N], F16) for g in range(GROUPS)] for w in range(2)]
        raw = [c.sb(f"at_raw{w}", [P, N]) for w in range(2)]
        one = c.sb("at_one", [P, 1])
        stack = [[c.sb(f"at_stack{w}{g}", [P, HG, N], F16) for g in range(GROUPS)] for w in range(2)]
        V = [c.sb(f"at_v{q}", [TP, NT, HEADS * HD]) for q in range(2)]
        gate = [c.sb(f"at_gate{g}", [P, N]) for g in range(GROUPS)]
        og = [c.sb(f"at_og{g}", [P, N]) for g in range(GROUPS)]
        E = c.sb("at_e", [TP, ERING, HG, N])
        vs = c.sb("at_vs", [TP, VRING, P])
        bias = c.sb("at_bias", [TP, 2 * HG])
        total = c.sb("at_total", [TP, 2, HG])
        inv = c.sb("at_inv", [TP, 2, HG])

        weights, prepared, loaded = c.sem("at_weights"), c.sem("at_prepared"), c.sem("at_loaded")
        filled = c.sem("at_filled")
        read = {"act": c.sem("at_act_read"), "dve": c.sem("at_dve_read")}
        high, low = c.sem("at_high"), c.sem("at_low")
        stacked = [c.sem(f"at_stacked{g}") for g in range(GROUPS)]
        biased, inverted, values = c.sem("at_biased"), c.sem("at_inverted"), c.sem("at_values")
        pv_done, gated = c.sem("at_pv_done"), c.sem("at_gated")
        VALUES, INVERTED = 4, 3
        STACKED = 2 * 4 * HG * 16

        def stacks(i, s, before=0):
            _, q, g, pair = s
            n = q + 2 * pair + 2 - before
            return i * (2 * STACKED) + n * STACKED

        with nc.Block() as block:

            @block.sync
            def _(sp):
                for g in range(GROUPS):
                    sp.sem_inc(stacked[g], STACKED)
                n = HEADS * HD
                for q in range(2):
                    r = slice(F * q, F * q + F)
                    sp.dma_start(W[r, 0:3 * n], d["W_qkv_t"]).then_inc(weights, 16)
                    sp.dma_start(W[r, 3 * n:4 * n], d["W_gate_t"]).then_inc(weights, 16)
                    sp.dma_start(bf[r, :], d["b_final"].unsqueeze(1)).then_inc(weights, 16)
                for g in range(GROUPS):
                    sp.dma_start(Wf[:, g, :], d["W_final_t"][g * P:(g + 1) * P]).then_inc(weights, 16)
                    sp.dma_start(bg[:, g:g + 1], d["b_gate"][g * P:(g + 1) * P].unsqueeze(1)).then_inc(weights, 16)

                def load(p):
                    sp.dma_start(norms[:], scratch[:, p].rearrange("p a j n -> p (a j) n")).then_inc(loaded, 16)

                def restack(kind, g):
                    w, parts = {"q": (0, (0, 0, 1, 1)), "k": (1, (0, 1, 0, 1))}[kind]
                    for h in range(HG):
                        for b, part in enumerate(parts):
                            sp.dma_start(stack[w][g][HD * b:HD * b + HD, h, :],
                                         split[w][g][HD * h:HD * h + HD, part, :]).then_inc(stacked[g], 16)

                load(slice(0, 1))
                for s in qk(first):
                    sp.wait_ge(low, n_split.ahead(s))
                    restack(s[0], s[2])
                with sp.Fori(0, NP) as i:
                    for s in order:
                        if s[0] in ("q", "k"):
                            sp.wait_ge(low, n_split.turn(i, s))
                            restack(s[0], s[2])
                        elif s[0] == "load":
                            sp.wait_ge(filled, n_filled.turn(i, ("g", 1, 1, 0)))
                            load(bass.ds(i + 1, 1))
                sp.wait_ge(loaded, 16 * (NP + 1))
                for g in range(GROUPS):
                    sp.wait_ge(stacked[g], (2 * NP + 2 - g) * STACKED)

            WEIGHTS = 16 * 10

            @block.tensor
            def _(pe):
                pe.sem_inc(pv_done, 2)
                pe.wait_ge(weights, WEIGHTS)
                pe.wait_ge(prepared, 10)

                def project(s, slot):
                    kind, q, g = s[0:3]
                    if kind == "v":
                        for k, t in enumerate(V_TILES[g]):
                            mm = pe.matmul(flat(slot)[0:TP, k * 256:(k + 1) * 256],
                                           xn[F * q:F * q + F, t * TP:(t + 1) * TP],
                                           W[F * q:F * q + F, 512:768], start=True, stop=True)
                    else:
                        col = {"q": 0, "k": 1, "g": 3}[kind] * HEADS * HD + g * P
                        src = x1 if kind == "g" else xn
                        for hf in range(2):
                            mm = pe.matmul(slot[:, hf, 0:HALF], W[F * q:F * q + F, col:col + P],
                                           src[F * q:F * q + F, hf * HALF:(hf + 1) * HALF], start=True, stop=True)
                    mm.then_inc(filled, 1)

                def attend(m, hf, t):
                    for h in range(HG):
                        mm = pe.matmul(ACC[HD * h:HD * h + HD, hf, 0:HALF], vs[:, m % VRING, HD * h:HD * h + HD],
                                       E[:, m % ERING, h, hf * HALF:(hf + 1) * HALF],
                                       start=(t == 0), stop=(t == NT - 1))
                    return mm

                def finish(q, hf, slot):
                    for g in range(GROUPS):
                        mm = pe.matmul(slot[F * q:F * q + F, hf, 0:HALF], Wf[:, g, :],
                                       og[g][:, hf * HALF:(hf + 1) * HALF],
                                       start=(g == 0), stop=(g == GROUPS - 1))
                    mm.then_inc(filled, 1)

                pe.wait_ge(loaded, 16)
                for n, s in enumerate(first):
                    if n >= RING:
                        old = first[n - RING]
                        e = LAST_READER[old[0]]
                        pe.wait_ge(read[e], n_read[e].ahead(old))
                    project(s, slot_of(s, ahead=True))
                for e in by:
                    pe.wait_ge(read[e], RING + len(by_first[e]))
                for hf in range(2):
                    attend(NM - LAG, hf, 0)
                with pe.Fori(0, NP) as i:
                    for s in order:
                        kind = s[0]
                        if is_job(s):
                            n = jobs.index(s)
                            old = jobs[n - RING]
                            e = LAST_READER[old[0]]
                            pe.wait_ge(read[e], n_read[e].turn(i, old) if n >= RING else n_read[e].turn_before(i, old))
                        if kind in ("q", "k", "g", "v"):
                            if s == ("q", 0, 0, 1):
                                pe.wait_ge(loaded, i * 16 + 32)
                            project(s, slot_of(s))
                        elif kind == "S":
                            _, q, g, t, h = s
                            if (t, h) == (0, 0):
                                pe.wait_ge(stacked[g], stacks(i, (0, q, g, 0)))
                            slot = slot_of(s)
                            for hf in range(2):
                                mm = pe.matmul(slot[0:TP, hf, 0:HALF], stack[0][g][:, h, t * TP:(t + 1) * TP],
                                               stack[1][g][:, h, hf * HALF:(hf + 1) * HALF], start=True, stop=True)
                            mm.then_inc(filled, 1)
                        elif kind == "pv":
                            _, q, g, t, pair, hf = s
                            m = group(q, g, t)
                            if hf == 0:
                                pe.wait_ge(values, i * NM + (m + NM * pair + VALUES))
                                if t == 0:
                                    u = UNITS.index((q, g))
                                    pe.wait_ge(gated, n_gated.turn(i, gs[u]))
                                attend(m, 0, t)
                            else:
                                attend(m, 1, t).then_inc(pv_done, 1)
                        elif kind == "final":
                            _, q, pair, hf = s
                            pe.wait_ge(gated, n_gated.turn(i, ("gated", q, 1, pair)))
                            finish(q, hf, slot_of(s))
                for t in range(NT - LAG, NT):
                    m = group(1, 1, t)
                    pe.wait_ge(values, (NP - 1) * NM + m + VALUES)
                    attend(m, 0, t)
                    attend(m, 1, t).then_inc(pv_done, 1)
                pe.wait_ge(gated, NP * 4 + 2)
                for e in by:
                    pe.wait_ge(read[e], RING + len(by_first[e]) + NP * len(by[e]))
                for hf in range(2):
                    finish(1, hf, slots[hf])

            @block.scalar
            def _(act):
                act.sem_inc(read["act"], RING)
                act.wait_ge(prepared, 10)

                def read_out(s, slot):
                    kind, q, g = s[0:3]
                    if kind in ("q", "k"):
                        w = 0 if kind == "q" else 1
                        act.activation(halves(raw[w][:]), wide(slot), ACT.Copy,
                                       scale=C if w == 0 else 1.0).then_inc(read["act"], 1)
                    elif kind == "g":
                        act.activation(halves(gate[g][:]), wide(slot), ACT.Tanh, bias=bg[:, g:g + 1],
                                       scale=0.5).then_inc(read["act"], 1)
                    else:
                        ts = V_TILES[g]
                        act.activation(V[q][:, ts[0]:ts[-1] + 1, :].rearrange("p t c -> p (t c)"),
                                       flat(slot)[0:TP, 0:len(ts) * 256], ACT.Copy).then_inc(read["act"], 1)

                for s in first:
                    act.wait_ge(filled, n_filled.ahead(s))
                    read_out(s, slot_of(s, ahead=True))
                with act.Fori(0, NP) as i:
                    for s in order:
                        kind = s[0]
                        if kind in ("q", "k", "g", "v"):
                            if kind in ("q", "k"):
                                act.wait_ge(low, n_split.turn(i, s) - 2)
                            if kind == "g":
                                u = UNITS.index(s[1:3]) + 4 * s[3]
                                act.wait_ge(gated, n_gated.turn(i, gs[u - 1]))
                            act.wait_ge(filled, n_filled.turn(i, s))
                            read_out(s, slot_of(s))
                        elif kind == "S":
                            _, q, g, t, h = s
                            n, m = tiles.index(s), group(q, g, t)
                            if h == 0:
                                act.wait_ge(pv_done, i * NM + m + 1)
                                act.wait_ge(inverted, i * NM + m + 1)
                            act.wait_ge(biased, n_biased.turn(i, s))
                            act.activation(halves(E[:, m % ERING, h, :]), wide(slot_of(s))[0:TP], ACT.Exp,
                                           bias=bias[:, n % 8:n % 8 + 1], scale=1.0,
                                           accum_out=total[:, m % 2, h:h + 1]).then_inc(read["act"], 1)

            @block.vector
            def _(v):
                v.sem_inc(read["dve"], RING)
                v.sem_inc(gated, 1)
                v.sem_inc(inverted, INVERTED - 2)
                for tile in (gate[1][:], og[0][:], E[:, NM % ERING - 2 + ERING:ERING], vs[:], H[:, 0, :],
                             V[1][:, NT - 1, :]):
                    v.memset(tile, 0.0).then_inc(prepared, 1)
                v.memset(one[:], 1.0).then_inc(prepared, 1)
                v.memset(total[:], 1.0).then_inc(prepared, 1)
                v.wait_ge(weights, WEIGHTS)
                v.tensor_scalar(bg[:], bg[:], 0.5, None, ALU.mult).then_inc(prepared, 1)
                v.tensor_scalar(Wf[:], Wf[:], 0.5, None, ALU.mult).then_inc(prepared, 1)
                v.wait_ge(prepared, 10)

                def invert(summed, used, m):
                    v.wait_ge(read["act"], summed)
                    v.wait_ge(values, used)
                    v.reciprocal(inv[:, m % 2, :], total[:, m % 2, :]).then_inc(inverted, 1)

                def apply_gate(g):
                    v.scalar_tensor_tensor(halves(og[g][:]), halves(gate[g][:]), 1.0, wide(ACC),
                                           ALU.add, ALU.mult).then_inc(gated, 1)

                def keep(q, hf, slot, p):
                    r = slice(F * q, F * q + F)
                    h = H[r, p, hf * HALF:(hf + 1) * HALF].rearrange("p a n -> p (a n)")
                    v.scalar_tensor_tensor(h, slot[r, hf, 0:HALF], bf[r, 0:1], h, ALU.add, ALU.add)\
                     .then_inc(read["dve"], 1)

                with v.Fori(0, NP) as i:
                    for s in order:
                        kind = s[0]
                        if kind == "S":
                            n = tiles.index(s)
                            v.wait_ge(filled, n_filled.turn(i, s))
                            v.tensor_reduce(bias[:, n % 8:n % 8 + 1], wide(slot_of(s))[0:TP], AX.XY, ALU.max, negate=True)\
                             .then_inc(biased, 1)
                        elif kind == "inv":
                            m, pair = group(*s[1:4]), s[4]
                            turn = n_read["act"].turn if pair == 0 else n_read["act"].turn_before
                            invert(turn(i, ("S",) + s[1:4] + (HG - 1,)), i * NM + (m + NM * pair + VALUES - 2), m)
                        elif kind == "gated":
                            _, q, g, pair = s
                            v.wait_ge(pv_done, i * NM + (group(q, g, NT - 1) + NM * pair + 5))
                            apply_gate(g)
                        elif kind == "final":
                            _, q, pair, hf = s
                            v.wait_ge(filled, n_filled.turn(i, s))
                            keep(q, hf, slot_of(s), bass.ds(i + 1 + pair, 1))
                invert(n_read["act"].turn(NP - 1, ("S", 1, 1, NT - 1, HG - 1)), NP * NM - 1 + VALUES - 2, NM - 1)
                v.wait_ge(pv_done, NP * NM + 4)
                apply_gate(1)
                for hf in range(2):
                    v.wait_ge(filled, len(first) + NP * len(jobs) + hf + 1)
                    keep(1, hf, slots[hf], slice(NP, NP + 1))

            @block.gpsimd
            def _(pool):
                pool.sem_inc(values, VALUES - 2)
                pool.wait_ge(prepared, 10)

                def split_parts(s, count):
                    w, g = (0 if s[0] == "q" else 1), s[2]
                    pool.tensor_tensor(split[w][g][:, 0, :], raw[w][:], one[:].broadcast_to([P, N]), ALU.mult).then_inc(high, 1)
                    pool.wait_ge(high, count)
                    pool.tensor_tensor(split[w][g][:, 1, :], raw[w][:], split[w][g][:, 0, :], ALU.subtract)\
                        .then_inc(low, 1)

                def scale(q, g, t, n):
                    m = group(q, g, t)
                    pool.wait_ge(inverted, n + INVERTED)
                    pool.wait_ge(pv_done, n + 3)
                    pool.tensor_tensor(vs[:, m % VRING, :].rearrange("p (h c) -> p h c", h=HG),
                                       V[q][:, t, g * P:(g + 1) * P].rearrange("p (h c) -> p h c", h=HG),
                                       inv[:, m % 2, :].unsqueeze(2).broadcast_to([TP, HG, HD]), ALU.mult)\
                        .then_inc(values, 1)

                for s in qk(first):
                    pool.wait_ge(read["act"], n_read["act"].ahead(s))
                    split_parts(s, n_split.ahead(s))
                with pool.Fori(0, NP) as i:
                    for s in order:
                        if s[0] in ("q", "k"):
                            pool.wait_ge(read["act"], n_read["act"].turn(i, s))
                            pool.wait_ge(stacked[s[2]], stacks(i, s, before=1))
                            split_parts(s, n_split.turn(i, s))
                        elif s[0] == "inv":
                            scale(*s[1:4], i * NM + (group(*s[1:4]) + NM * s[4]))
                scale(1, 1, NT - 1, NP * NM - 1)


HID, LAYERS = 128, 2


def routed_ffn(core, slots, d, H, NP):
    nc = core.nc
    NE = d["Wr_t"].shape[1]
    SEG = 4
    with ExitStack() as st:
        c = Core(nc, st)
        center, mean = c.sb("rf_center", [P, P]), c.sb("rf_mean", [P, P])
        Wi = c.sb("rf_wi", [P, HID])
        bi, bo, eps = c.sb("rf_bi", [P, 1]), c.sb("rf_bo", [P, 1]), c.sb("rf_eps", [P, 1])
        Wo = c.sb("rf_wo", [P, F])
        table = c.sb("rf_table", [P, NE + 1, LAYERS, HID + 1])
        shared = c.sb("rf_shared", [P, LAYERS, HID + 1])
        eye = c.sb("rf_eye", [P, P])
        ids = c.sb("rf_ids", [1, 2 * 2 * NP], I32)
        idf = c.sb("rf_idf", [1, 3, 2 * 2 * NP])
        chosen = [c.sb(f"rf_chosen{k}", [P, SEG, LAYERS, HID + 1]) for k in range(2)]
        t0 = [c.sb(f"rf_t{k}", [P, N]) for k in range(2)]
        r1 = [c.sb(f"rf_r{k}", [P, N]) for k in range(2)]
        xn = [c.sb(f"rf_xn{k}", [P, N]) for k in range(2)]
        a = [[c.sb(f"rf_a{k}{q}", [P, N]) for q in range(2)] for k in range(2)]
        weights, tables, routed = c.sem("rf_weights"), c.sem("rf_tables"), c.sem("rf_routed")
        sems = lambda name: [c.sem(f"rf_{name}{k}") for k in range(2)]
        centered, squared, varied, logged, rooted, normed = map(
            sems, ("centered", "squared", "varied", "logged", "rooted", "normed"))
        widened, hidden = sems("widened"), sems("hidden")
        mixed = [[c.sem(f"rf_mixed{k}_{l}") for l in range(LAYERS)] for k in range(2)]
        left = [[c.sem(f"rf_left{k}_{l}") for l in range(LAYERS)] for k in range(2)]
        right = [[c.sem(f"rf_right{k}_{l}") for l in range(LAYERS)] for k in range(2)]
        projected, kept, gathered = sems("projected"), sems("kept"), sems("gathered")
        loops = NP // 2
        WEIGHTS = 16 * (2 * 2 + 5 + 5)

        with nc.Block() as block:

            @block.sync
            def _(sp):
                for q in range(2):
                    sp.dma_start(Wi[F * q:F * q + F, :], d["Wi_t"]).then_inc(weights, 16)
                    sp.dma_start(bo[F * q:F * q + F, :], d["bo"].unsqueeze(1)).then_inc(weights, 16)
                for tile, src in ((bi, d["bi"].unsqueeze(1)), (Wo, d["Wo_t"]), (center, d["center"]),
                                  (mean, d["mean"]), (eye, d["eye"])):
                    sp.dma_start(tile[:], src).then_inc(weights, 16)
                for l in range(LAYERS):
                    sp.dma_start(table[:, 0:NE, l, 0:HID], d["Wr_t"][:, :, l]).then_inc(weights, 16)
                sp.dma_start(shared[:, :, 0:HID], d["Ws"]).then_inc(weights, 16)
                with nc.allow_non_contiguous_dma(reason="a bias column per expert"):
                    sp.dma_start(table[:, 0:NE, :, HID:HID + 1], d["br_t"].unsqueeze(3)).then_inc(weights, 16)
                    sp.dma_start(shared[:, :, HID:HID + 1], d["bs"].unsqueeze(2)).then_inc(weights, 16)
                sp.dma_start(ids[:], d["route"]).then_inc(routed, 16)

            @block.gpsimd
            def _(pool):
                for k in range(2):
                    pool.sem_inc(gathered[k], LEAD)
                pool.wait_ge(tables, 4)
                with pool.Fori(0, loops) as i:
                    for k in range(2):
                        pool.wait_ge(projected[k], at(i - 1))
                        for s in range(SEG):
                            e = pool.value_load(ids[0:1, bass.ds(i * 8 + (SEG * k + s), 1)], min_val=0, max_val=NE)
                            copy = pool.tensor_copy(chosen[k][:, s, :, :].rearrange("p l f -> p (l f)"),
                                                    table[:, bass.ds(e, 1), :, :].rearrange("p a l f -> p (a l f)"))
                        copy.then_inc(gathered[k], 1)

            @block.tensor
            def _(pe):
                for k in range(2):
                    lead(pe, [centered[k], varied[k], projected[k]])
                    lead(pe, [widened[k]] + mixed[k], 2)
                pe.wait_ge(weights, WEIGHTS)
                with pe.Fori(0, loops) as i:
                    for k in range(2):
                        pe.wait_ge(kept[k], at(i - 1))
                        for hf in range(2):
                            mm = pe.matmul(slots[2 * k][:, hf, 0:HALF], center[:],
                                           H[:, bass.ds(2 * i + k + 1, 1), hf * HALF:(hf + 1) * HALF]
                                           .rearrange("p a n -> p (a n)"), start=True, stop=True)
                        mm.then_inc(centered[k], 1)
                    for k in range(2):
                        pe.wait_ge(squared[k], at(i))
                        for hf in range(2):
                            mm = pe.matmul(slots[2 * k + 1][:, hf, 0:HALF], mean[:], t0[k][:, hf * HALF:(hf + 1) * HALF],
                                           start=True, stop=True)
                        mm.then_inc(varied[k], 1)
                    for k in range(2):
                        pe.wait_ge(normed[k], at(i))
                        for q in range(2):
                            for hf in range(2):
                                mm = pe.matmul(slots[2 * k + q][:, hf, 0:HALF], Wi[F * q:F * q + F, :],
                                               xn[k][F * q:F * q + F, hf * HALF:(hf + 1) * HALF], start=True, stop=True)
                            mm.then_inc(widened[k], 1)
                    for l in range(LAYERS):
                        for k in range(2):
                            if l == 0:
                                pe.wait_ge(gathered[k], at(i))
                            for q in range(2):
                                if l == 0:
                                    pe.wait_ge(hidden[k], 2 * i + q + 1 + 2 * LEAD)
                                else:
                                    pe.wait_ge(left[k][0], 2 * i + q + 1 + 2 * LEAD)
                                    pe.wait_ge(right[k][0], 2 * i + q + 1 + 2 * LEAD)
                                for hf in range(2):
                                    mm = pe.matmul(slots[2 * k + q][:, hf, 0:HALF], chosen[k][:, 2 * q + hf, l, 0:HID],
                                                   a[k][q][:, hf * HALF:(hf + 1) * HALF], start=True, stop=True)
                                mm.then_inc(mixed[k][l], 1)
                    for k in range(2):
                        pe.wait_ge(left[k][1], 2 * i + 2 + 2 * LEAD)
                        pe.wait_ge(right[k][1], 2 * i + 2 + 2 * LEAD)
                        for hf in range(2):
                            for q in range(2):
                                mm = pe.matmul(slots[2 * k][F * q:F * q + F, hf, 0:HALF], Wo[:],
                                               a[k][q][:, hf * HALF:(hf + 1) * HALF], start=True, stop=True)
                        mm.then_inc(projected[k], 1)

            @block.scalar
            def _(act):
                for k in range(2):
                    lead(act, [squared[k], logged[k], rooted[k]])
                    lead(act, [hidden[k]] + left[k], 2)
                act.wait_ge(tables, 4)
                with act.Fori(0, loops) as i:
                    for k in range(2):
                        act.wait_ge(centered[k], at(i))
                        act.activation(halves(t0[k][:]), wide(slots[2 * k]), ACT.Square).then_inc(squared[k], 1)
                    for k in range(2):
                        act.wait_ge(varied[k], at(i))
                        act.activation(halves(r1[k][:]), wide(slots[2 * k + 1]), ACT.Ln, bias=eps[:, 0:1])\
                           .then_inc(logged[k], 1)
                    for k in range(2):
                        act.wait_ge(logged[k], at(i))
                        act.activation(t0[k][:], r1[k][:], ACT.Exp, scale=-0.5).then_inc(rooted[k], 1)
                    for k in range(2):
                        for q in range(2):
                            act.wait_ge(widened[k], 2 * i + q + 1 + 2 * LEAD)
                            act.activation(halves(a[k][q][:]), wide(slots[2 * k + q]), ACT.Relu, bias=bi[:, 0:1])\
                               .then_inc(hidden[k], 1)
                    for l in range(LAYERS):
                        for k in range(2):
                            for q in range(2):
                                act.wait_ge(mixed[k][l], 2 * i + q + 1 + 2 * LEAD)
                                act.activation(a[k][q][:, 0:HALF], slots[2 * k + q][:, 0, 0:HALF], ACT.Relu,
                                               bias=chosen[k][:, 2 * q, l, HID:HID + 1]).then_inc(left[k][l], 1)

            @block.vector
            def _(v):
                for k in range(2):
                    lead(v, [normed[k], kept[k]])
                    lead(v, right[k], 2)
                v.memset(eps[:], EPS).then_inc(tables, 1)
                v.memset(table[:, NE, :, :], 0.0).then_inc(tables, 1)
                v.wait_ge(weights, WEIGHTS)
                v.tensor_tensor(shared[:, :, 0:HID], shared[:, :, 0:HID],
                                eye[:].unsqueeze(1).broadcast_to([P, LAYERS, HID]), ALU.add).then_inc(tables, 1)
                v.wait_ge(tables, 3)
                for l in range(LAYERS):
                    ins = v.tensor_tensor(table[:, :, l, :], table[:, :, l, :],
                                          shared[:, l, :].unsqueeze(1).broadcast_to([P, NE + 1, HID + 1]), ALU.add)
                v.wait_ge(routed, 16)
                v.tensor_copy(idf[:, 0, :], ids[:]).then_inc(routed, 1)
                v.wait_ge(routed, 17)
                v.tensor_scalar(idf[:, 1, :], idf[:, 0, :], 0.0, None, ALU.is_ge).then_inc(routed, 1)
                v.tensor_scalar(idf[:, 2, :], idf[:, 0, :], float(NE), None, ALU.is_lt).then_inc(routed, 1)
                v.wait_ge(routed, 19)
                v.tensor_tensor(idf[:, 1, :], idf[:, 1, :], idf[:, 2, :], ALU.mult).then_inc(routed, 1)
                v.tensor_scalar(idf[:, 0, :], idf[:, 0, :], float(NE), None, ALU.subtract).then_inc(routed, 1)
                v.wait_ge(routed, 21)
                v.tensor_tensor(idf[:, 0, :], idf[:, 0, :], idf[:, 1, :], ALU.mult).then_inc(routed, 1)
                v.wait_ge(routed, 22)
                v.tensor_scalar(ids[:], idf[:, 0, :], float(NE), None, ALU.add).then_inc(tables, 1)
                with v.Fori(0, loops) as i:
                    for k in range(2):
                        v.wait_ge(rooted[k], at(i))
                        v.tensor_tensor(halves(xn[k][:]), wide(slots[2 * k]), halves(t0[k][:]), ALU.mult)\
                         .then_inc(normed[k], 1)
                    for l in range(LAYERS):
                        for k in range(2):
                            for q in range(2):
                                v.wait_ge(mixed[k][l], 2 * i + q + 1 + 2 * LEAD)
                                v.tensor_scalar(a[k][q][:, HALF:N], slots[2 * k + q][:, 1, 0:HALF],
                                                chosen[k][:, 2 * q + 1, l, HID:HID + 1], 0.0, ALU.add, ALU.max)\
                                 .then_inc(right[k][l], 1)
                    for k in range(2):
                        v.wait_ge(projected[k], at(i))
                        h = H[:, bass.ds(2 * i + k + 1, 1), :].rearrange("p a (h n) -> p (a h) n", h=2)
                        v.scalar_tensor_tensor(h, wide(slots[2 * k]), bo[:, 0:1], h, ALU.add, ALU.add)\
                         .then_inc(kept[k], 1)


CUT = 448


def causal_attention(core, slots, d, H, X, sums, NP):
    nc = core.nc
    with ExitStack() as st:
        c = Core(nc, st)
        center, mean, eps = c.sb("ca_center", [P, P]), c.sb("ca_mean", [P, P]), c.sb("ca_eps", [P, 1])
        W = c.sb("ca_w", [F, 4, F])
        A, Bv = c.sb("ca_a", [P, P]), c.sb("ca_b", [P, P])
        ab = c.sb("ca_ab", [F, 2, F])
        causal = c.sb("ca_causal", [TP, TP])
        per_row = c.sb("ca_per_row", [P, N])
        t0, r1 = [c.sb(f"ca_t{k}", [P, N]) for k in range(2)], [c.sb(f"ca_r{k}", [P, N]) for k in range(2)]
        t2 = [c.sb(f"ca_t2_{k}", [P, N]) for k in range(2)]
        xn = [c.sb(f"ca_xn{k}", [P, N]) for k in range(2)]
        U = [c.sb(f"ca_u{k}", [P, N]) for k in range(2)]
        V = [c.sb(f"ca_v{k}", [TP, NT, P]) for k in range(2)]
        PB = 4
        prob = c.sb("ca_prob", [TP, PB, N])
        weights, ready = c.sem("ca_weights"), c.sem("ca_ready")
        sems = lambda name: [c.sem(f"ca_{name}{k}") for k in range(2)]
        centered, squared, varied, logged, rooted, normed = map(
            sems, ("centered", "squared", "varied", "logged", "rooted", "normed"))
        turned, scaled, valued, v_ready = map(sems, ("turned", "scaled", "valued", "v_ready"))
        scored, diag, rest = c.sem("ca_scored"), c.sem("ca_diag"), c.sem("ca_rest")
        used = c.sem("ca_used")
        kept, last = sems("kept"), sems("last")
        centered2, squared2, varied2, logged2, rooted2 = map(
            sems, ("centered2_", "squared2_", "varied2_", "logged2_", "rooted2_"))
        loops = NP // 2
        NS = 2 * 2 * NT
        tiles = [(k, m, q) for k in range(2) for m in range(NT) for q in range(2)]

        NR = sum(m * TP < CUT for _, m, _ in tiles)

        def rests(n):
            return sum(m * TP < CUT for _, m, _ in tiles[:n + 1])

        def parts(lo):
            return [(b, max(lo, CUT * b) - CUT * b, (CUT, N - CUT)[b], CUT * b) for b in range(2)
                    if lo < (CUT, N)[b]]

        with nc.Block() as block:

            @block.sync
            def _(sp):
                for j, name in enumerate(("Wq", "Wk", "Wv", "Wo1_t")):
                    sp.dma_start(W[:, j, :], d[name]).then_inc(weights, 16)
                for tile, name in ((center, "center"), (mean, "mean"), (causal, "causal"), (per_row, "per_row")):
                    sp.dma_start(tile[:], d[name]).then_inc(weights, 16)
                sp.wait_ge(ready, 5)
                for j, tile in enumerate((A, Bv)):
                    for q in range(2):
                        r = slice(F * q, F * q + F)
                        sp.dma_start(tile[r, r], ab[:, j, :]).then_inc(weights, 16)

            @block.gpsimd
            def _(pool):
                pool.memset(A[:], 0.0).then_inc(ready, 1)
                pool.memset(Bv[:], 0.0).then_inc(ready, 1)

            def norm_mm(pe, lhs, src, slot, wait, value, done):
                pe.wait_ge(wait, value)
                for hf in range(2):
                    mm = pe.matmul(slot[:, hf, 0:HALF], lhs[:], src[:, hf * HALF:(hf + 1) * HALF], start=True, stop=True)
                mm.then_inc(done, 1)

            @block.tensor
            def _(pe):
                for k in range(2):
                    lead(pe, [centered[k], varied[k], turned[k], valued[k], centered2[k], varied2[k]])
                pe.sem_inc(used, PB)
                pe.wait_ge(weights, 16 * 8)
                pe.matmul(slots[0][0:F, 0, 0:F], W[:, 0, :], W[:, 1, :], start=True, stop=True)
                pe.matmul(slots[0][0:F, 0, F:2 * F], W[:, 2, :], W[:, 3, :], start=True, stop=True).then_inc(ready, 1)
                pe.wait_ge(weights, 16 * 12)
                with pe.Fori(0, loops) as i:
                    for k in range(2):
                        norm_mm(pe, center, H[:, bass.ds(2 * i + k + 1, 1), :].rearrange("p a n -> p (a n)"),
                                slots[2 + k], logged2[k], at(i - 1), centered[k])
                    for k in range(2):
                        pe.wait_ge(last[k], at(i - 1))
                        norm_mm(pe, mean, t0[k], slots[k], squared[k], at(i), varied[k])
                    for k in range(2):
                        norm_mm(pe, A, xn[k], slots[k], normed[k], at(i), turned[k])
                        for t in range(NT):
                            mm = pe.matmul(flat(slots[2 + k])[0:TP, t * P:(t + 1) * P], xn[k][:, t * TP:(t + 1) * TP],
                                           Bv[:], start=True, stop=True)
                        mm.then_inc(valued[k], 1)

                    def scores(n):
                        k, m, q = tiles[n]
                        slot = slots[n % 3]
                        if n < 3:
                            pe.wait_ge(scaled[1], at(i))
                            pe.wait_ge(v_ready[0], at(i))
                        else:
                            pe.wait_ge(diag, i * NS + n - 2)
                            pe.wait_ge(rest, i * NR + rests(n - 3))
                        for b, lo, hi, c0 in parts(m * TP):
                            mm = pe.matmul(slot[0:TP, b, lo:hi], xn[k][F * q:F * q + F, m * TP:(m + 1) * TP],
                                           U[k][F * q:F * q + F, c0 + lo:c0 + hi], start=True, stop=True)
                        mm.then_inc(scored, 1)

                    def values(n):
                        k, m, _ = tiles[n]
                        if m == 0:
                            pe.wait_ge(v_ready[1], at(i))
                            if k == 1:
                                pe.wait_ge(kept[0], at(i))
                        pe.wait_ge(diag, i * NS + n + 2)
                        pe.wait_ge(rest, i * NR + rests(n + 1))
                        for b, lo, hi, c0 in parts(m * TP):
                            for q in range(2):
                                mm = pe.matmul(slots[3][F * q:F * q + F, b, lo:hi], V[k][:, m, F * q:F * q + F],
                                               prob[:, (n + q) % PB, c0 + lo:c0 + hi],
                                               start=(m == 0), stop=(m == (3 if b == 0 else NT - 1)))
                        mm.then_inc(used, 2)

                    for n in range(0, NS, 2):
                        scores(n)
                        scores(n + 1)
                        if n >= 2:
                            values(n - 2)
                    values(NS - 2)
                    for k in range(2):
                        norm_mm(pe, center, H[:, bass.ds(2 * i + k + 1, 1), :].rearrange("p a n -> p (a n)"),
                                slots[k], kept[k], at(i), centered2[k])
                    for k in range(2):
                        norm_mm(pe, mean, t2[k], slots[2 + k], squared2[k], at(i), varied2[k])

            @block.scalar
            def _(act):
                for k in range(2):
                    lead(act, [squared[k], logged[k], rooted[k], v_ready[k], squared2[k], logged2[k], rooted2[k]])
                act.wait_ge(ready, 4)
                with act.Fori(0, loops) as i:

                    def inverse_root(t, xc, var, centered, squared, varied, logged, rooted):
                        for k in range(2):
                            act.wait_ge(centered[k], at(i))
                            act.activation(halves(t[k][:]), wide(slots[xc + k]), ACT.Square).then_inc(squared[k], 1)
                        for k in range(2):
                            act.wait_ge(varied[k], at(i))
                            act.activation(halves(r1[k][:]), wide(slots[var + k]), ACT.Ln, bias=eps[:, 0:1])\
                               .then_inc(logged[k], 1)
                        for k in range(2):
                            act.wait_ge(logged[k], at(i))
                            act.activation(t[k][:], r1[k][:], ACT.Exp, scale=-0.5).then_inc(rooted[k], 1)

                    inverse_root(t0, 2, 0, centered, squared, varied, logged, rooted)
                    for k in range(2):
                        act.wait_ge(valued[k], at(i))
                        act.activation(V[k][:].rearrange("p t f -> p (t f)"), flat(slots[2 + k])[0:TP, 0:NT * P],
                                       ACT.Copy).then_inc(v_ready[k], 1)
                    for n, (k, m, q) in enumerate(tiles):
                        if m * TP >= CUT:
                            continue
                        act.wait_ge(scored, i * NS + n + 1)
                        act.wait_ge(used, i * NS + n // 2 * 2 + 2)
                        act.activation(prob[:, n % PB, CUT:N], slots[n % 3][0:TP, 1, 0:N - CUT], ACT.Relu)\
                           .then_inc(rest, 1)
                    inverse_root(t2, 0, 2, centered2, squared2, varied2, logged2, rooted2)

            @block.vector
            def _(v):
                for k in range(2):
                    lead(v, [normed[k], scaled[k], kept[k], last[k]])
                v.memset(eps[:], EPS).then_inc(ready, 1)
                v.wait_ge(ready, 4)
                v.tensor_copy(ab[:].rearrange("p a f -> p (a f)"), slots[0][0:F, 0, 0:2 * F]).then_inc(ready, 1)
                with v.Fori(0, loops) as i:
                    for k in range(2):
                        v.wait_ge(rooted[k], at(i))
                        v.tensor_tensor(halves(xn[k][:]), wide(slots[2 + k]), halves(t0[k][:]), ALU.mult)\
                         .then_inc(normed[k], 1)
                    for k in range(2):
                        v.wait_ge(turned[k], at(i))
                        v.tensor_tensor(halves(U[k][:]), wide(slots[k]), halves(per_row[:]), ALU.mult)\
                         .then_inc(scaled[k], 1)

                    def keep(k):
                        v.wait_ge(used, i * NS + (k + 1) * 2 * NT + PB)
                        h = H[:, bass.ds(2 * i + k + 1, 1), :].rearrange("p a n -> p (a n)")
                        v.tensor_tensor(h[:, 0:CUT], h[:, 0:CUT], slots[3][:, 0, 0:CUT], ALU.add)
                        v.tensor_tensor(h[:, CUT:N], h[:, CUT:N], slots[3][:, 1, 0:N - CUT], ALU.add)\
                         .then_inc(kept[k], 1)

                    for n, (k, m, q) in enumerate(tiles):
                        v.wait_ge(scored, i * NS + n + 1)
                        v.wait_ge(used, i * NS + n // 2 * 2 + 2)
                        slot, b, c0 = slots[n % 3], m * TP // CUT, m * TP // CUT * CUT
                        d0 = m * TP - c0
                        ins = v.scalar_tensor_tensor(prob[:, n % PB, m * TP:(m + 1) * TP], slot[0:TP, b, d0:d0 + TP],
                                                     0.0, causal[:], ALU.max, ALU.mult)
                        end = (CUT, N)[b]
                        if (m + 1) * TP < end:
                            ins = v.tensor_scalar(prob[:, n % PB, (m + 1) * TP:end],
                                                  slot[0:TP, b, d0 + TP:end - c0], 0.0, None, ALU.max)
                        ins.then_inc(diag, 1)
                        if n == 2 * NT + 1:
                            keep(0)
                    keep(1)
                    for k in range(2):
                        v.wait_ge(rooted2[k], at(i))
                        x = X[:, bass.ds(2 * i + k, 1), :].rearrange("p a (h n) -> p (a h) n", h=2)
                        v.scalar_tensor_tensor(x, wide(slots[k]), 1.0, halves(t2[k][:]), ALU.mult, ALU.mult,
                                               accum_out=sums[:, bass.ds(2 * i + k, 1)]).then_inc(last[k], 1)


TOP = 2
FF = 128
LIFTS = ("lift0", "lift1")
STEPS = (*LIFTS, "lower", "center", "vary", "turn")


class Routes:

    def __init__(self, core, NP):
        self.expert = core.sb("rt_expert", [1, 2 * TOP, NP], I32)
        self.weight = core.sb("rt_weight", [P, 2 * TOP, NP])
        self.b2 = core.sb("rt_b2", [P, NP])


def routing(core, slots, d, sums, R, NP):
    nc = core.nc
    E = d["Wr1"].shape[1]
    B = 2 * NP
    capacity = float(-(-B * N * 5 // (4 * E)))
    with ExitStack() as st:
        c = Core(nc, st)
        Wr = c.sb("rt_wr", [P, E])
        br, ids = c.sb("rt_br", [NP, E]), c.sb("rt_ids", [NP, E])
        b2 = c.sb("rt_b2w", [E, F])
        eye, ones = c.sb("rt_eye", [P, P]), c.sb("rt_ones", [NP, NP])
        z, w = c.sb("rt_z", [NP, 2, E]), c.sb("rt_w", [NP, 2, E])
        m = c.sb("rt_m", [NP, 2])
        load = c.sb("rt_load", [NP, E])
        top, topi, topf = c.sb("rt_top", [NP, 2, 8]), c.sb("rt_topi", [NP, 2, 8], U32), c.sb("rt_topf", [NP, 2, 8])
        e2, tw = c.sb("rt_e2", [NP, 2]), c.sb("rt_tw", [NP, 2, TOP])
        wide_w = c.sb("rt_wide", [NP, 2 * TOP, P])
        dense = c.sb("rt_dense", [NP, 2, TOP, E])
        denseT = c.sb("rt_denseT", [E, 2, NP])
        loaded, step, mm_done, act_done = c.sem("rt_loaded"), c.sem("rt_step"), c.sem("rt_mm"), c.sem("rt_act")
        both = lambda t: t.unsqueeze(1).broadcast_to([NP, 2, E])
        each = lambda t: t.unsqueeze(2).broadcast_to([NP, 2, E])
        LOADED = 16 * 6
        with nc.Block() as block:

            @block.sync
            def _(sp):
                for q in range(2):
                    sp.dma_start(Wr[F * q:F * q + F, :], d["Wr1"]).then_inc(loaded, 16)
                for tile, name in ((br, "br1"), (ids, "experts"), (b2, "b2"), (eye, "eye")):
                    sp.dma_start(tile[:], d[name]).then_inc(loaded, 16)

            @block.vector
            def _(v):
                n = [0]

                def done(ins):
                    n[0] += 1
                    ins.then_inc(step, 1)
                    v.wait_ge(step, n[0])

                def softmax(turn):
                    done(v.tensor_reduce(m[:], z[:], AX.X, ALU.max))
                    done(v.tensor_tensor(z[:], z[:], each(m[:]), ALU.subtract))
                    v.wait_ge(act_done, turn)
                    done(v.tensor_reduce(m[:], w[:], AX.X, ALU.add))
                    done(v.reciprocal(m[:], m[:]))
                    done(v.tensor_tensor(w[:], w[:], each(m[:]), ALU.mult))

                v.memset(ones[:], 1.0)
                v.wait_ge(loaded, LOADED)
                v.wait_ge(mm_done, 1)
                for q in range(2):
                    v.scalar_tensor_tensor(z[:, q, :], slots[q][0:NP, 0, 0:E], 1.0 / N, br[:], ALU.mult, ALU.add)
                done(v.tensor_copy(topf[:].rearrange("p q e -> p (q e)")[:, 0:E], br[:]))
                softmax(1)
                v.wait_ge(mm_done, 2)
                done(v.tensor_copy(load[:], slots[2][0:NP, 0, 0:E]))
                done(v.tensor_tensor(load[:], load[:], slots[2][0:NP, 0, E:2 * E], ALU.add))
                done(v.tensor_scalar(load[:], load[:], float(N), 1e-30, ALU.mult, ALU.max))
                done(v.reciprocal(load[:], load[:]))
                done(v.tensor_scalar(load[:], load[:], capacity, 1.0, ALU.mult, ALU.min))
                done(v.tensor_tensor(z[:], w[:], both(load[:]), ALU.mult))
                softmax(2)
                for q in range(2):
                    done(v.max(top[:, q, :], w[:, q, :]))
                    done(v.max_index(topi[:, q, :], top[:, q, :], w[:, q, :]))
                done(v.tensor_copy(topf[:], topi[:]))
                done(v.tensor_tensor(m[:], top[:, :, 1], top[:, :, 0], ALU.subtract))
                v.wait_ge(act_done, 3)
                done(v.tensor_scalar(m[:], e2[:], 1.0, None, ALU.add))
                done(v.reciprocal(tw[:, :, 0], m[:]))
                done(v.tensor_tensor(tw[:, :, 1], tw[:, :, 0], e2[:], ALU.mult))
                done(v.tensor_copy(wide_w[:], tw[:].rearrange("p q r -> p (q r)").unsqueeze(2)
                                   .broadcast_to([NP, 2 * TOP, P])))
                for q in range(2):
                    for r in range(TOP):
                        done(v.tensor_scalar(dense[:, q, r, :], ids[:], topf[:, q, r:r + 1], tw[:, q, r:r + 1],
                                             ALU.is_equal, ALU.mult))
                done(v.tensor_tensor(dense[:, :, 0, :], dense[:, :, 0, :], dense[:, :, 1, :], ALU.add))
                v.wait_ge(mm_done, 3)
                for q in range(2):
                    v.tensor_copy(denseT[:, q, :], slots[0][0:E, 0, q * NP:(q + 1) * NP])
                v.tensor_copy(R.expert[:].rearrange("a j p -> a (j p)"), slots[1][0:1, 0, 0:2 * TOP * NP])
                done(v.tensor_copy(R.weight[:].rearrange("a j p -> a (j p)"), slots[2][:, 0, 0:2 * TOP * NP]))
                v.wait_ge(mm_done, 4)
                done(v.tensor_copy(R.b2[:], slots[3][:, 0, 0:NP]))

            @block.scalar
            def _(act):
                for turn, after in ((1, 3), (2, 14)):
                    act.wait_ge(step, after)
                    act.activation(w[:], z[:], ACT.Exp).then_inc(act_done, 1)
                act.wait_ge(step, 23)
                act.activation(e2[:], m[:], ACT.Exp).then_inc(act_done, 1)

            @block.tensor
            def _(pe):
                pe.wait_ge(loaded, LOADED)
                for q in range(2):
                    mm = pe.matmul(slots[q][0:NP, 0, 0:E], sums[F * q:F * q + F, :], Wr[F * q:F * q + F, :],
                                   start=True, stop=True)
                mm.then_inc(mm_done, 1)
                pe.wait_ge(step, 6)
                pe.matmul(slots[2][0:NP, 0, 0:2 * E], ones[:], w[:].rearrange("p q e -> p (q e)"),
                          start=True, stop=True).then_inc(mm_done, 1)
                pe.wait_ge(step, 32)
                for q in range(2):
                    pe.matmul(slots[0][0:E, 0, q * NP:(q + 1) * NP], dense[:, q, 0, :], eye[0:NP, 0:NP],
                              start=True, stop=True)
                for q in range(2):
                    for r in range(TOP):
                        j = 2 * q + r
                        pe.matmul(slots[1][0:1, 0, j * NP:(j + 1) * NP], topf[:, q, r:r + 1], eye[0:NP, 0:NP],
                                  start=True, stop=True)
                for j in range(2 * TOP):
                    mm = pe.matmul(slots[2][:, 0, j * NP:(j + 1) * NP], wide_w[:, j, :], eye[0:NP, 0:NP],
                                   start=True, stop=True)
                mm.then_inc(mm_done, 1)
                pe.wait_ge(step, 33)
                for q in range(2):
                    mm = pe.matmul(slots[3][F * q:F * q + F, 0, 0:NP], b2[:], denseT[:, q, :], start=True, stop=True)
                mm.then_inc(mm_done, 1)


def mixture(core, slots, d, H, X, R, out, NP):
    nc = core.nc
    E = d["W1"].shape[1]
    with ExitStack() as st:
        c = Core(nc, st)
        center, mean, eye = c.sb("mx_center", [P, P]), c.sb("mx_mean", [P, P]), c.sb("mx_eye", [P, P])
        eps, gamma, beta = c.sb("mx_eps", [P, 1]), c.sb("mx_gamma", [P, 1]), c.sb("mx_beta", [P, 1])
        T1, b1, T2 = c.sb("mx_w1", [P, E, FF]), c.sb("mx_b1", [FF, E]), c.sb("mx_w2", [FF, E, F])
        pair = lambda name, shape: [c.sb(f"mx_{name}{k}", shape) for k in range(2)]
        C1, cb1, C2 = pair("c1_", [P, 2 * TOP, FF]), pair("cb1_", [FF, 2, TOP]), pair("c2_", [FF, 2, TOP, F])
        xs, t0, r1, z = pair("xs", [P, N]), pair("t", [P, N]), pair("r", [P, N]), pair("z", [P, N])
        G = [[[c.sb(f"mx_g{k}{q}{r}", [FF, N]) for r in range(TOP)] for q in range(2)] for k in range(2)]
        OT = pair("out", [TP, 2, NT, F])
        weights, ready = c.sem("mx_weights"), c.sem("mx_ready")
        sems = lambda name: [c.sem(f"mx_{name}{k}") for k in range(2)]
        x_in, gathered, lifted, gelued, lowered, summed = map(
            sems, ("x_in", "gathered", "lifted", "gelued", "lowered", "summed"))
        centered, squared, varied, logged, rooted = map(
            sems, ("centered", "squared", "varied", "logged", "rooted"))
        normed, scaled, shifted, turned, copied, stored = map(
            sems, ("normed", "scaled", "shifted", "turned", "copied", "stored"))
        loops = NP // 2
        WEIGHTS = 16 * (3 * 2 + 5)
        out_v = out.rearrange("b (p t) f -> p b (t f)", t=NT)

        with nc.Block() as block:

            @block.sync
            def _(sp):
                for k in range(2):
                    lead(sp, [x_in[k]], 16)
                for q in range(2):
                    r = slice(F * q, F * q + F)
                    sp.dma_start(T1[r], d["W1"]).then_inc(weights, 16)
                    sp.dma_start(gamma[r, :], d["gamma1"].unsqueeze(1)).then_inc(weights, 16)
                    sp.dma_start(beta[r, :], d["beta1"].unsqueeze(1)).then_inc(weights, 16)
                for tile, name in ((center, "center"), (mean, "mean"), (eye, "eye"), (b1, "b1"), (T2, "W2")):
                    sp.dma_start(tile[:], d[name]).then_inc(weights, 16)
                with sp.Fori(0, loops) as i:
                    for k in range(2):
                        sp.wait_ge(summed[k], at(i - 1))
                        sp.dma_start(xs[k][:], X[:, bass.ds(2 * i + k, 1), :].rearrange("p a n -> p (a n)"))\
                          .then_inc(x_in[k], 16)
                for k in range(2):
                    sp.wait_ge(stored[k], at(loops - 1, 16))

            @block.gpsimd
            def _(pool):
                for k in range(2):
                    lead(pool, [gathered[k]])
                pool.wait_ge(weights, WEIGHTS)
                with pool.Fori(0, loops) as i:
                    for k in range(2):
                        pool.wait_ge(lowered[k], at(i - 1))
                        for q in range(2):
                            for r in range(TOP):
                                j = 2 * q + r
                                e = pool.value_load(R.expert[0:1, j, bass.ds(2 * i + k, 1)], min_val=0, max_val=E - 1)
                                pool.tensor_copy(C1[k][:, j, :], T1[:, bass.ds(e, 1), :].rearrange("p a f -> p (a f)"))
                                pool.tensor_copy(cb1[k][:, q, r:r + 1], b1[:, bass.ds(e, 1)])
                                ins = pool.tensor_tensor(C2[k][:, q, r, :],
                                                         T2[:, bass.ds(e, 1), :].rearrange("p a f -> p (a f)"),
                                                         R.weight[:, j, bass.ds(2 * i + k, 1)].broadcast_to([FF, F]),
                                                         ALU.mult)
                        ins.then_inc(gathered[k], 1)

            @block.tensor
            def _(pe):
                for k in range(2):
                    lead(pe, [lifted[k]], 4)
                    lead(pe, [lowered[k], centered[k], varied[k], turned[k]])
                pe.wait_ge(weights, WEIGHTS)

                def part(step, k, i):
                    if step == "lift0":
                        pe.wait_ge(gathered[k], at(i))
                        pe.wait_ge(x_in[k], i * 16 + (16 + 16 * LEAD))
                        pe.wait_ge(copied[k], at(i - 1))
                    if step in LIFTS:
                        q = LIFTS.index(step)
                        for r in range(TOP):
                            j = 2 * q + r
                            if q == 1:
                                pe.wait_ge(gelued[k], 4 * i + ((j - 1) + 4 * LEAD))
                            for hf in range(2):
                                mm = pe.matmul(slots[2 * k + r][:, hf, 0:HALF], C1[k][F * q:F * q + F, j, :],
                                               xs[k][F * q:F * q + F, hf * HALF:(hf + 1) * HALF],
                                               start=True, stop=True)
                            mm.then_inc(lifted[k], 1)
                    elif step == "lower":
                        pe.wait_ge(gelued[k], 4 * i + (4 + 4 * LEAD))
                        for hf in range(2):
                            for r in range(TOP):
                                for q in range(2):
                                    mm = pe.matmul(slots[2 * k][F * q:F * q + F, hf, 0:HALF], C2[k][:, q, r, :],
                                                   G[k][q][r][:, hf * HALF:(hf + 1) * HALF],
                                                   start=(r == 0), stop=(r == TOP - 1))
                        mm.then_inc(lowered[k], 1)
                    elif step == "center":
                        pe.wait_ge(summed[k], at(i))
                        for hf in range(2):
                            mm = pe.matmul(slots[2 * k + 1][:, hf, 0:HALF], center[:], z[k][:, hf * HALF:(hf + 1) * HALF],
                                           start=True, stop=True)
                        mm.then_inc(centered[k], 1)
                    elif step == "vary":
                        pe.wait_ge(squared[k], at(i))
                        for hf in range(2):
                            mm = pe.matmul(slots[2 * k][:, hf, 0:HALF], mean[:], t0[k][:, hf * HALF:(hf + 1) * HALF],
                                           start=True, stop=True)
                        mm.then_inc(varied[k], 1)
                    elif step == "turn":
                        pe.wait_ge(shifted[k], at(i))
                        for t in range(NT):
                            mm = pe.transpose(flat(slots[2 * k])[0:TP, t * P:(t + 1) * P],
                                              z[k][:, t:t + NT * (TP - 1) + 1:NT], eye[:])
                        mm.then_inc(turned[k], 1)

                run_staggered(pe, loops, STEPS, part)

            @block.scalar
            def _(act):
                for k in range(2):
                    lead(act, [gelued[k]], 4)
                    lead(act, [squared[k], logged[k], rooted[k], copied[k]])
                    lead(act, [stored[k]], 16)
                act.wait_ge(ready, 1)

                def part(step, k, i):
                    if step in LIFTS:
                        q = LIFTS.index(step)
                        for r in range(TOP):
                            act.wait_ge(lifted[k], 4 * i + ((2 * q + r + 1) + 4 * LEAD))
                            act.activation(halves(G[k][q][r][:]), wide(slots[2 * k + r]), ACT.Gelu,
                                           bias=cb1[k][:, q, r:r + 1]).then_inc(gelued[k], 1)
                    elif step == "center":
                        act.wait_ge(centered[k], at(i))
                        act.activation(halves(t0[k][:]), wide(slots[2 * k + 1]), ACT.Square).then_inc(squared[k], 1)
                    elif step == "vary":
                        act.wait_ge(varied[k], at(i))
                        act.activation(halves(r1[k][:]), wide(slots[2 * k]), ACT.Ln, bias=eps[:, 0:1])\
                           .then_inc(logged[k], 1)
                        act.wait_ge(logged[k], at(i))
                        act.activation(t0[k][:], r1[k][:], ACT.Exp, scale=-0.5).then_inc(rooted[k], 1)
                    elif step == "turn":
                        act.wait_ge(turned[k], at(i))
                        act.wait_ge(stored[k], i * 16 + 16 * LEAD)
                        act.activation(OT[k][:].rearrange("p q t f -> p t q f"),
                                       flat(slots[2 * k])[0:TP, 0:NT * P].rearrange("p (t q f) -> p t q f", t=NT, q=2),
                                       ACT.Copy).then_inc(copied[k], 1)
                        act.wait_ge(copied[k], at(i))
                        act.dma_start(out_v[:, bass.ds(4 * i + 2 * k, 2), :],
                                      OT[k][:].rearrange("p q t f -> p q (t f)")).then_inc(stored[k], 16)

                run_staggered(act, loops, STEPS, part)

            @block.vector
            def _(v):
                for k in range(2):
                    lead(v, [summed[k], normed[k], scaled[k], shifted[k]])
                v.memset(eps[:], EPS).then_inc(ready, 1)
                v.wait_ge(weights, WEIGHTS)

                def part(step, k, i):
                    if step == "lower":
                        v.wait_ge(lowered[k], at(i))
                        v.scalar_tensor_tensor(halves(z[k][:]), wide(slots[2 * k]), R.b2[:, bass.ds(2 * i + k, 1)],
                                               halves(xs[k][:]), ALU.add, ALU.add).then_inc(summed[k], 1)
                    elif step == "vary":
                        v.wait_ge(rooted[k], at(i))
                        v.tensor_tensor(halves(r1[k][:]), wide(slots[2 * k + 1]), halves(t0[k][:]), ALU.mult)\
                         .then_inc(normed[k], 1)
                        v.wait_ge(normed[k], at(i))
                        v.scalar_tensor_tensor(r1[k][:], r1[k][:], gamma[:, 0:1],
                                               H[:, bass.ds(2 * i + k + 1, 1), :].rearrange("p a n -> p (a n)"),
                                               ALU.mult, ALU.add).then_inc(scaled[k], 1)
                        v.wait_ge(scaled[k], at(i))
                        v.tensor_scalar(z[k][:], r1[k][:], beta[:, 0:1], None, ALU.add).then_inc(shifted[k], 1)

                run_staggered(v, loops, STEPS, part)


def tower(nc, d, out):
    B = d["x"].shape[0]
    NP = B // 2
    with ExitStack() as st:
        core = Core(nc, st)
        slots = [core.ps(f"slot{i}", [P, 2, 512]) for i in range(4)]
        H = core.sb("H", [P, NP + 1, N])
        scratch = nc.dram_tensor("norms", (P, NP + 1, 2, N), F32, kind="Internal").ap()
        tokens(core, slots, d, H, scratch, NP)
        attention(core, slots, d, H, scratch, NP)
        routed_ffn(core, slots, d, H, NP)
        X = core.sb("X", [P, NP, N])
        sums = core.sb("X_sums", [P, NP])
        causal_attention(core, slots, d, H, X, sums, NP)
        R = Routes(core, NP)
        routing(core, slots, d, sums, R, NP)
        mixture(core, slots, d, H, X, R, out, NP)


def shape_constants(pairs, experts):
    pos = np.arange(N, dtype=np.float32)[:, None]
    step = np.arange(0, F, 2, dtype=np.float32) * np.float32(-np.log(10000.0) / F)
    angle = (pos * np.exp(step.astype(np.float64)).astype(np.float32)).astype(np.float64)
    pe = np.zeros((N, F), np.float32)
    pe[:, 0::2] = np.sin(angle)
    pe[:, 1::2] = np.cos(angle)
    img = np.arange(P) // F
    same = (img[:, None] == img[None, :]).astype(np.float32)
    eye = np.eye(P, dtype=np.float32)
    patch = np.arange(N, dtype=np.float32)
    return {
        "pos": np.concatenate([pe.T, pe.T]).copy(),
        "iota": np.tile(patch, (TP, 1)),
        "center": eye - same / F,
        "mean": same / F,
        "eye": eye,
        "causal": np.triu(np.ones((TP, TP), np.float32)),
        "experts": np.tile(np.arange(experts, dtype=np.float32), (pairs, 1)),
        "per_row": np.tile(1.0 / np.maximum(patch, 1.0), (P, 1)).astype(np.float32),
    }


def laid_out(inputs):
    a = {k: np.asarray(v) for k, v in inputs.items()}
    B = a["x"].shape[0]
    edges = a["L0_tok_edge_index"].astype(np.int32)
    E = edges.shape[1]
    KE = -(-E // TP)
    rows = np.full((2, KE * TP), -1, np.int32)
    rows[:, :E] = edges
    own = np.tile(np.arange(N, dtype=np.int32), (2, 1))
    t = lambda x, *axes: np.ascontiguousarray(np.transpose(x, axes or None))
    d = {
        "x": a["x"],
        "edges": t(np.concatenate([rows, own], 1).reshape(2, KE + NT, TP), 2, 0, 1),
        "W_embed": a["L0_tok_W_embed"], "b_embed": a["L0_tok_b_embed"],
        "W_gcn": a["L0_tok_W_gcn"], "b_gcn": t(a["L0_tok_b_gcn"]),
        "W_out": a["L0_tok_W_out"], "b_out": a["L0_tok_b_out"],
        "gamma0": a["L0_attn_ln_gamma"], "beta0": a["L0_attn_ln_beta"],
        "W_qkv_t": t(a["L0_attn_W_qkv"]), "W_gate_t": t(a["L0_attn_W_gate"]),
        "b_gate": a["L0_attn_b_gate"], "W_final_t": t(a["L0_attn_W_final"]), "b_final": a["L0_attn_b_final"],
        "route": a["L0_ffn_route_id"].astype(np.int32).reshape(1, -1),
        "Wi_t": t(a["L0_ffn_Wi"]), "bi": a["L0_ffn_bi"],
        "Wr_t": t(a["L0_ffn_Wr"], 3, 1, 0, 2), "br_t": t(a["L0_ffn_br"], 2, 1, 0),
        "Ws": t(a["L0_ffn_Ws"][:, 0], 2, 0, 1), "bs": t(a["L0_ffn_bs"][:, 0]),
        "Wo_t": t(a["L0_ffn_Wo"]), "bo": a["L0_ffn_bo"],
        "Wq": a["L1_attn_Wq"], "Wk": a["L1_attn_Wk"], "Wv": a["L1_attn_Wv"], "Wo1_t": t(a["L1_attn_Wo"]),
        "Wr1": a["L1_ffn_Wr"], "br1": np.tile(a["L1_ffn_br"], (B // 2, 1)),
        "W1": t(a["L1_ffn_W1"], 1, 0, 2), "b1": t(a["L1_ffn_b1"]),
        "W2": t(a["L1_ffn_W2"], 1, 0, 2), "b2": a["L1_ffn_b2"],
        "gamma1": a["L1_ffn_gamma"], "beta1": a["L1_ffn_beta"],
    }
    return {**d, **shape_constants(B // 2, a["L1_ffn_br"].size)}


def kernel(**inputs):
    import concourse.bacc as _bacc
    from concourse import mybir as _mybir
    from concourse.bass_utils import run_bass_kernel_spmd as _run

    nc = _bacc.Bacc("TRN2", target_bir_lowering=False, num_devices=1)
    data = laid_out(inputs)
    B = data["x"].shape[0]
    d = {n: nc.dram_tensor(f"in_{n}", a.shape, _mybir.dt.from_np(a.dtype), kind="ExternalInput").ap()
         for n, a in data.items()}
    out = nc.dram_tensor("tokens_out", (B, N, F), F32, kind="ExternalOutput").ap()
    tower(nc, d, out)
    r = _run(nc, [{f"in_{n}": a for n, a in data.items()}], core_ids=[0])
    return r.results[0]["tokens_out"]
```
